# Optimizing a Trainium2 kernel written in Bass

```python
import numpy as np
import jax
import jax.numpy as jnp

def _softmax(x, axis=-1):
    return jax.nn.softmax(x, axis=axis)

def _gelu(x):
    return jax.nn.gelu(x, approximate=True)

def _silu(x):
    return jax.nn.silu(x)

def _sigmoid(x):
    return jax.nn.sigmoid(x)

def _layernorm(x, axis=-1, eps=1e-05):
    m = jnp.mean(x, axis=axis, keepdims=True)
    v = jnp.var(x, axis=axis, keepdims=True)
    return (x - m) / jnp.sqrt(v + eps)

def _scatter_add(tgt, idx, src, axis=0):
    return tgt.at[idx].add(src)

def _segment_sum(src, seg, n):
    return jax.ops.segment_sum(src, seg, n)
kernel_name = 'mk_early_fusion_embed_d1_tok_img768_r4_8f1197'

def setup_inputs(seed: int=0):
    np.random.seed(seed)
    _w = jnp.asarray

    def _rec_inputs():
        import jax
        import jax.numpy as jnp
        _rk = jax.random.key(seed)
        x = -0.000356955 + 1 * jax.random.normal(jax.random.fold_in(_rk, 1), (16, 3, 64, 64), jnp.float32)
        x_txt = jax.random.randint(jax.random.fold_in(_rk, 51), (16, 512), 0, 31999, jnp.int32)
        itok_BS_0_15 = jax.random.randint(jax.random.fold_in(_rk, 71), (16, 512), 0, 16, jnp.int32)
        itok_BS_0_3 = jax.random.randint(jax.random.fold_in(_rk, 72), (16, 512), 0, 4, jnp.int32)
        itok_BS_0_9999 = jax.random.randint(jax.random.fold_in(_rk, 73), (16, 512), 0, 2500, jnp.int32)
        itok_BS_0_2047 = jax.random.randint(jax.random.fold_in(_rk, 74), (16, 512), 0, 512, jnp.int32)
        fside_BS_age_tau = 49.5725 + 28.8366 * jax.random.normal(jax.random.fold_in(_rk, 75), (16, 512), jnp.float32)
        fside_BS_delays_tau = 49.8282 + 28.8637 * jax.random.normal(jax.random.fold_in(_rk, 76), (16, 512), jnp.float32)
        return (x, x_txt, itok_BS_0_15, itok_BS_0_3, itok_BS_0_9999, itok_BS_0_2047, fside_BS_age_tau, fside_BS_delays_tau)
    x, x_txt, itok_BS_0_15, itok_BS_0_3, itok_BS_0_9999, itok_BS_0_2047, fside_BS_age_tau, fside_BS_delays_tau = _rec_inputs()

    def _L0_tok_setup():
        import jax, jax.numpy as jnp
        import numpy as np
        PATCH = 16
        EMBED = 192
        IN_DIM = PATCH * PATCH * 3

        def extract_patches(x, p):
            B, C, H, Wd = x.shape
            h, w = (H // p, Wd // p)
            xr = x.reshape(B, C, h, p, w, p)
            xr = xr.transpose(0, 2, 4, 3, 5, 1)
            return xr.reshape(B, h * w, p * p * C)
        key = jax.random.key(seed)
        kx, kw, kb = jax.random.split(key, 3)
        x = jax.random.normal(kx, (128, 3, 224, 224), dtype=jnp.float32)
        bound = 1.0 / np.sqrt(IN_DIM)
        W = jax.random.uniform(kw, (EMBED, IN_DIM), jnp.float32, -bound, bound)
        b = jax.random.uniform(kb, (EMBED,), jnp.float32, -bound, bound)
        return {'x': x, 'W': W, 'b': b}
    _L0_tok_all = _L0_tok_setup()
    _L0_tok_in = {k: v for k, v in _L0_tok_all.items() if k in ('W', 'b')}
    del _L0_tok_all

    def _L0_txt_setup():
        import jax, jax.numpy as jnp
        import numpy as np
        B, S, H = (8, 512, 192)
        VOCAB, MODAL_V, SEG_V, NPI_V, MAX_POS = (8000, 16, 4, 2500, 512)
        LN_EPS = 1e-12

        def _sinusoidal_table(max_pos, hidden):
            pos = np.arange(max_pos, dtype=np.float32)[:, None]
            idx = np.arange(hidden, dtype=np.float32)[None, :]
            angle = pos / np.power(10000.0, 2.0 * idx / hidden)
            tab = np.where(np.arange(hidden)[None, :] % 2 == 0, np.sin(angle), np.cos(angle))
            return jnp.asarray(tab, dtype=jnp.float32)

        def _time2vec(tau, w, b, w0, b0):
            t = tau[..., None]
            v1 = jnp.sin(t * w[0] + b)
            v2 = t * w0[0] + b0
            return jnp.concatenate([v1, v2], axis=-1)

        def _layer_norm(x, gamma, beta, eps):
            mu = jnp.mean(x, axis=-1, keepdims=True)
            var = jnp.mean(jnp.square(x - mu), axis=-1, keepdims=True)
            return (x - mu) * jax.lax.rsqrt(var + eps) * gamma + beta
        key = jax.random.key(seed)
        ks = jax.random.split(key, 16)
        inp = {'word_ids': jax.random.randint(ks[0], (B, S), 0, VOCAB), 'modalities_ids': jax.random.randint(ks[1], (B, S), 0, MODAL_V), 'seg_ids': jax.random.randint(ks[2], (B, S), 0, SEG_V), 'npi_ids': jax.random.randint(ks[3], (B, S), 0, NPI_V), 'posi_ids': jnp.sort(jax.random.randint(ks[4], (B, S), 0, MAX_POS), axis=-1), 'age_tau': jax.random.uniform(ks[5], (B, S), dtype=jnp.float32) * 100.0, 'delays_tau': jax.random.uniform(ks[6], (B, S), dtype=jnp.float32) * 100.0, 'word_table': jax.random.normal(ks[7], (VOCAB, H), dtype=jnp.float32) * 0.02, 'modalities_table': jax.random.normal(ks[8], (MODAL_V, H), dtype=jnp.float32) * 0.02, 'seg_table': jax.random.normal(ks[9], (SEG_V, H), dtype=jnp.float32) * 0.02, 'npi_table': jax.random.normal(ks[10], (NPI_V, H), dtype=jnp.float32) * 0.02, 'posi_table': _sinusoidal_table(MAX_POS, H), 'age_w': jax.random.normal(ks[11], (1, H - 1), dtype=jnp.float32), 'age_b': jax.random.normal(ks[12], (H - 1,), dtype=jnp.float32), 'age_w0': jax.random.normal(ks[13], (1, 1), dtype=jnp.float32), 'age_b0': jax.random.normal(ks[14], (1,), dtype=jnp.float32), 'delay_w': jax.random.normal(ks[15], (1, H - 1), dtype=jnp.float32), 'delay_b': jax.random.normal(jax.random.fold_in(key, 100), (H - 1,), dtype=jnp.float32), 'delay_w0': jax.random.normal(jax.random.fold_in(key, 101), (1, 1), dtype=jnp.float32), 'delay_b0': jax.random.normal(jax.random.fold_in(key, 102), (1,), dtype=jnp.float32), 'ln_gamma': jnp.ones((H,), dtype=jnp.float32), 'ln_beta': jnp.zeros((H,), dtype=jnp.float32)}
        return inp
    _L0_txt_all = _L0_txt_setup()
    _L0_txt_in = {k: v for k, v in _L0_txt_all.items() if k in ('word_table', 'modalities_table', 'seg_table', 'npi_table', 'posi_table', 'age_w', 'age_b', 'age_w0', 'age_b0', 'delay_w', 'delay_b', 'delay_w0', 'delay_b0', 'ln_gamma', 'ln_beta')}
    del _L0_txt_all

    def _L0_attn_setup():
        import jax, jax.numpy as jnp
        import numpy as np
        NUM_HEADS = 12
        NUM_LANDMARKS = 64
        PINV_ITERS = 6

        def moore_penrose_iter_pinv(x, iters=PINV_ITERS):
            abs_x = jnp.abs(x)
            col = abs_x.sum(axis=-1)
            row = abs_x.sum(axis=-2)
            z = jnp.swapaxes(x, -1, -2) / (jnp.max(col) * jnp.max(row))
            I = jnp.eye(x.shape[-1], dtype=x.dtype)
            for _ in range(iters):
                xz = x @ z
                z = 0.25 * z @ (13.0 * I - xz @ (15.0 * I - xz @ (7.0 * I - xz)))
            return z

        def _reference_tuple_inner(x, w_qkv, w_proj, b_proj):
            B, N, C = x.shape
            H = NUM_HEADS
            m = NUM_LANDMARKS
            d = C // H
            scale = d ** (-0.5)
            original_N = N
            rem = N % m
            if rem > 0:
                x = jnp.pad(x, ((0, 0), (m - rem, 0), (0, 0)))
                N = x.shape[1]
            qkv = x @ w_qkv.T
            q, k, v = jnp.split(qkv, 3, axis=-1)
            to_heads = lambda t: t.reshape(B, N, H, d).transpose(0, 2, 1, 3)
            q, k, v = (to_heads(q), to_heads(k), to_heads(v))
            q = q * scale
            l = N // m
            q_landmarks = q.reshape(B, H, m, l, d).mean(axis=3)
            k_landmarks = k.reshape(B, H, m, l, d).mean(axis=3)
            sim1 = jnp.einsum('bhnd,bhmd->bhnm', q, k_landmarks)
            sim2 = jnp.einsum('bhid,bhjd->bhij', q_landmarks, k_landmarks)
            sim3 = jnp.einsum('bhmd,bhnd->bhmn', q_landmarks, k)
            attn1 = jax.nn.softmax(sim1, axis=-1)
            attn2 = jax.nn.softmax(sim2, axis=-1)
            attn3 = jax.nn.softmax(sim3, axis=-1)
            attn2_inv = moore_penrose_iter_pinv(attn2, PINV_ITERS)
            attn = attn1 @ attn2_inv @ attn3
            out = attn1 @ (attn2_inv @ (attn3 @ v))
            out = out.transpose(0, 2, 1, 3).reshape(B, N, C)
            out = out[:, -original_N:]
            out = out @ w_proj.T + b_proj
            return (out, attn)
        key = jax.random.key(seed)
        k1, k2, k3, k4 = jax.random.split(key, 4)
        B, N, C = (2, 512, 192)
        x = jax.random.normal(k1, (B, N, C), dtype=jnp.float32)
        w_qkv = jax.random.normal(k2, (3 * C, C), dtype=jnp.float32) * 0.02
        w_proj = jax.random.normal(k3, (C, C), dtype=jnp.float32) * 0.02
        b_proj = jax.random.normal(k4, (C,), dtype=jnp.float32) * 0.02
        return {'x': x, 'w_qkv': w_qkv, 'w_proj': w_proj, 'b_proj': b_proj}
    _L0_attn_all = _L0_attn_setup()
    _L0_attn_in = {k: v for k, v in _L0_attn_all.items() if k in ('w_qkv', 'w_proj', 'b_proj')}
    del _L0_attn_all

    def _L0_ffn_setup():
        import jax, jax.numpy as jnp
        import numpy as np
        B, M, D = (32, 196, 192)
        N, P, H = (64, 1, 768)
        EPS = 1e-12

        def _l2norm(v, axis):
            n = jnp.sqrt(jnp.sum(v * v, axis=axis, keepdims=True))
            return v / jnp.maximum(n, EPS)
        key = jax.random.key(seed)
        ks = jax.random.split(key, 7)
        x = jax.random.normal(ks[0], (B, M, D), dtype=jnp.float32)
        phi = jax.random.normal(ks[1], (D, N, P), dtype=jnp.float32) * (1.0 / D ** 0.5)
        scale = jnp.ones((1,), dtype=jnp.float32)
        w1 = jax.random.normal(ks[2], (N, D, H), dtype=jnp.float32) * (1.0 / D ** 0.5)
        b1 = jnp.zeros((N, H), dtype=jnp.float32)
        w2 = jax.random.normal(ks[3], (N, H, D), dtype=jnp.float32) * (1.0 / H ** 0.5)
        b2 = jnp.zeros((N, D), dtype=jnp.float32)
        return {'x': x, 'phi': phi, 'scale': scale, 'w1': w1, 'b1': b1, 'w2': w2, 'b2': b2}
    _L0_ffn_all = _L0_ffn_setup()
    _L0_ffn_in = {k: v for k, v in _L0_ffn_all.items() if k in ('phi', 'scale', 'w1', 'b1', 'w2', 'b2')}
    del _L0_ffn_all
    return {'x': x, 'x_txt': x_txt, 'itok_BS_0_15': itok_BS_0_15, 'itok_BS_0_3': itok_BS_0_3, 'itok_BS_0_9999': itok_BS_0_9999, 'itok_BS_0_2047': itok_BS_0_2047, 'fside_BS_age_tau': fside_BS_age_tau, 'fside_BS_delays_tau': fside_BS_delays_tau, 'L0_tok_W': _L0_tok_in['W'], 'L0_tok_b': _L0_tok_in['b'], 'L0_txt_word_table': _L0_txt_in['word_table'], 'L0_txt_modalities_table': _L0_txt_in['modalities_table'], 'L0_txt_seg_table': _L0_txt_in['seg_table'], 'L0_txt_npi_table': _L0_txt_in['npi_table'], 'L0_txt_posi_table': _L0_txt_in['posi_table'], 'L0_txt_age_w': _L0_txt_in['age_w'], 'L0_txt_age_b': _L0_txt_in['age_b'], 'L0_txt_age_w0': _L0_txt_in['age_w0'], 'L0_txt_age_b0': _L0_txt_in['age_b0'], 'L0_txt_delay_w': _L0_txt_in['delay_w'], 'L0_txt_delay_b': _L0_txt_in['delay_b'], 'L0_txt_delay_w0': _L0_txt_in['delay_w0'], 'L0_txt_delay_b0': _L0_txt_in['delay_b0'], 'L0_txt_ln_gamma': _L0_txt_in['ln_gamma'], 'L0_txt_ln_beta': _L0_txt_in['ln_beta'], 'L0_attn_w_qkv': _L0_attn_in['w_qkv'], 'L0_attn_w_proj': _L0_attn_in['w_proj'], 'L0_attn_b_proj': _L0_attn_in['b_proj'], 'L0_ffn_phi': _L0_ffn_in['phi'], 'L0_ffn_scale': _L0_ffn_in['scale'], 'L0_ffn_w1': _L0_ffn_in['w1'], 'L0_ffn_b1': _L0_ffn_in['b1'], 'L0_ffn_w2': _L0_ffn_in['w2'], 'L0_ffn_b2': _L0_ffn_in['b2']}

def reference(x, x_txt, itok_BS_0_15, itok_BS_0_3, itok_BS_0_9999, itok_BS_0_2047, fside_BS_age_tau, fside_BS_delays_tau, L0_tok_W, L0_tok_b, L0_txt_word_table, L0_txt_modalities_table, L0_txt_seg_table, L0_txt_npi_table, L0_txt_posi_table, L0_txt_age_w, L0_txt_age_b, L0_txt_age_w0, L0_txt_age_b0, L0_txt_delay_w, L0_txt_delay_b, L0_txt_delay_w0, L0_txt_delay_b0, L0_txt_ln_gamma, L0_txt_ln_beta, L0_attn_w_qkv, L0_attn_w_proj, L0_attn_b_proj, L0_ffn_phi, L0_ffn_scale, L0_ffn_w1, L0_ffn_b1, L0_ffn_w2, L0_ffn_b2):
    import jax
    import jax.numpy as jnp

    def _L0_tok_ref(x, W, b):
        import jax, jax.numpy as jnp
        import numpy as np
        PATCH = 16
        EMBED = 192
        IN_DIM = PATCH * PATCH * 3

        def extract_patches(x, p):
            B, C, H, Wd = x.shape
            h, w = (H // p, Wd // p)
            xr = x.reshape(B, C, h, p, w, p)
            xr = xr.transpose(0, 2, 4, 3, 5, 1)
            return xr.reshape(B, h * w, p * p * C)
        patches = extract_patches(x, PATCH)
        return jnp.einsum('bnd,ed->bne', patches, W) + b

    def _L0_txt_ref(word_ids, modalities_ids, seg_ids, npi_ids, posi_ids, age_tau, delays_tau, word_table, modalities_table, seg_table, npi_table, posi_table, age_w, age_b, age_w0, age_b0, delay_w, delay_b, delay_w0, delay_b0, ln_gamma, ln_beta):
        import jax, jax.numpy as jnp
        import numpy as np
        B, S, H = (8, 512, 192)
        VOCAB, MODAL_V, SEG_V, NPI_V, MAX_POS = (8000, 16, 4, 2500, 512)
        LN_EPS = 1e-12

        def _sinusoidal_table(max_pos, hidden):
            pos = np.arange(max_pos, dtype=np.float32)[:, None]
            idx = np.arange(hidden, dtype=np.float32)[None, :]
            angle = pos / np.power(10000.0, 2.0 * idx / hidden)
            tab = np.where(np.arange(hidden)[None, :] % 2 == 0, np.sin(angle), np.cos(angle))
            return jnp.asarray(tab, dtype=jnp.float32)

        def _time2vec(tau, w, b, w0, b0):
            t = tau[..., None]
            v1 = jnp.sin(t * w[0] + b)
            v2 = t * w0[0] + b0
            return jnp.concatenate([v1, v2], axis=-1)

        def _layer_norm(x, gamma, beta, eps):
            mu = jnp.mean(x, axis=-1, keepdims=True)
            var = jnp.mean(jnp.square(x - mu), axis=-1, keepdims=True)
            return (x - mu) * jax.lax.rsqrt(var + eps) * gamma + beta
        word_e = word_table[word_ids]
        seg_e = seg_table[seg_ids]
        modal_e = modalities_table[modalities_ids]
        npi_e = npi_table[npi_ids]
        posi_e = posi_table[posi_ids]
        age_e = _time2vec(age_tau, age_w, age_b, age_w0, age_b0)
        delay_e = _time2vec(delays_tau, delay_w, delay_b, delay_w0, delay_b0)
        emb = word_e + seg_e + posi_e + modal_e + delay_e + age_e + npi_e
        emb = _layer_norm(emb, ln_gamma, ln_beta, LN_EPS)
        return emb

    def _L0_attn_ref(x, w_qkv, w_proj, b_proj):
        import jax, jax.numpy as jnp
        import numpy as np
        NUM_HEADS = 12
        NUM_LANDMARKS = 64
        PINV_ITERS = 6

        def moore_penrose_iter_pinv(x, iters=PINV_ITERS):
            abs_x = jnp.abs(x)
            col = abs_x.sum(axis=-1)
            row = abs_x.sum(axis=-2)
            z = jnp.swapaxes(x, -1, -2) / (jnp.max(col) * jnp.max(row))
            I = jnp.eye(x.shape[-1], dtype=x.dtype)
            for _ in range(iters):
                xz = x @ z
                z = 0.25 * z @ (13.0 * I - xz @ (15.0 * I - xz @ (7.0 * I - xz)))
            return z

        def _reference_tuple_inner(x, w_qkv, w_proj, b_proj):
            B, N, C = x.shape
            H = NUM_HEADS
            m = NUM_LANDMARKS
            d = C // H
            scale = d ** (-0.5)
            original_N = N
            rem = N % m
            if rem > 0:
                x = jnp.pad(x, ((0, 0), (m - rem, 0), (0, 0)))
                N = x.shape[1]
            qkv = x @ w_qkv.T
            q, k, v = jnp.split(qkv, 3, axis=-1)
            to_heads = lambda t: t.reshape(B, N, H, d).transpose(0, 2, 1, 3)
            q, k, v = (to_heads(q), to_heads(k), to_heads(v))
            q = q * scale
            l = N // m
            q_landmarks = q.reshape(B, H, m, l, d).mean(axis=3)
            k_landmarks = k.reshape(B, H, m, l, d).mean(axis=3)
            sim1 = jnp.einsum('bhnd,bhmd->bhnm', q, k_landmarks)
            sim2 = jnp.einsum('bhid,bhjd->bhij', q_landmarks, k_landmarks)
            sim3 = jnp.einsum('bhmd,bhnd->bhmn', q_landmarks, k)
            attn1 = jax.nn.softmax(sim1, axis=-1)
            attn2 = jax.nn.softmax(sim2, axis=-1)
            attn3 = jax.nn.softmax(sim3, axis=-1)
            attn2_inv = moore_penrose_iter_pinv(attn2, PINV_ITERS)
            attn = attn1 @ attn2_inv @ attn3
            out = attn1 @ (attn2_inv @ (attn3 @ v))
            out = out.transpose(0, 2, 1, 3).reshape(B, N, C)
            out = out[:, -original_N:]
            out = out @ w_proj.T + b_proj
            return (out, attn)
        return _reference_tuple_inner(x, w_qkv, w_proj, b_proj)[0]

    def _L0_ffn_ref(x, phi, scale, w1, b1, w2, b2):
        import jax, jax.numpy as jnp
        import numpy as np
        B, M, D = (32, 196, 192)
        N, P, H = (64, 1, 768)
        EPS = 1e-12

        def _l2norm(v, axis):
            n = jnp.sqrt(jnp.sum(v * v, axis=axis, keepdims=True))
            return v / jnp.maximum(n, EPS)
        xn = _l2norm(x, axis=2)
        phin = scale * _l2norm(phi, axis=0)
        logits = jnp.einsum('bmd,dnp->bmnp', xn, phin)
        d = jax.nn.softmax(logits, axis=1)
        b_, m_, n_, p_ = logits.shape
        c = jax.nn.softmax(logits.reshape(b_, m_, n_ * p_), axis=-1).reshape(b_, m_, n_, p_)
        xs = jnp.einsum('bmd,bmnp->bnpd', xn, d)
        h = jax.nn.gelu(jnp.einsum('bnpd,ndh->bnph', xs, w1) + b1[None, :, None, :], approximate=False)
        ys = jnp.einsum('bnph,nhd->bnpd', h, w2) + b2[None, :, None, :]
        y = jnp.einsum('bnpd,bmnp->bmd', ys, c)
        return y
    h = _L0_tok_ref(x, L0_tok_W, L0_tok_b)
    h = jnp.concatenate([h, _L0_txt_ref(x_txt, itok_BS_0_15, itok_BS_0_3, itok_BS_0_9999, itok_BS_0_2047, fside_BS_age_tau, fside_BS_delays_tau, L0_txt_word_table, L0_txt_modalities_table, L0_txt_seg_table, L0_txt_npi_table, L0_txt_posi_table, L0_txt_age_w, L0_txt_age_b, L0_txt_age_w0, L0_txt_age_b0, L0_txt_delay_w, L0_txt_delay_b, L0_txt_delay_w0, L0_txt_delay_b0, L0_txt_ln_gamma, L0_txt_ln_beta)], axis=1)
    h = h + _L0_attn_ref(_layernorm(h, axis=-1), L0_attn_w_qkv, L0_attn_w_proj, L0_attn_b_proj)
    h = h + _L0_ffn_ref(_layernorm(h, axis=-1), L0_ffn_phi, L0_ffn_scale, L0_ffn_w1, L0_ffn_b1, L0_ffn_w2, L0_ffn_b2)
    return h

_drawn_inputs = setup_inputs


def setup_inputs(seed=0):
    import zlib

    import numpy as np

    out = dict(_drawn_inputs(seed))
    spreads = {'L0_txt_ln_gamma': (1.0, 0.2),
     'L0_txt_ln_beta': (0.0, 0.1),
     'L0_ffn_b1': (0.0, 0.8),
     'L0_ffn_b2': (0.0, 0.8)}
    factors = {'L0_tok_b': 8.0,
     'L0_txt_word_table': 7.791,
     'L0_txt_modalities_table': 7.721,
     'L0_txt_seg_table': 7.692,
     'L0_txt_npi_table': 7.531,
     'L0_attn_b_proj': 3.621,
     'L0_ffn_phi': 8.0,
     'L0_ffn_w1': 8.0,
     'L0_ffn_w2': 8.0}
    for name, (base, spread) in spreads.items():
        noise = np.random.default_rng([zlib.crc32(name.encode()), seed]).standard_normal(out[name].shape)
        drawn = base * np.exp(spread * noise) if base else spread * noise
        out[name] = jnp.asarray(drawn.astype(out[name].dtype))
    for name, factor in factors.items():
        out[name] = (out[name] * factor).astype(out[name].dtype)
    return out
```

```python
from contextlib import ExitStack

import numpy as np

import concourse.bass as bass
from concourse import mybir

F32 = mybir.dt.float32
I32 = mybir.dt.int32
U32 = mybir.dt.uint32
ALU = mybir.AluOpType
ACT = mybir.ActivationFunctionType
AX = mybir.AxisListType
RMAX = bass.bass_isa.ReduceOp.max

P = 128
B, S, H = 16, 512, 192
NI = 16
N = S + NI
M = 64
PAD = (M - N % M) % M
NP = N + PAD
L = NP // M
NH, D = 12, H // 12
PAIRS = NH // 2
TT = S // P
NT = B * TT
K2 = H // 2
HW = 2 * M
EV = HW + D
ITERS = 6
NE, F = 64, 768
FC = F // P
TWO_PI = 2.0 * np.pi
MAGIC = 1.5 * 2.0 ** 23
SEED = float(0x5F3759DF)
VOCAB, NPI, POS, MODAL, SEG = 8000, 2500, 512, 16, 4


def constants():
    ident = np.eye(P, dtype=np.float32)
    mask = np.zeros((P, 8, M), np.float32)
    for r in range(P):
        mask[r, r // D] = D ** -0.5
    ones_bd = np.zeros((P, 2, D), np.float32)
    ones_bd[:M, 0] = 1.0
    ones_bd[M:, 1] = 1.0
    pick = np.zeros((P, MODAL * SEG), np.float32)
    for m in range(MODAL):
        for s in range(SEG):
            pick[m, SEG * m + s] = 1.0
            pick[MODAL + s, SEG * m + s] = 1.0
    return np.concatenate([ident, mask.reshape(P, -1), ones_bd.reshape(P, -1), pick], axis=1)


C_ID, C_MASK, C_ONES, C_PICK, C_ALL = 0, P, P + 8 * M, P + 8 * M + 2 * D, P + 8 * M + 2 * D + M


class Chain:

    def __init__(self, eng, sem):
        self.eng, self.sem, self.base, self.n = eng, sem, 0, 0

    def __call__(self, ins):
        ins.then_inc(self.sem, 1)
        self.n += 1

    def wait(self, back=0):
        self.eng.wait_ge(self.sem, self.base + (self.n - back))

    def link(self, ins):
        self(ins)
        self.wait()

    def enter(self, i, per):
        self.start, self.per = self.base + self.n, per
        self.base, self.n = self.start + i * per, 0

    def leave(self, turns, what):
        assert self.n == self.per, f"{what}: {self.n} in a turn, {self.per} given"
        self.base, self.n = self.start + self.per * turns, 0


ONE, DMA = 1, 16


def give(eng, ones, transfers, *slots):
    for s in ones + [s for x in slots for s in (*x.full_sem.values(), *x.free_sem.values())]:
        eng.sem_inc(s, ONE)
    for s in transfers:
        eng.sem_inc(s, DMA)


class Slots:

    def __init__(self, sem, name, products):
        self.uses, self.at = {}, {}
        for product, slot in products:
            self.at[product] = (slot, self.uses.get(slot, 0))
            self.uses[slot] = self.uses.get(slot, 0) + 1
        self.full_sem = {s: sem(f"{name}_{s}_full") for s in self.uses}
        self.free_sem = {s: sem(f"{name}_{s}_free") for s in self.uses}

    def turn(self, product, i):
        slot, k = self.at[product]
        return i * self.uses[slot] + k

    def claim(self, eng, product, i):
        eng.wait_ge(self.free_sem[self.at[product][0]], ONE + self.turn(product, i))

    def full(self, product):
        return self.full_sem[self.at[product][0]]

    def free(self, product):
        return self.free_sem[self.at[product][0]]

    def wait_full(self, eng, product, i):
        eng.wait_ge(self.full(product), ONE + self.turn(product, i) + 1)

    def wait_free(self, eng, product, i):
        eng.wait_ge(self.free(product), ONE + self.turn(product, i) + 1)


def spread(ap, parts):
    return bass.AP(tensor=ap.tensor, offset=ap.offset, ap=[[0, parts]] + [list(x) for x in ap.ap])


def rsqrt(nc, ch, y, t, v):
    ch.link(nc.vector.tensor_scalar(t.bitcast(I32), v.bitcast(I32), 1, None, ALU.logical_shift_right))
    ch.link(nc.vector.tensor_scalar(y.bitcast(I32), t.bitcast(I32), -1.0, SEED, ALU.mult, ALU.add))
    for _ in range(3):
        ch.link(nc.vector.tensor_tensor(t, y, y, ALU.mult))
        ch.link(nc.vector.scalar_tensor_tensor(t, t, -0.5, v, ALU.mult, ALU.mult))
        ch.link(nc.vector.scalar_tensor_tensor(y, t, 1.5, y, ALU.add, ALU.mult))


class Core:
    pass


def build(nc, t):
    with ExitStack() as ctx:
        def sb(name, shape, dt=F32, where=ctx):
            return where.enter_context(nc.sbuf_tensor(name, shape, dt))

        def sem(name):
            return ctx.enter_context(nc.semaphore(name))

        c = Core()
        c.psum = ctx.enter_context(nc.psum_tensor("psum", [P, 8, 512], F32))
        c.const = sb("const", [P, C_ALL])
        c.ident = c.const[:, C_ID:C_ID + P]
        c.mask = c.const[:, C_MASK:C_MASK + 8 * M].rearrange("p (h m) -> p h m", m=M)
        c.ones_bd = c.const[:, C_ONES:C_ONES + 2 * D]
        c.h = sb("h", [P, NT, H])
        c.h_img = sb("h_img", [NI, B, H])
        c.rsum = sb("rsum", [P, B, TT + 1])
        c.late_room = sb("late_room", [P, 2 * NE * 2 * B])
        c.xsT = c.late_room[0:K2 + 1, :].rearrange("p (k n b) -> p k n b", k=2, n=NE)
        late = ctx.enter_context(ExitStack())
        c.V = sb("V", [P, B, PAIRS, D], where=late)
        c.landk = sb("landk", [P, B, 2, M], where=late)
        c.wprojT = sb("wprojT", [P, 2, H], where=late)
        c.phin = sb("phin", [K2, 2, 2 * NE], where=late)
        c.q_dram = nc.dram_tensor("q_rows", (B, P, 2, N), F32, kind="Internal").ap()
        c.c_dram = nc.dram_tensor("router_rows", (B, NE, N), F32, kind="Internal").ap()
        c.y_dram = nc.dram_tensor("expert_rows", (NE, B, H), F32, kind="Internal").ap()
        c.x_dram = nc.dram_tensor("attn2_rows", (B, P, PAIRS, HW), F32, kind="Internal").ap()
        c.pair_dram = nc.dram_tensor("modal_seg_table", (MODAL * SEG, H), F32, kind="Internal").ap()
        with ExitStack() as three:
            c.E = sb("E", [P, B, PAIRS, M], where=three)
            c.rows = sb("rows", [P, B, PAIRS], where=three)
            c.cols = sb("cols", [P, B, PAIRS], where=three)
            with ExitStack() as two:
                used = 0

                def early(parts, *shape):
                    nonlocal used
                    size = int(np.prod(shape))
                    a = c.late_room[0:parts, used:used + size]
                    used += size
                    return a.rearrange("p (a b) -> p a b", b=shape[1]) if len(shape) == 2 else a
                c.wT = early(K2, 2, 640)
                c.turns_w = early(P, 2, H)
                c.turns_b = early(P, 2, H)
                c.gamma = early(P, H)
                c.beta = early(P, H)
                c.tau = early(P, 2, NT)
                c.linear = early(P, NT)
                c.hnT_img = early(K2, 2, B * NI)
                c.idx = sb("idx", [P, 4, NT], U32, where=two)
                with ExitStack() as work:
                    setup(nc, c, t, lambda n, s, d=F32: sb(n, s, d, work), sem)
                with ExitStack() as work:
                    landmarks(nc, c, t, lambda n, s, d=F32: sb("lm_" + n, s, d, work), sem)
            with ExitStack() as work:
                pseudo_inverse(nc, c, lambda n, s, d=F32: sb("pi_" + n, s, d, work), sem)
        with ExitStack() as work:
            attention(nc, c, lambda n, s, d=F32: sb("at_" + n, s, d, work), sem)
        late.close()
        with ExitStack() as work:
            experts(nc, c, t, lambda n, s, d=F32: sb("ex_" + n, s, d, work), sem)
        with ExitStack() as work:
            combine(nc, c, t, lambda n, s, d=F32: sb("co_" + n, s, d, work), sem)


def setup(nc, c, t, sb, sem):
    tokw = sb("tokw", [K2, 2, F])
    wq = sb("wq", [K2, 6, H])
    wp = sb("wp", [K2, 2, H])
    phi = sb("phi", [K2, 2, NE])
    phi_sq = sb("phi_sq", [K2, 2, NE])
    tokwT = sb("tokwT", [P, 6, H])
    room = c.h[:].rearrange("p k h -> p (k h)")
    img = room[0:3 * B, 0:4096]
    regrouped = room[0:3 * B, 4096:8192].rearrange("p (i j r q) -> p i j r q", i=4, j=4, r=16)
    patches = sb("patches", [P, 16, 2, 3 * B])
    tok_b = sb("tok_b", [NI, H])
    ids = sb("ids", [NT, 5, P], I32)
    idf = sb("idf", [NT, 5, P])
    below = sb("below", [NT, 5, P])
    taus = sb("taus", [NT, 2, P])
    tables = sb("tables", [MODAL + SEG, H])
    pair_rows = sb("pair_rows", [MODAL * SEG, H])
    lin_w = sb("lin_w", [P, 4])
    scale = sb("scale", [P, 1])
    ones = sb("ones", [P, P])
    tmp = sb("tmp", [P, NE])
    tmp2 = sb("tmp2", [P, NE])
    stats = sb("stats_i", [NI, B, 6])
    mv = sb("mv_i", [NI, B, 2])
    rstd = sb("rstd_i", [NI, B])
    hn_img = sb("hn_img", [NI, B, H])
    loaded, gp_loaded = sem("setup_loaded"), sem("setup_gp_loaded")
    pe, dve, act = sem("setup_pe"), sem("setup_dve"), sem("setup_act")
    regroup = sem("setup_regrouped")
    zeroed, stored = sem("setup_zeroed"), sem("setup_stored")
    ps = c.psum

    with nc.Block() as block:
        @block.sync
        def _(sp):
            n = 0

            def load(dst, src):
                nonlocal n
                sp.dma_start(dst, src).then_inc(loaded, 16)
                n += 16
            load(c.const[:], t["const"])
            load(tokw[:], t["L0_tok_W"].rearrange("(k p) f -> p k f", k=2))
            load(wq[:], t["L0_attn_w_qkv"].rearrange("(k p) f -> p k f", k=6))
            load(wp[:], t["L0_attn_w_proj"].rearrange("(k p) f -> p k f", k=2))
            load(phi[:], t["L0_ffn_phi"].rearrange("(k p) n o -> p k (n o)", k=2))
            load(img, t["x"].rearrange("b c h w -> (b c) (h w)"))
            load(tok_b[:], spread(t["L0_tok_b"], NI))
            for k, name in enumerate(("x_txt", "itok_BS_0_9999", "itok_BS_0_2047", "itok_BS_0_15", "itok_BS_0_3")):
                load(ids[:, k, :], t[name].rearrange("b (t p) -> (b t) p", p=P))
            for k, name in enumerate(("fside_BS_age_tau", "fside_BS_delays_tau")):
                load(taus[:, k, :], t[name].rearrange("b (t p) -> (b t) p", p=P))
            load(tables[0:MODAL, :], t["L0_txt_modalities_table"])
            load(tables[MODAL:MODAL + SEG, :], t["L0_txt_seg_table"])
            for k, name in enumerate(("age", "delay")):
                load(lin_w[:, k:k + 1], spread(t[f"L0_txt_{name}_w0"][0], P))
                load(lin_w[:, 2 + k:3 + k], spread(t[f"L0_txt_{name}_b0"], P))
            load(scale[:], spread(t["L0_ffn_scale"], P))
            load(c.gamma[:], spread(t["L0_txt_ln_gamma"], P))
            load(c.beta[:], spread(t["L0_txt_ln_beta"], P))
            sp.wait_ge(zeroed, 3)
            for k, name in enumerate(("age", "delay")):
                load(c.turns_w[:, k, 0:H - 1], spread(t[f"L0_txt_{name}_w"][0], P))
                load(c.turns_b[:, k, 0:H - 1], spread(t[f"L0_txt_{name}_b"], P))
            assert n == LOADED
            sp.wait_ge(dve, SETUP_DVE["pair_rows"])
            sp.dma_start(c.pair_dram, pair_rows[:]).then_inc(stored, 16)
            sp.wait_ge(dve, SETUP_DVE["proj"])
            sp.dma_start(c.wprojT[M:M + 1, 1, :], t["L0_attn_b_proj"].rearrange("(a h) -> a h", a=1)).then_inc(stored, 16)
            sp.wait_ge(stored, 32)

        @block.gpsimd
        def _(gp):
            nc.gpsimd.memset(c.turns_w[:], 0.0).then_inc(zeroed, 1)
            nc.gpsimd.memset(c.turns_b[:], 0.0).then_inc(zeroed, 1)
            nc.gpsimd.memset(ones[:], 1.0).then_inc(zeroed, 1)

        @block.tensor
        def _(te):
            te.wait_ge(loaded, LOADED)
            for k in range(6):
                ch, half = k // 2, k % 2
                if k >= 2:
                    te.wait_ge(dve, k - 1)
                for e in range(2):
                    src = tokw[:, e, 384 * half + ch:384 * half + 384:3]
                    last = nc.tensor.transpose(ps[:, k % 2, K2 * e:K2 * e + K2], src, c.ident[0:K2, 0:K2])
                last.then_inc(pe, 1)
            for k in range(6):
                te.wait_ge(dve, 5 + k)
                for e in range(2):
                    last = nc.tensor.transpose(ps[0:K2, k % 2, K2 * e:K2 * e + K2], wq[:, k, K2 * e:K2 * e + K2],
                                               c.ident[0:K2, 0:K2])
                last.then_inc(pe, 1)
            te.wait_ge(dve, SETUP_DVE["qkv"])
            for e in range(2):
                nc.tensor.transpose(ps[:, 0, K2 * e:K2 * e + K2], wp[:, e, 0:P], c.ident[0:K2, 0:K2])
                last = nc.tensor.transpose(ps[0:M, 1, K2 * e:K2 * e + K2], wp[:, e, P:H], c.ident[0:K2, 0:K2])
            last.then_inc(pe, 1)
            te.wait_ge(dve, SETUP_DVE["proj"])
            te.wait_ge(dve, SETUP_DVE["ids"])
            for k in range(4):
                nc.tensor.transpose(ps[:, 2, M * k:M * k + M], idf[:, k, :], c.ident[0:NT, 0:NT])
            for k in range(2):
                last = nc.tensor.transpose(ps[:, 3, M * k:M * k + M], taus[:, k, :], c.ident[0:NT, 0:NT])
            last.then_inc(pe, 1)
            nc.tensor.matmul(ps[0:MODAL * SEG, 4, 0:H], c.const[0:MODAL + SEG, C_PICK:C_PICK + M], tables[:],
                             start=True, stop=True).then_inc(pe, 1)
            te.wait_ge(dve, SETUP_DVE["phi_sq"])
            te.wait_ge(zeroed, 3)
            for k in range(2):
                last = nc.tensor.matmul(ps[:, 5, 0:NE], ones[0:K2, :], phi_sq[:, k, :], start=(k == 0), stop=(k == 1))
            last.then_inc(pe, 1)
            for i in range(4):
                te.wait_ge(regroup, i + 1)
                for j in range(4):
                    g = 4 * i + j
                    if g >= 2:
                        te.wait_ge(act, g - 1)
                    for half in range(2):
                        src = regrouped[:, i, j, 8 * half:8 * half + 8, :].rearrange("p r q -> p (r q)")
                        last = nc.tensor.transpose(ps[:, 6 + g % 2, 48 * half:48 * half + 48], src, c.ident[0:48, 0:48])
                    last.then_inc(pe, 1)
            te.wait_ge(act, 16)
            for g in range(4):
                if g >= 2:
                    te.wait_ge(dve, SETUP_DVE["embed"] + 4 * (g - 1))
                for k in range(6):
                    ch, half = k // 2, k % 2
                    for j in range(4):
                        b = 4 * g + j
                        last = nc.tensor.matmul(ps[32 * j:32 * j + NI, g % 2, 0:H], patches[:, :, half, 3 * b + ch],
                                                tokwT[:, k, :], start=(k == 0), stop=(k == 5))
                last.then_inc(pe, 1)
            te.wait_ge(dve, SETUP_DVE["hn_img"])
            for b in range(B):
                for k in range(2):
                    last = nc.tensor.transpose(ps[0:K2, 2, 256 * k + NI * b:256 * k + NI * b + NI],
                                               hn_img[:, b, K2 * k:K2 * k + K2], c.ident[0:NI, 0:NI])
            last.then_inc(pe, 1)

        @block.scalar
        def _(sc):
            sc.wait_ge(loaded, LOADED)
            for i in range(4):
                src = img[:, 1024 * i:1024 * i + 1024].rearrange("p (r j q) -> p j r q", r=16, j=4)
                nc.scalar.activation(regrouped[:, i], src, ACT.Copy).then_inc(regroup, 1)
            for g in range(16):
                sc.wait_ge(pe, 17 + g)
                nc.scalar.activation(patches[:, g, :, :].rearrange("p h f -> p (h f)"), ps[:, 6 + g % 2, 0:96],
                                     ACT.Copy).then_inc(act, 1)
            sc.wait_ge(pe, 37)
            nc.scalar.activation(c.hnT_img[:], ps[0:K2, 2, 0:512].rearrange("p (k n) -> p k n", k=2),
                                 ACT.Copy).then_inc(act, 1)

        @block.vector
        def _(v):
            ch = Chain(v, dve)

            def mark(name):
                assert ch.n == SETUP_DVE[name], (name, ch.n)
            for k in range(6):
                v.wait_ge(pe, k + 1)
                ch(nc.vector.tensor_copy(tokwT[:, k, :], ps[:, k % 2, 0:H]))
            for k in range(6):
                v.wait_ge(pe, 7 + k)
                part, lo = k // 2, 96 * (k % 2)
                runs = []
                if part == 0:
                    runs = [(lo, lo + 96, 0)] + ([(128, 192, 128)] if lo else [])
                elif part == 1:
                    runs = [(0, 96, 320)] if lo == 0 else [(96, 128, 320), (128, 192, 64)]
                else:
                    runs = [(lo, lo + 96, 448)]
                for r0, r1, off in runs:
                    src = ps[0:K2, k % 2, 0:H].rearrange("p (e r) -> p e r", e=2)[:, :, r0 - lo:r1 - lo]
                    dst = c.wT[:, :, r0 + off:r1 + off]
                    ins = nc.vector.tensor_copy(dst, src)
                ch(ins)
            mark("qkv")
            v.wait_ge(pe, 13)
            ch(nc.vector.tensor_copy(c.wprojT[:, 0, :], ps[:, 0, 0:H]))
            ch(nc.vector.tensor_copy(c.wprojT[0:M, 1, :], ps[0:M, 1, 0:H]))
            mark("proj")
            v.wait_ge(loaded, LOADED)
            for k, size in enumerate((VOCAB, NPI, POS, MODAL, SEG)):
                ch(nc.vector.tensor_scalar(below[:, k, :], ids[:, k, :], 0.0, float(size), ALU.is_lt, ALU.mult))
            for k in range(5):
                ch.wait(4)
                ch(nc.vector.tensor_tensor(idf[:, k, :], ids[:, k, :], below[:, k, :], ALU.add))
            for k, size in enumerate((VOCAB, NPI, POS, MODAL, SEG)):
                ch.wait(4)
                ch(nc.vector.tensor_scalar(idf[:, k, :], idf[:, k, :], 0.0, float(size - 1), ALU.max, ALU.min))
            ch.wait()
            ch.link(nc.vector.scalar_tensor_tensor(idf[:, 3, :], idf[:, 3, :], float(SEG), idf[:, 4, :], ALU.mult, ALU.add))
            mark("ids")
            ch.link(nc.vector.tensor_tensor(phi_sq[:], phi[:], phi[:], ALU.mult))
            mark("phi_sq")
            v.wait_ge(pe, 14)
            ch(nc.vector.tensor_copy(c.idx[:], ps[:, 2, 0:4 * NT].rearrange("p (k n) -> p k n", k=4)))
            ch.link(nc.vector.tensor_copy(c.tau[:], ps[:, 3, 0:2 * NT].rearrange("p (k n) -> p k n", k=2)))
            v.wait_ge(pe, 15)
            ch(nc.vector.tensor_copy(pair_rows[:], ps[0:MODAL * SEG, 4, 0:H]))
            mark("pair_rows")
            ch.link(nc.vector.tensor_scalar(c.linear[:], c.tau[:, 0, :], lin_w[:, 0:1], lin_w[:, 2:3], ALU.mult, ALU.add))
            ch.link(nc.vector.scalar_tensor_tensor(c.linear[:], c.tau[:, 1, :], lin_w[:, 1:2], c.linear[:], ALU.mult, ALU.add))
            ch.link(nc.vector.tensor_scalar(c.linear[:], c.linear[:], lin_w[:, 3:4], None, ALU.add))
            ch(nc.vector.tensor_scalar(c.turns_w[:], c.turns_w[:], 1.0 / TWO_PI, None, ALU.mult))
            ch(nc.vector.tensor_scalar(c.turns_b[:], c.turns_b[:], 1.0 / TWO_PI, None, ALU.mult))
            v.wait_ge(pe, 16)
            ch.link(nc.vector.tensor_scalar(tmp2[:], ps[:, 5, 0:NE], 1e-24, None, ALU.max))
            y = sb("phi_rn", [P, NE])
            rsqrt(nc, ch, y[:], tmp[:], tmp2[:])
            ch.link(nc.vector.tensor_scalar(y[:], y[:], scale[:, 0:1], None, ALU.mult))
            for k in range(2):
                for j in range(2):
                    ch(nc.vector.tensor_tensor(c.phin[:, k, NE * j:NE * j + NE], phi[:, k, :], y[0:K2, :], ALU.mult))
            mark("embed")
            for g in range(4):
                v.wait_ge(pe, 33 + g)
                for j in range(4):
                    ch(nc.vector.tensor_tensor(c.h_img[:, 4 * g + j, :], ps[32 * j:32 * j + NI, g % 2, 0:H], tok_b[:], ALU.add))
            ch.wait()
            layer_norm(nc, ch, c.h_img, hn_img, stats, mv, rstd, sb("rt_i", [NI, B]), sb("ve_i", [NI, B]), range(B), 1e-5)
            mark("hn_img")


LOADED = 16 * 27
SETUP_DVE = dict(qkv=12, proj=14, ids=30, phi_sq=31, pair_rows=34, embed=56, hn_img=132)


def layer_norm(nc, ch, src, dst, stats, mv, rstd, rt, ve, tiles, eps, ready=None):
    n = len(tiles)
    for k in tiles:
        ch(nc.vector.bn_stats(stats[:, k, :], src[:, k, :]))
    ch.wait()
    nc.vector.tensor_copy(rt[:, 0:1], stats[:, 0, 0:1])
    for k in tiles:
        ch(nc.vector.bn_aggr(mv[:, k, :], stats[:, k, :]))
    ch.wait()
    ch.link(nc.vector.tensor_scalar(ve[:, 0:n], mv[:, 0:n, 1], eps, None, ALU.add))
    rsqrt(nc, ch, rstd[:, 0:n], rt[:, 0:n], ve[:, 0:n])
    for k in tiles:
        ins = nc.vector.tensor_scalar(dst[:, k, :], src[:, k, :], mv[:, k, 0:1], rstd[:, k:k + 1], ALU.subtract, ALU.mult)
        if ready is None or k != tiles[-1]:
            ch(ins)
        else:
            ins.then_inc(ready, 1)
    if ready is None:
        ch.wait()


HALF = NP // 2
LM_PRODUCTS = [("hnT0", "A0"), ("hnT1", "A1"), ("hnT2", "A2"), ("hnT3", "A3"),
               ("k2a", "A0"), ("k2b", "A1"), ("land", "A2"), ("q1a", "A3"), ("q1b", "A0"), ("q0a", "A1"), ("q0b", "A2"),
               ("sim2", "A3"), ("v01", "A0"), ("v23", "A1"), ("v4", "A2")]
for _p in range(PAIRS):
    LM_PRODUCTS += [(f"sim3_{_p}", f"S{_p % 2}"), (f"p3T_{_p}", "A1" if _p % 2 else "A3"), (f"p3I_{_p}", "A2")]
LM_PRODUCTS += [("xT0", "A0"), ("xT1", "A1"), ("u", "A2"), ("x0", "A3"), ("x1", "A0"), ("uT", "A1")]
LM_DVE = 74


def landmarks(nc, c, t, sb, sem):
    got = sb("got", [P, TT, 4, H])
    emb = sb("emb", [P, TT, H])
    turns = sb("turns", [P, TT, 2, H])
    whole = sb("whole", [P, TT, 2, H])
    hn = sb("hn", [P, TT, H])
    hnT = sb("hnT", [K2, 2, NP])
    hnl = sb("hnl", [K2, 2, M])
    q0 = sb("q0", [P, 2, N])
    k1 = sb("k1", [P, NP])
    k2 = sb("k2", [P, NP])
    v = sb("v", [P, TT + 1, H])
    land = sb("land", [P, 4, M])
    ql = sb("ql", [P, 12, M])
    w2 = sb("w2", [P, PAIRS, M])
    e2 = sb("e2", [P, PAIRS, M])
    small = sb("small", [P, 6, PAIRS])
    x2 = sb("x2", [P, PAIRS, HW])
    x2T = sb("x2T", [P, PAIRS, HW])
    p3 = sb("p3", [P, 2, NP])
    p3T = sb("p3T", [P, TT + 1, PAIRS, HW])
    u = sb("u", [P, 2, HW])
    stats, mv = sb("stats", [P, TT, 6]), sb("mv", [P, TT, 2])
    rstd, rt, ve = sb("rstd", [P, TT]), sb("rt", [P, TT]), sb("ve", [P, TT])
    S = Slots(sem, "lm", LM_PRODUCTS)
    slot = {"A0": 0, "A1": 1, "A2": 2, "A3": 3, "S0": 4, "S1": 6}

    def bank(product):
        return slot[S.at[product][0]]
    cleared = sem("lm_cleared")
    gathered, summed, paired, emb_in = sem("lm_gathered"), sem("lm_summed"), sem("lm_paired"), sem("lm_emb_in")
    turned, rounded, reduced, sined = sem("lm_turned"), sem("lm_rounded"), sem("lm_reduced"), sem("lm_sined")
    hn_ready, img_in, hnT_in = sem("lm_hn_ready"), sem("lm_img_in"), sem("lm_hnT_in")
    hnl_ready, ql_ready = sem("lm_hnl_ready"), sem("lm_ql_ready")
    sub2, exp2, x2_ready, max3, exp3 = sem("lm_sub2"), sem("lm_exp2"), sem("lm_x2_ready"), sem("lm_max3"), sem("lm_exp3")
    x2_stored = sem("lm_x2_stored")
    q_stored = sem("lm_q_stored")
    dve_done, act_done, gp_done = sem("lm_dve"), sem("lm_act"), sem("lm_gp")
    ps = c.psum

    with nc.Block() as block:
        @block.gpsimd
        def _(gp):
            nc.gpsimd.memset(hnT[:], 0.0).then_inc(cleared, 1)
            nc.gpsimd.memset(x2[:], 0.0).then_inc(cleared, 1)
            nc.gpsimd.memset(c.landk[:, :, 0:1, :], 0.0).then_inc(cleared, 1)

            idx_b, spare = sb("idx_b", [P, 4, TT], U32), sb("spare", [P, 1])

            def gathers(b):
                nc.gpsimd.tensor_copy(idx_b[:], c.idx[:, :, bass.ds(b * TT, TT)]).then_inc(gp_done, 1)
                gp.wait_ge(gp_done, b + 1)
                nc.gpsimd.tensor_tensor(spare[:], c.const[:, 0:1], c.const[:, 0:1], ALU.add)
                for k in range(TT):
                    for r, table in enumerate(("L0_txt_word_table", "L0_txt_npi_table", "L0_txt_posi_table", None)):
                        gp.indirect_dma_start(out=got[:, k, r, :], out_offset=None, in_=t[table] if table else c.pair_dram,
                                              in_offset=bass.IndirectOffsetOnAxis(ap=idx_b[:, r, k:k + 1], axis=0)
                                              ).then_inc(gathered, 16)

            with gp.Fori(0, B) as b:
                gp.wait_ge(emb_in, ONE + b)
                gathers(b)
                gp.wait_ge(gathered, b * (16 * 4 * TT) + 16 * 4 * TT)
                nc.gpsimd.tensor_tensor(got[:, :, 0:2, :], got[:, :, 0:2, :], got[:, :, 2:4, :], ALU.add).then_inc(paired, 1)
                gp.wait_ge(paired, b + 1)
                gp.wait_ge(summed, ONE + b)
                nc.gpsimd.tensor_tensor(emb[:], got[:, :, 0, :], got[:, :, 1, :], ALU.add).then_inc(emb_in, 1)

        @block.sync
        def _(sp):
            give(sp, [emb_in, summed, exp3], [q_stored, x2_stored], S)
            def store(b):
                S.wait_free(sp, "q0b", b)
                S.wait_free(sp, "q1b", b)
                S.wait_free(sp, "q0a", b)
                sp.dma_start(c.q_dram[b], q0[:]).then_inc(q_stored, 16)
                sp.wait_ge(x2_ready, b + 1)
                sp.dma_start(c.x_dram[b], x2[:]).then_inc(x2_stored, 16)
            with sp.Fori(0, B) as b:
                store(b)
            sp.wait_ge(q_stored, DMA + 16 * B)
            sp.wait_ge(x2_stored, DMA + 16 * B)

        @block.tensor
        def _(te):
            te.wait_ge(cleared, 3)

            def turn(b):
                te.wait_ge(hn_ready, b + 1)
                for k in range(TT):
                    S.claim(te, f"hnT{k}", b)
                    for e in range(2):
                        last = nc.tensor.transpose(ps[0:K2, bank(f"hnT{k}"), P * e:P * e + P],
                                                   hn[:, k, K2 * e:K2 * e + K2], c.ident)
                    last.then_inc(S.full(f"hnT{k}"), 1)
                for k in range(TT):
                    S.wait_free(te, f"hnT{k}", b)
                te.wait_ge(img_in, b + 1)

                def rows(product, lo, c0, width):
                    S.claim(te, product, b)
                    for e in range(2):
                        last = nc.tensor.matmul(ps[:, bank(product), 0:width], c.wT[:, e, lo:lo + P],
                                                hnT[:, e, c0:c0 + width], start=(e == 0), stop=(e == 1))
                    last.then_inc(S.full(product), 1)
                rows("k2a", 320, 0, HALF)
                rows("k2b", 320, HALF, HALF)
                te.wait_ge(hnl_ready, b + 1)
                S.claim(te, "land", b)
                for k, lo in enumerate((0, 128, 192, 320)):
                    for e in range(2):
                        last = nc.tensor.matmul(ps[:, bank("land"), M * k:M * k + M], c.wT[:, e, lo:lo + P], hnl[:, e, :],
                                                start=(e == 0), stop=(e == 1))
                last.then_inc(S.full("land"), 1)
                rows("q1a", 128, 0, HALF)
                rows("q1b", 128, HALF, HALF)
                rows("q0a", 0, PAD, N // 2)
                rows("q0b", 0, PAD + N // 2, N // 2)
                te.wait_ge(ql_ready, b + 1)
                S.claim(te, "sim2", b)
                for p in range(PAIRS):
                    last = nc.tensor.matmul(ps[:, bank("sim2"), M * p:M * p + M], ql[:, 2 * p:2 * p + 2, :],
                                            land[:, 3 if p < 4 else 1, :], start=True, stop=True)
                last.then_inc(S.full("sim2"), 1)
                for k in range(TT + 1):
                    product = ("v01", "v23", "v4")[k // 2]
                    rows_n, c0 = (P, PAD + NI + P * k) if k < TT else (NI, PAD)
                    if k % 2 == 0:
                        S.claim(te, product, b)
                    for e in range(2):
                        last = nc.tensor.matmul(ps[0:rows_n, bank(product), H * (k % 2):H * (k % 2) + H],
                                                hnT[:, e, c0:c0 + rows_n], c.wT[:, e, 448:640],
                                                start=(e == 0), stop=(e == 1))
                    if k % 2 or k == TT:
                        last.then_inc(S.full(product), 1)

                def scores(p):
                    product = f"sim3_{p}"
                    if p == 0:
                        S.wait_free(te, "k2b", b)
                    if p == 4:
                        S.wait_free(te, "q1b", b)
                    te.wait_ge(exp3, ONE + b * PAIRS + max(p - 1, 0))
                    src = k2 if p < 4 else k1
                    nc.tensor.matmul(ps[:, bank(product), 0:512], ql[:, 2 * p:2 * p + 2, :], src[:, 0:512], start=True, stop=True)
                    nc.tensor.matmul(ps[:, bank(product) + 1, 0:NP - 512], ql[:, 2 * p:2 * p + 2, :], src[:, 512:NP],
                                     start=True, stop=True).then_inc(S.full(product), 1)

                def turn_probs(p):
                    te.wait_ge(exp3, ONE + b * PAIRS + (p + 1))
                    S.claim(te, f"p3T_{p}", b)
                    S.claim(te, f"p3I_{p}", b)
                    for k in range(TT):
                        c0 = PAD + NI + P * k
                        last = nc.tensor.transpose(ps[:, bank(f"p3T_{p}"), HW * k:HW * k + HW], p3[:, p % 2, c0:c0 + P], c.ident)
                    last.then_inc(S.full(f"p3T_{p}"), 1)
                    nc.tensor.transpose(ps[0:NI, bank(f"p3I_{p}"), 0:HW], p3[:, p % 2, PAD:PAD + NI], c.ident
                                        ).then_inc(S.full(f"p3I_{p}"), 1)
                scores(0)
                scores(1)
                for p in range(PAIRS):
                    turn_probs(p)
                    if p + 2 < PAIRS:
                        scores(p + 2)
                te.wait_ge(x2_ready, b + 1)
                for g in range(2):
                    S.claim(te, f"xT{g}", b)
                    for k in range(3):
                        last = nc.tensor.transpose(ps[:, bank(f"xT{g}"), HW * k:HW * k + HW], x2[:, 3 * g + k, :], c.ident)
                    last.then_inc(S.full(f"xT{g}"), 1)
                S.claim(te, "u", b)
                S.wait_free(te, f"p3T_{PAIRS - 1}", b)
                S.wait_free(te, f"p3I_{PAIRS - 1}", b)
                S.wait_free(te, f"p3T_{PAIRS - 2}", b)
                for g in range(2):
                    for k in range(TT + 1):
                        n = P if k < TT else NI
                        for p in range(4 * g, min(4 * g + 4, PAIRS)):
                            j = p % 4
                            last = nc.tensor.matmul(ps[32 * j:32 * j + 32, bank("u"), HW * g:HW * g + HW],
                                                    v[0:n, k, 32 * p:32 * p + 32], p3T[0:n, k, p, :],
                                                    start=(k == 0), stop=(k == TT))
                last.then_inc(S.full("u"), 1)
                for g in range(2):
                    S.wait_free(te, f"xT{g}", b)
                    S.claim(te, f"x{g}", b)
                    for k in range(3):
                        last = nc.tensor.matmul(ps[:, bank(f"x{g}"), HW * k:HW * k + HW], x2T[:, 3 * g + k, :],
                                                x2T[:, 3 * g + k, :], start=True, stop=True)
                    last.then_inc(S.full(f"x{g}"), 1)
                S.wait_free(te, "u", b)
                S.claim(te, "uT", b)
                nc.tensor.transpose(ps[:, bank("uT"), 0:P], u[:, 0, :], c.ident)
                nc.tensor.transpose(ps[:, bank("uT"), P:P + M], u[0:M, 1, :], c.ident[0:M, 0:M]).then_inc(S.full("uT"), 1)
            with te.Fori(0, B) as b:
                turn(b)

        @block.scalar
        def _(sc):
            def copy(dst, src, scale=1.0):
                return nc.scalar.activation(dst, src, ACT.Copy, scale=scale)

            def rounds(b):
                sc.wait_ge(turned, b + 1)
                nc.scalar.activation(whole[:], turns[:], ACT.Copy, bias=MAGIC).then_inc(rounded, 1)

            def sines(b):
                sc.wait_ge(reduced, b + 1)
                nc.scalar.activation(whole[:], turns[:], ACT.Sin, scale=-TWO_PI).then_inc(sined, 1)

            def turn(b, with_text):
                if not isinstance(b, int):
                    pass
                sc.wait_ge(S.full("v4"), ONE + b * S.uses["A2"])
                copy(hnT[:, :, PAD:PAD + NI], c.hnT_img[:, :, bass.ds(b * NI, NI)]).then_inc(img_in, 1)
                for k in range(TT):
                    S.wait_full(sc, f"hnT{k}", b)
                    c0 = PAD + NI + P * k
                    copy(hnT[:, :, c0:c0 + P], ps[0:K2, bank(f"hnT{k}"), 0:2 * P].rearrange("p (e n) -> p e n", e=2)
                         ).then_inc(S.free(f"hnT{k}"), 1)
                for part, half in (("k2a", 0), ("k2b", 1)):
                    S.wait_full(sc, part, b)
                    copy(k2[:, HALF * half:HALF * half + HALF], ps[:, bank(part), 0:HALF]).then_inc(S.free(part), 1)
                S.wait_full(sc, "land", b)
                copy(land[:], ps[:, bank("land"), 0:4 * M].rearrange("p (k m) -> p k m", k=4), 1.0 / L
                     ).then_inc(S.free("land"), 1)
                sc.wait_ge(q_stored, DMA + b * 16)
                for part, half in (("q1a", 0), ("q1b", 1)):
                    S.wait_full(sc, part, b)
                    copy(k1[:, HALF * half:HALF * half + HALF], ps[:, bank(part), 0:HALF]).then_inc(act_done, 1)
                    if half == 0:
                        copy(q0[:, 1, 0:HALF - PAD], ps[:, bank(part), PAD:HALF]).then_inc(S.free(part), 1)
                    else:
                        copy(q0[:, 1, HALF - PAD:N], ps[:, bank(part), 0:HALF]).then_inc(S.free(part), 1)
                for part, half in (("q0a", 0), ("q0b", 1)):
                    S.wait_full(sc, part, b)
                    copy(q0[:, 0, N // 2 * half:N // 2 * half + N // 2], ps[:, bank(part), 0:N // 2]).then_inc(S.free(part), 1)
                if with_text:
                    rounds(b + 1)
                    sines(b + 1)
                sc.wait_ge(sub2, b + 1)
                nc.scalar.activation(e2[:], w2[:], ACT.Exp).then_inc(exp2, 1)
                for p in range(PAIRS):
                    sc.wait_ge(max3, b * PAIRS + (p + 1))
                    if p >= 2:
                        S.wait_full(sc, f"p3I_{p - 2}", b)
                    src = ps[:, bank(f"sim3_{p}"):bank(f"sim3_{p}") + 2, :].rearrange("p k n -> p (k n)")[:, 0:NP]
                    nc.scalar.activation(p3[:, p % 2, :], src, ACT.Exp, bias=small[:, 3, p:p + 1],
                                         accum_out=small[:, 4, p:p + 1]).then_inc(exp3, 1)
                    S.wait_full(sc, f"p3I_{p}", b)
                    copy(p3T[0:NI, TT, p, :], ps[0:NI, bank(f"p3I_{p}"), 0:HW]).then_inc(S.free(f"p3I_{p}"), 1)
                for g in range(2):
                    S.wait_full(sc, f"xT{g}", b)
                    copy(x2T[:, 3 * g:3 * g + 3, :], ps[:, bank(f"xT{g}"), 0:3 * HW].rearrange("p (k m) -> p k m", k=3)
                         ).then_inc(S.free(f"xT{g}"), 1)
            rounds(0)
            sines(0)
            with sc.Fori(0, B - 1) as b:
                turn(b, True)
            turn(B - 1, False)

        @block.vector
        def _(ve_):
            ch = Chain(ve_, dve_done)

            def angles(b):
                for k in range(TT):
                    for j in range(2):
                        ch(nc.vector.scalar_tensor_tensor(turns[:, k, j, :], c.turns_w[:, j, :],
                                                          c.tau[:, j, bass.ds(b * TT + k, 1)], c.turns_b[:, j, :], ALU.mult, ALU.add)) \
                            if (k, j) != (TT - 1, 1) else \
                            nc.vector.scalar_tensor_tensor(turns[:, k, j, :], c.turns_w[:, j, :],
                                                           c.tau[:, j, bass.ds(b * TT + k, 1)], c.turns_b[:, j, :],
                                                           ALU.mult, ALU.add).then_inc(turned, 1)

            def fractions(b):
                ve_.wait_ge(rounded, b + 1)
                ve_.wait_ge(turned, b + 1)
                nc.vector.scalar_tensor_tensor(turns[:].rearrange("p a j h -> p (a j h)"), whole[:].rearrange("p a j h -> p (a j h)"),
                                               MAGIC, turns[:].rearrange("p a j h -> p (a j h)"), ALU.subtract, ALU.subtract
                                               ).then_inc(reduced, 1)

            def embed(b):
                ve_.wait_ge(sined, b + 1)
                ve_.wait_ge(emb_in, ONE + b + 1)
                ht = c.h[:, bass.ds(b * TT, TT), :] if not isinstance(b, int) else c.h[:, TT * b:TT * b + TT, :]
                ch.link(nc.vector.tensor_tensor(hn[:], emb[:], whole[:, :, 0, :], ALU.add))
                nc.vector.tensor_tensor(hn[:], hn[:], whole[:, :, 1, :], ALU.add).then_inc(summed, 1)
                ve_.wait_ge(summed, ONE + b + 1)
                ch.link(nc.vector.tensor_tensor(hn[:, :, H - 1], hn[:, :, H - 1], c.linear[:, bass.ds(b * TT, TT)], ALU.add))
                layer_norm(nc, ch, hn, hn, stats, mv, rstd, rt, ve, range(TT), 1e-12)
                ch.link(nc.vector.tensor_tensor(hn[:], hn[:], c.gamma[:].unsqueeze(1).to_broadcast([P, TT, H]), ALU.mult))
                ch.link(nc.vector.tensor_tensor(hn[:], hn[:], c.beta[:].unsqueeze(1).to_broadcast([P, TT, H]), ALU.add))
                ch(nc.vector.tensor_copy(ht, hn[:]))
                layer_norm(nc, ch, hn, hn, stats, mv, rstd, rt, ve, range(TT), 1e-5, hn_ready)

            def turn(b, with_text):
                S.wait_free(ve_, "hnT3", b)
                ve_.wait_ge(img_in, b + 1)
                nc.vector.tensor_reduce(hnl[:], hnT[:].rearrange("p e (m l) -> p e m l", l=L), AX.X, ALU.add
                                        ).then_inc(hnl_ready, 1)
                if with_text:
                    angles(b + 1)
                S.wait_free(ve_, "land", b)
                ch(nc.vector.tensor_tensor(ql[:, 0:8, :], c.mask, land[:, 0:1, :].to_broadcast([P, 8, M]), ALU.mult))
                nc.vector.tensor_tensor(ql[:, 8:12, :], c.mask[:, 4:8, :], land[:, 2:3, :].to_broadcast([P, 4, M]), ALU.mult
                                        ).then_inc(ql_ready, 1)
                ch(nc.vector.tensor_copy(c.landk[:, bass.ds(b, 1), :, :].rearrange("p b k m -> p (b k) m"), land[:, 2:4, :]))
                if with_text:
                    fractions(b + 1)
                S.wait_full(ve_, "sim2", b)
                sim2 = ps[:, bank("sim2"), 0:PAIRS * M].rearrange("p (k m) -> p k m", m=M)
                ch.link(nc.vector.tensor_reduce(small[:, 0, :], sim2, AX.X, ALU.max, negate=True))
                ch(nc.vector.tensor_tensor(w2[:], sim2, small[:, 0, :].unsqueeze(2).to_broadcast([P, PAIRS, M]), ALU.add))
                ch.wait()
                ch.link(nc.vector.tensor_copy(small[:, 5, :], small[:, 0, :]))
                nc.vector.tensor_copy(small[:, 1, :], small[:, 0, :]).then_inc(sub2, 1)
                nc.vector.tensor_copy(small[:, 2, :], small[:, 0, :]).then_inc(S.free("sim2"), 1)
                for k, part in enumerate(("v01", "v23", "v4")):
                    S.wait_full(ve_, part, b)
                    if k < 2:
                        nc.vector.tensor_copy(v[:, 2 * k:2 * k + 2, :], ps[:, bank(part), 0:2 * H].rearrange("p (k h) -> p k h", k=2)
                                              ).then_inc(S.free(part), 1)
                    else:
                        nc.vector.tensor_copy(v[0:NI, TT, :], ps[0:NI, bank(part), 0:H]).then_inc(S.free(part), 1)
                ve_.wait_ge(exp2, b + 1)
                ve_.wait_ge(S.free("sim2"), S.turn("sim2", b) + 1)
                ch.link(nc.vector.tensor_reduce(small[:, 1, :], e2[:], AX.X, ALU.add))
                ch.link(nc.vector.reciprocal(small[:, 2, :], small[:, 1, :]))
                ve_.wait_ge(x2_stored, DMA + b * 16)
                ch(nc.vector.tensor_tensor(x2[0:M, :, 0:M], e2[0:M], small[0:M, 2, :].unsqueeze(2).to_broadcast([M, PAIRS, M]), ALU.mult))
                nc.vector.tensor_tensor(x2[M:P, :, M:HW], e2[M:P], small[M:P, 2, :].unsqueeze(2).to_broadcast([M, PAIRS, M]), ALU.mult
                                        ).then_inc(x2_ready, 1)
                ve_.wait_ge(x2_ready, b + 1)
                ch(nc.vector.tensor_reduce(c.rows[:, bass.ds(b, 1), :].rearrange("p b k -> p (b k)"), x2[:], AX.X, ALU.add))

                for p in range(PAIRS):
                    S.wait_full(ve_, f"sim3_{p}", b)
                    src = ps[:, bank(f"sim3_{p}"):bank(f"sim3_{p}") + 2, :].rearrange("p k n -> p (k n)")[:, 0:NP]
                    nc.vector.tensor_reduce(small[:, 3, p:p + 1], src, AX.X, ALU.max, negate=True).then_inc(max3, 1)
                    if p:
                        probs_out(p - 1, b)
                probs_out(PAIRS - 1, b)
                S.wait_full(ve_, "u", b)
                ch(nc.vector.tensor_copy(u[:, 0, :], ps[:, bank("u"), 0:HW]))
                nc.vector.tensor_copy(u[0:M, 1, :], ps[0:M, bank("u"), HW:2 * HW]).then_inc(S.free("u"), 1)
                ch.link(nc.vector.reciprocal(small[:, 5, :], small[:, 4, :]))
                S.wait_full(ve_, "uT", b)
                uT = ps[:, bank("uT"), 0:H].rearrange("p (k e d) -> p k e d", e=2, d=D)
                at = c.V[:, bass.ds(b, 1), :, :].rearrange("p b k d -> p (b k) d")
                ch(nc.vector.tensor_tensor(at[0:M], uT[0:M, :, 0, :], small[0:M, 5, :].unsqueeze(2).to_broadcast([M, PAIRS, D]), ALU.mult))
                nc.vector.tensor_tensor(at[M:P], uT[M:P, :, 1, :], small[M:P, 5, :].unsqueeze(2).to_broadcast([M, PAIRS, D]),
                                        ALU.mult).then_inc(S.free("uT"), 1)
                if with_text:
                    embed(b + 1)
                for g in range(2):
                    S.wait_full(ve_, f"x{g}", b)
                    x = ps[:, bank(f"x{g}"), 0:3 * HW].rearrange("p (k w) -> p k w", w=HW)
                    for half in range(2):
                        r0 = M * half
                        at = c.E[r0:r0 + M, bass.ds(b, 1), 3 * g:3 * g + 3, :].rearrange("p b k w -> p (b k) w")
                        ins = nc.vector.tensor_copy(at, x[r0:r0 + M, :, r0:r0 + M])
                        ins.then_inc(S.free(f"x{g}"), 1) if half else ch(ins)
                S.wait_free(ve_, "xT1", b)
                ch(nc.vector.tensor_reduce(c.cols[:, bass.ds(b, 1), :].rearrange("p b k -> p (b k)"), x2T[:], AX.X, ALU.add))

            def probs_out(p, b):
                S.wait_full(ve_, f"p3T_{p}", b)
                nc.vector.tensor_copy(p3T[:, 0:TT, p, :], ps[:, bank(f"p3T_{p}"), :].rearrange("p (k m) -> p k m", m=HW)
                                      ).then_inc(S.free(f"p3T_{p}"), 1)
            ve_.wait_ge(cleared, 3)
            angles(0)
            fractions(0)
            embed(0)
            with ve_.Fori(0, B - 1) as b:
                ch.enter(b, LM_DVE)
                turn(b, True)
                ch.leave(B - 1, "landmarks dve")
            turn(B - 1, False)


STREAMS = 4
PI_GP = 5 * STREAMS
PI_V = ITERS + 1


def pseudo_inverse(nc, c, sb, sem):
    peak = sb("peak", [P, 2])
    peak_all = sb("peak_all", [P, 2])
    inv_c = sb("inv_c", [P, 2])
    start = sb("start", [P, STREAMS, 3, EV])
    ev = sb("ev", [P, STREAMS, 3, EV])
    q = sb("q", [P, STREAMS, 3, EV])
    r = sb("r", [P, STREAMS, 3, EV])
    w = sb("w", [P, STREAMS, 3, D])
    x2 = sb("x2_in", [P, STREAMS, 3, HW])
    streams = range(STREAMS)
    peaks, peaked, scaled, prep = sem("pi_peaks"), sem("pi_peaked"), sem("pi_scaled"), sem("pi_prep")
    cleared = sem("pi_cleared")
    p1, p2, q_in, r_in, e_in, v_in = ([sem(f"pi_{n}_{s}") for s in streams] for n in ("p1", "p2", "q_in", "r_in", "e_in", "v_in"))
    a = [c.psum[:, 2 * s, 0:3 * EV].rearrange("p (k w) -> p k w", k=3) for s in streams]
    bb = [c.psum[:, 2 * s + 1, 0:3 * EV].rearrange("p (k w) -> p k w", k=3) for s in streams]
    turns = B // 2

    x2_in = sem("pi_x2_in")

    with nc.Block() as block:
        @block.sync
        def _(sp):
            give(sp, [*p1, *r_in, *v_in], [])
            with sp.Fori(0, turns) as i:
                for s in streams:
                    sp.wait_ge(p1[s], ONE + i * PI_V)
                    g = s % 2
                    src = c.x_dram[bass.ds(i * 2 + s // 2, 1), :, 3 * g:3 * g + 3, :].rearrange("b p k m -> (b p) k m")
                    sp.dma_start(x2[:, s], src).then_inc(x2_in, 16)

        @block.gpsimd
        def _(gp):
            ch = Chain(gp, prep)
            nc.gpsimd.memset(start[:], 0.0).then_inc(cleared, 1)
            nc.gpsimd.memset(ev[:], 0.0).then_inc(cleared, 1)
            gp.wait_ge(peaks, 2)
            nc.gpsimd.partition_all_reduce(peak_all[:], peak[:], channels=P, reduce_op=RMAX).then_inc(peaked, 1)
            gp.wait_ge(scaled, 2)
            gp.wait_ge(cleared, 2)

            with gp.Fori(0, turns) as i:
                ch.enter(i, PI_GP)
                for s in streams:
                    gp.wait_ge(r_in[s], ONE + i * ITERS)
                    g = s % 2
                    bx = bass.ds(i * 2 + s // 2, 1)
                    for half in range(2):
                        r0 = M * half
                        src = c.E[r0:r0 + M, bx, 3 * g:3 * g + 3, :].rearrange("p b k m -> p (b k) m")
                        ch.link(nc.gpsimd.tensor_tensor(start[r0:r0 + M, s, :, r0:r0 + M], src,
                                                        inv_c[r0:r0 + M, 1:2].unsqueeze(2).to_broadcast([M, 3, M]), ALU.mult))
                    src = c.V[:, bx, 3 * g:3 * g + 3, :].rearrange("p b k d -> p (b k) d")
                    ch.link(nc.gpsimd.tensor_copy(start[:, s, :, HW:EV], src))
                    for half in range(2):
                        r0 = M * half
                        at = start[r0:r0 + M, s, :, r0:r0 + M]
                        one = c.ident[r0:r0 + M, r0:r0 + M].unsqueeze(1).to_broadcast([M, 3, M])
                        ch.link(nc.gpsimd.tensor_tensor(at, at, one, ALU.add))
                ch.leave(turns, "pseudo-inverse pool")

        @block.tensor
        def _(te):
            te.wait_ge(cleared, 2)

            def turn(i):
                for k in range(ITERS):
                    for s in streams:
                        if k == 0:
                            te.wait_ge(prep, i * PI_GP + 5 * (s + 1))
                        te.wait_ge(v_in[s], ONE + i * PI_V + k)
                        x = start if k == 0 else ev
                        for p in range(3):
                            last = nc.tensor.matmul(a[s][:, p, :], x[:, s, p, 0:HW], x[:, s, p, :], start=True, stop=True)
                        last.then_inc(p1[s], 1)
                    for s in streams:
                        te.wait_ge(r_in[s], ONE + i * ITERS + (k + 1))
                        lo = 0 if k < ITERS - 1 else HW
                        for p in range(3):
                            last = nc.tensor.matmul(bb[s][:, p, lo:EV], q[:, s, p, 0:HW], r[:, s, p, lo:EV], start=True, stop=True)
                        last.then_inc(p2[s], 1)
                te.wait_ge(x2_in, i * (16 * STREAMS) + 16 * STREAMS)
                for s in streams:
                    te.wait_ge(v_in[s], ONE + i * PI_V + ITERS)
                    for p in range(3):
                        last = nc.tensor.matmul(a[s][:, p, HW:EV], x2[:, s, p, :], ev[:, s, p, HW:EV], start=True, stop=True)
                    last.then_inc(p1[s], 1)
            with te.Fori(0, turns) as i:
                turn(i)

        @block.scalar
        def _(sc):
            def turn(i):
                for k in range(ITERS):
                    for s in streams:
                        sc.wait_ge(p1[s], ONE + i * PI_V + (k + 1))
                        nc.scalar.activation(q[:, s], a[s], ACT.Copy).then_inc(q_in[s], 1)
                    if k < ITERS - 1:
                        for s in streams:
                            sc.wait_ge(p2[s], i * ITERS + (k + 1))
                            nc.scalar.activation(ev[:, s, :, 0:HW], bb[s][:, :, 0:HW], ACT.Copy, scale=0.25).then_inc(e_in[s], 1)
            with sc.Fori(0, turns) as i:
                turn(i)

        @block.vector
        def _(ve):
            nc.vector.tensor_reduce(peak[:, 0:1], c.rows[:].rearrange("p b k -> p (b k)"), AX.X, ALU.max).then_inc(peaks, 1)
            nc.vector.tensor_reduce(peak[:, 1:2], c.cols[:].rearrange("p b k -> p (b k)"), AX.X, ALU.max).then_inc(peaks, 1)
            ve.wait_ge(peaked, 1)
            nc.vector.tensor_tensor(peak[:, 0:1], peak_all[:, 0:1], peak_all[:, 1:2], ALU.mult).then_inc(peaks, 1)
            ve.wait_ge(peaks, 3)
            nc.vector.reciprocal(inv_c[:, 0:1], peak[:, 0:1]).then_inc(scaled, 1)
            ve.wait_ge(scaled, 1)
            nc.vector.tensor_scalar(inv_c[:, 1:2], inv_c[:, 0:1], -1.0, None, ALU.mult).then_inc(scaled, 1)

            def turn(i):
                for k in range(ITERS):
                    x = start if k == 0 else ev
                    for s in streams:
                        ve.wait_ge(q_in[s], i * ITERS + (k + 1))
                        ve.wait_ge(v_in[s], ONE + i * PI_V + k)
                        nc.vector.tensor_tensor(w[:, s], x[:, s, :, HW:EV], q[:, s, :, HW:EV], ALU.add)
                        nc.vector.scalar_tensor_tensor(r[:, s, :, HW:EV], x[:, s, :, HW:EV], 4.0, q[:, s, :, HW:EV], ALU.mult, ALU.add)
                        nc.vector.scalar_tensor_tensor(r[:, s, :, 0:HW], x[:, s, :, 0:HW], 3.0, q[:, s, :, 0:HW], ALU.mult, ALU.add
                                                       ).then_inc(r_in[s], 1)
                    for s in streams:
                        ve.wait_ge(p2[s], i * ITERS + (k + 1))
                        if k < ITERS - 1:
                            ve.wait_ge(e_in[s], i * (ITERS - 1) + (k + 1))
                        dst = ev[:, s, :, HW:EV]
                        ve.wait_ge(r_in[s], ONE + i * ITERS + (k + 1))
                        nc.vector.scalar_tensor_tensor(dst, bb[s][:, :, HW:EV], 0.25, w[:, s], ALU.mult, ALU.add).then_inc(v_in[s], 1)
                for s in streams:
                    g = s % 2
                    dst = c.V[:, bass.ds(i * 2 + s // 2, 1), 3 * g:3 * g + 3, :].rearrange("p b k d -> p (b k) d")
                    ve.wait_ge(p1[s], ONE + i * PI_V + PI_V)
                    nc.vector.tensor_scalar(dst, a[s][:, :, HW:EV], inv_c[:, 0:1], None, ALU.mult).then_inc(v_in[s], 1)
            with ve.Fori(0, turns) as i:
                turn(i)


AT_FRONT = [(f"scores{k}", f"S{k % 2}") if q == 0 else (f"probs{k}", "T") for k in range(TT + 1) for q in range(2)]
AT_FRONT += [("outA", "T"), ("outB", "T")]
AT_TAIL = [("out_img", "R0"), ("proj0", "R1"), ("proj1", "R0"), ("proj2", "R1")]
AT_TAIL += [(f"xnT{k}", f"R{k % 2}") for k in range(TT + 1)]
AT_TAIL += [("lgT", "R0"), ("lgT_img", "R1"), ("rt", "R0"), ("rt_img", "R1"), ("xs", "R0"), ("eCT", "R1"), ("xsT", "R0")]
AT_DVE, AT_GP = 40, 4
TILES = TT + 1


def attention(nc, c, sb, sem):
    qb = sb("qb", [P, 2, N])
    kl = sb("kl", [P, 12, M])
    zb = sb("zb", [P, PAIRS, 2 * D])
    e1 = sb("e1", [P, 2, NH * M])
    p1T = sb("p1T", [P, PAIRS, N])
    neg = sb("neg", [P, 2, NH])
    rden = sb("rden", [P, S])
    rden_img = sb("rden_img", [P, 2 * NI])
    oA = sb("oA", [P, N])
    oB = sb("oB", [M + 1, N])
    stats, mv = sb("stats", [P, TILES, 6]), sb("mv", [P, TILES, 2])
    v192, t1, rn = sb("v192", [P, TILES]), sb("t1", [P, TILES]), sb("rn", [P, TILES])
    hw = sb("hw", [P, TILES, H])
    xn = sb("xn", [P, TILES, H])
    xnT = sb("xnT", [K2, 2, N])
    rT = sb("rT", [P, N])
    rt = sb("rt", [P, TILES, 2 * NE])
    dstat = sb("dstat", [P, 4])
    eC = sb("eC", [P, TILES, NE])
    negC = sb("negC", [P, TILES])
    sumC = sb("sumC", [P, TILES])
    xs = sb("xs", [P, H])
    CT = sb("CT", [NE, N])
    F_ = Slots(sem, "at", AT_FRONT)
    R_ = Slots(sem, "at", AT_TAIL)
    banks = {"S0": 0, "S1": 2, "T": 4, "R0": 6, "R1": 7}
    ps = c.psum

    def two(product):
        b0 = banks[F_.at[product][0]]
        return ps[:, b0:b0 + 2, :].rearrange("p k n -> p (k n)")

    def one(product):
        return ps[:, banks[R_.at[product][0]], :]

    q_in, kl_in, zb_in, cleared = sem("at_q_in"), sem("at_kl_in"), sem("at_zb_in"), sem("at_cleared")
    shifted, exp_in, o_in = sem("at_shifted"), sem("at_exp_in"), sem("at_o_in")
    h_in = sem("at_h_in")
    normed, xn_in = sem("at_normed"), sem("at_xn_in")
    d_shift, eD_in, c_shift, eC_in, d_scale = (sem("at_" + n) for n in ("d_shift", "eD_in", "c_shift", "eC_in", "d_scale"))
    dve_done, gp_done, c_stored = sem("at_dve"), sem("at_gp"), sem("at_c_stored")

    chunks = [(0, NI)] + [(NI + P * k, P) for k in range(TT)]
    tiles = [(P, NI + P * k) for k in range(TT)] + [(NI, 0)]

    with nc.Block() as block:
        @block.sync
        def _(sp):
            give(sp, [shifted, h_in], [c_stored], F_, R_)
            def load(b):
                sp.wait_ge(F_.full("outA"), ONE + b * F_.uses["T"])
                sp.dma_start(qb[:], c.q_dram[bass.ds(b, 1)].rearrange("b p k n -> (b p) k n")).then_inc(q_in, 16)

            def store(b):
                R_.wait_free(sp, "eCT", b)
                R_.wait_free(sp, "xsT", b)
                sp.dma_start(c.c_dram[bass.ds(b, 1)].rearrange("b n t -> (b n) t"), CT[:]).then_inc(c_stored, 16)
            load(0)
            load(1)
            with sp.Fori(0, B - 2) as b:
                store(b)
                load(b + 2)
            store(B - 2)
            store(B - 1)
            sp.wait_ge(c_stored, DMA + 16 * B)

        @block.gpsimd
        def _(gp):
            ch = Chain(gp, gp_done)
            for k, (tile, value) in enumerate(((zb[:], 0.0), (mv[:], 0.0), (e1[:], 0.0), (hw[:, TT, :], 0.0), (xs[:], 0.0), (oB[M:M + 1, :], 1.0), (c.xsT[:], 0.0),
                                               (c.xsT[K2:K2 + 1, 0:1], 1.0), (c.rsum[:], 1.0))):
                nc.gpsimd.memset(tile, value).then_inc(cleared, 1)
                gp.wait_ge(cleared, k + 1)

            def front(b):
                gp.wait_ge(F_.full("outB"), ONE + b * F_.uses["T"])
                ch.link(nc.gpsimd.tensor_tensor(kl[:, 0:8, :], c.mask, c.landk[:, bass.ds(b, 1), 1, :].to_broadcast([P, 8, M]), ALU.mult))
                nc.gpsimd.tensor_tensor(kl[:, 8:12, :], c.mask[:, 0:4, :], c.landk[:, bass.ds(b, 1), 0, :].to_broadcast([P, 4, M]), ALU.mult
                                        ).then_inc(kl_in, 1)
                gp.wait_ge(kl_in, b + 1)
                for half in range(2):
                    r0 = M * half
                    src = c.V[r0:r0 + M, bass.ds(b, 1), :, :].rearrange("p b k d -> p (b k) d")
                    ins = nc.gpsimd.tensor_copy(zb[r0:r0 + M, :, D * half:D * half + D], src)
                    if half:
                        ins.then_inc(zb_in, 1)
                        gp.wait_ge(zb_in, b + 1)
                    else:
                        ch.link(ins)

            def tail(b):
                gp.wait_ge(normed, b + 1)
                ch.link(nc.gpsimd.tensor_tensor(xn[:], hw[:], mv[:, :, 0:1].to_broadcast([P, TILES, H]), ALU.subtract))
                nc.gpsimd.tensor_tensor(xn[:], xn[:], rn[:].unsqueeze(2).to_broadcast([P, TILES, H]), ALU.mult).then_inc(xn_in, 1)
                gp.wait_ge(xn_in, b + 1)
                ch.link(nc.gpsimd.tensor_copy(c.h[:, bass.ds(b * TT, TT), :], hw[:, 0:TT, :]))
                nc.gpsimd.tensor_copy(c.h_img[:, bass.ds(b, 1), :], hw[0:NI, TT:TILES, :]).then_inc(h_in, 1)
                gp.wait_ge(h_in, ONE + b + 1)

            front(0)
            with gp.Fori(0, B - 1) as b:
                ch.enter(b, AT_GP)
                front(b + 1)
                tail(b)
                ch.leave(B - 1, "attention pool")
            tail(B - 1)

        @block.tensor
        def _(te):
            te.wait_ge(cleared, 9)

            def scores(k, b):
                c0, n = chunks[k]
                if k == 0:
                    te.wait_ge(q_in, b * 16 + 16)
                    te.wait_ge(kl_in, b + 1)
                te.wait_ge(shifted, ONE + b * TILES + max(k - 1, 0))
                out = two(f"scores{k}")
                klf = kl[:].rearrange("p h m -> p (h m)")
                nc.tensor.matmul(out[0:n, 0:512], qb[:, 0, c0:c0 + n], klf[:, 0:512], start=True, stop=True)
                nc.tensor.matmul(out[0:n, 512:768], qb[:, 1, c0:c0 + n], klf[:, 512:768], start=True, stop=True
                                 ).then_inc(F_.full(f"scores{k}"), 1)

            def probs(k, b):
                c0, n = chunks[k]
                te.wait_ge(exp_in, b * TILES + (k + 1))
                F_.claim(te, f"probs{k}", b)
                out = two(f"probs{k}")
                for p in range(PAIRS):
                    last = nc.tensor.transpose(out[:, P * p:P * p + P], e1[:, k % 2, HW * p:HW * p + HW], c.ident)
                last.then_inc(F_.full(f"probs{k}"), 1)

            def out(b):
                te.wait_ge(zb_in, b + 1)
                F_.wait_free(te, f"probs{TT}", b)
                R_.claim(te, "out_img", b)
                for p in range(PAIRS):
                    j = p % 4
                    for q in range(2):
                        c0 = 2 * NI * (p // 4) + NI * q
                        last = nc.tensor.matmul(one("out_img")[32 * j:32 * j + 32, c0:c0 + NI], c.ones_bd if q else zb[:, p, :],
                                                p1T[:, p, 0:NI], start=True, stop=True)
                last.then_inc(R_.full("out_img"), 1)
                for g, product in enumerate(("outA", "outB")):
                    F_.claim(te, product, b)
                    for q in range(2):
                        for p in range(4 * g, min(4 * g + 4, PAIRS)):
                            j = p % 4
                            lhsT = c.ones_bd if q else zb[:, p, :]
                            last = nc.tensor.matmul(two(product)[32 * j:32 * j + 32, 512 * q:512 * q + S], lhsT,
                                                    p1T[:, p, NI:N], start=True, stop=True)
                    last.then_inc(F_.full(product), 1)

            def tail0(b):
                te.wait_ge(o_in, b + 1)
                for k in (4, 0, 1, 2, 3):
                    n, c0 = tiles[k]
                    product = "proj0" if k == 4 else f"proj{1 + k // 2}"
                    lo = H * (k % 2) if k < 4 else 0
                    if k in (4, 0, 2):
                        R_.claim(te, product, b)
                    nc.tensor.matmul(one(product)[0:n, lo:lo + H], oA[:, c0:c0 + n], c.wprojT[:, 0, :], start=True, stop=False)
                    last = nc.tensor.matmul(one(product)[0:n, lo:lo + H], oB[:, c0:c0 + n], c.wprojT[0:M + 1, 1, :],
                                            start=False, stop=True)
                    if k in (4, 1, 3):
                        last.then_inc(R_.full(product), 1)

            def tail1(b):
                te.wait_ge(xn_in, b + 1)
                for k, (n, c0) in enumerate(tiles):
                    R_.claim(te, f"xnT{k}", b)
                    for e in range(2):
                        last = nc.tensor.transpose(one(f"xnT{k}")[0:K2, P * e:P * e + P], xn[:, k, K2 * e:K2 * e + K2], c.ident)
                    last.then_inc(R_.full(f"xnT{k}"), 1)

            def tail2(b):
                R_.wait_free(te, "xnT3", b)
                R_.wait_free(te, "xnT4", b)
                for product, c0, n in (("lgT", NI, S), ("lgT_img", 0, NI)):
                    R_.claim(te, product, b)
                    for e in range(2):
                        last = nc.tensor.matmul(one(product)[:, 0:n], c.phin[:, e, :], xnT[:, e, c0:c0 + n], start=(e == 0), stop=(e == 1))
                    last.then_inc(R_.full(product), 1)

            def tail3(b):
                te.wait_ge(eD_in, b + 1)
                R_.claim(te, "rt", b)
                R_.claim(te, "rt_img", b)
                for k in range(TT):
                    last = nc.tensor.transpose(one("rt")[:, P * k:P * k + P], rT[:, NI + P * k:NI + P * k + P], c.ident)
                last.then_inc(R_.full("rt"), 1)
                nc.tensor.transpose(one("rt_img")[0:NI, 0:P], rT[:, 0:NI], c.ident).then_inc(R_.full("rt_img"), 1)

            def tail4(b):
                te.wait_ge(eC_in, b + 1)
                R_.wait_free(te, "rt", b)
                R_.wait_free(te, "rt_img", b)
                R_.claim(te, "xs", b)
                R_.claim(te, "eCT", b)
                for k, (n, c0) in enumerate(tiles):
                    last = nc.tensor.matmul(one("xs")[NE:P, 0:H], rt[0:n, k, NE:P], xn[0:n, k, :], start=(k == 0), stop=(k == TT))
                last.then_inc(R_.full("xs"), 1)
                for k in range(TT):
                    last = nc.tensor.transpose(one("eCT")[0:NE, P * k:P * k + P], eC[:, k, :], c.ident)
                last.then_inc(R_.full("eCT"), 1)

            def tail5(b):
                R_.wait_free(te, "xs", b)
                R_.claim(te, "xsT", b)
                for e in range(2):
                    nc.tensor.transpose(one("xsT")[0:K2, P * e:P * e + P], xs[:, e:H:2], c.ident)
                nc.tensor.transpose(one("xsT")[0:NE, 2 * P:2 * P + NI], eC[0:NI, TT, :], c.ident[0:NI, 0:NI]).then_inc(R_.full("xsT"), 1)

            def turn(b, front, tail):
                if front:
                    scores(0, b + 1)
                    scores(1, b + 1)
                if tail:
                    tail0(b)
                for k in range(TILES):
                    if front:
                        probs(k, b + 1)
                        if k + 2 < TILES:
                            scores(k + 2, b + 1)
                    if tail:
                        (tail1, tail2, tail3, tail4, tail5)[k](b)
                if front:
                    out(b + 1)
            turn(-1, True, False)
            with te.Fori(0, B - 1) as b:
                turn(b, True, True)
            turn(B - 1, False, True)

        @block.scalar
        def _(sc):
            def copy(dst, src, scale=1.0):
                return nc.scalar.activation(dst, src, ACT.Copy, scale=scale)

            def front(k, b):
                c0, n = chunks[k]
                sc.wait_ge(shifted, ONE + b * TILES + (k + 1))
                nc.scalar.activation(e1[0:n, k % 2, :], e1[0:n, k % 2, :], ACT.Exp).then_inc(exp_in, 1)
                F_.wait_full(sc, f"probs{k}", b)
                src = two(f"probs{k}").rearrange("p (k n) -> p k n", n=P)
                copy(p1T[:, 0:4, c0:c0 + n], src[:, 0:4, 0:n])
                copy(p1T[:, 4:6, c0:c0 + n], src[:, 4:6, 0:n]).then_inc(F_.free(f"probs{k}"), 1)

            def tail1(b):
                for k, (n, c0) in enumerate(tiles):
                    R_.wait_full(sc, f"xnT{k}", b)
                    ins = copy(xnT[:, :, c0:c0 + n], one(f"xnT{k}")[0:K2, 0:2 * P].rearrange("p (e n) -> p e n", e=2)[:, :, 0:n])
                    ins.then_inc(R_.free(f"xnT{k}"), 1)

            def tail2(b):
                for product, c0, n in (("lgT", NI, S), ("lgT_img", 0, NI)):
                    R_.wait_full(sc, product, b)
                    copy(rT[:, c0:c0 + n], one(product)[:, 0:n]).then_inc(R_.free(product), 1)

            def tail3(b):
                sc.wait_ge(d_shift, b + 1)
                nc.scalar.activation(rT[NE:P], rT[NE:P], ACT.Exp, bias=dstat[NE:P, 0:1], accum_out=dstat[NE:P, 1:2]).then_inc(eD_in, 1)
                R_.wait_full(sc, "rt", b)
                copy(rt[:, 0:TT, :], one("rt").rearrange("p (k n) -> p k n", n=P)).then_inc(R_.free("rt"), 1)
                R_.wait_full(sc, "rt_img", b)
                copy(rt[0:NI, TT, :], one("rt_img")[0:NI, 0:P]).then_inc(R_.free("rt_img"), 1)
                sc.wait_ge(c_shift, b + 1)
                nc.scalar.activation(eC[:, 0:TT, :], eC[:, 0:TT, :], ACT.Exp)
                nc.scalar.activation(eC[0:NI, TT, :], eC[0:NI, TT, :], ACT.Exp).then_inc(eC_in, 1)

            def tail4(b):
                R_.wait_full(sc, "xs", b)
                sc.wait_ge(d_scale, b + 1)
                copy(xs[NE:P], one("xs")[NE:P, 0:H], dstat[NE:P, 2:3]).then_inc(R_.free("xs"), 1)
                R_.wait_full(sc, "eCT", b)
                sc.wait_ge(c_stored, DMA + b * 16)
                copy(CT[:, NI:N], one("eCT")[0:NE, 0:S]).then_inc(R_.free("eCT"), 1)

            def turn(b, front_, tail):
                for k in range(TILES):
                    if front_:
                        front(k, b + 1)
                    if tail and k < 4:
                        (tail1, tail2, tail3, tail4)[k](b)
            turn(-1, True, False)
            with sc.Fori(0, B - 1) as b:
                turn(b, True, True)
            turn(B - 1, False, True)

        @block.vector
        def _(ve):
            ch = Chain(ve, dve_done)
            ve.wait_ge(cleared, 9)

            def front(k, b):
                c0, n = chunks[k]
                F_.wait_full(ve, f"scores{k}", b)
                src = two(f"scores{k}")[0:n, 0:NH * M].rearrange("p (h m) -> p h m", m=M)
                ch.link(nc.vector.tensor_reduce(neg[0:n, k % 2, :], src, AX.X, ALU.max, negate=True))
                if k >= 2:
                    F_.wait_full(ve, f"probs{k - 2}", b)
                nc.vector.tensor_tensor(e1[0:n, k % 2, :].rearrange("p (h m) -> p h m", m=M), src,
                                        neg[0:n, k % 2, :].unsqueeze(2).to_broadcast([n, NH, M]), ALU.add).then_inc(shifted, 1)
                ve.wait_ge(shifted, ONE + b * TILES + (k + 1))

            def out(b):
                for g, (product, o, n) in enumerate((("outA", oA, P), ("outB", oB, M))):
                    F_.wait_full(ve, product, b)
                    ch.link(nc.vector.reciprocal(rden[0:n, :], two(product)[0:n, 512:512 + S]))
                    nc.vector.tensor_tensor(o[0:n, NI:N], two(product)[0:n, 0:S], rden[0:n, :], ALU.mult).then_inc(F_.free(product), 1)
                R_.wait_full(ve, "out_img", b)
                for g, (o, n) in enumerate(((oA, P), (oB, M))):
                    src = one("out_img")[0:n, 2 * NI * g:2 * NI * g + 2 * NI]
                    ch.link(nc.vector.reciprocal(rden_img[0:n, NI * g:NI * g + NI], src[:, NI:2 * NI]))
                    ins = nc.vector.tensor_tensor(o[0:n, 0:NI], src[:, 0:NI], rden_img[0:n, NI * g:NI * g + NI], ALU.mult)
                    ins.then_inc(R_.free("out_img"), 1) if g else ch(ins)
                R_.wait_free(ve, "out_img", b)
                F_.wait_free(ve, "outB", b)
                nc.vector.tensor_copy(rden_img[0:1, 0:1], rden_img[0:1, 1:2]).then_inc(o_in, 1)

            def tail0(b):
                R_.wait_full(ve, "proj0", b)
                h = c.h_img[:, bass.ds(b, 1), :].rearrange("p a h -> p (a h)")
                ve.wait_ge(h_in, ONE + b)
                nc.vector.tensor_tensor(hw[0:NI, TT, :], one("proj0")[0:NI, 0:H], h, ALU.add).then_inc(R_.free("proj0"), 1)
                for j in range(2):
                    R_.wait_full(ve, f"proj{1 + j}", b)
                    h = c.h[:, bass.ds(b * TT + 2 * j, 2), :]
                    nc.vector.tensor_tensor(hw[:, 2 * j:2 * j + 2, :], one(f"proj{1 + j}")[:, 0:2 * H].rearrange("p (a h) -> p a h", h=H), h, ALU.add
                                            ).then_inc(R_.free(f"proj{1 + j}"), 1)
                for j in range(3):
                    R_.wait_free(ve, f"proj{j}", b)
                for k in range(TT):
                    ch(nc.vector.bn_stats(stats[:, k, :], hw[:, k, :]))
                ch(nc.vector.bn_stats(stats[0:NI, TT, :], hw[0:NI, TT, :]))
                ch.wait()
                nc.vector.tensor_copy(t1[:, 0:1], stats[:, 0, 0:1])
                for k in range(TILES):
                    n = tiles[k][0]
                    ch(nc.vector.bn_aggr(mv[0:n, k, :], stats[0:n, k, :]))
                ch.wait()
                ch.link(nc.vector.tensor_scalar(t1[:], mv[:, :, 1], 1e-24, 1e-29, ALU.mult, ALU.add))
                ch.link(nc.vector.scalar_tensor_tensor(v192[:], mv[:, :, 1], float(H), t1[:], ALU.mult, ALU.max))
                rsqrt(nc, ch, rn[:], t1[:], v192[:])
                nc.vector.tensor_copy(t1[:, 0:1], rn[:, 0:1]).then_inc(normed, 1)

            def tail2(b):
                R_.wait_free(ve, "lgT", b)
                R_.wait_free(ve, "lgT_img", b)
                nc.vector.tensor_reduce(dstat[:, 0:1], rT[:], AX.X, ALU.max, negate=True).then_inc(d_shift, 1)

            def tail3(b):
                R_.wait_free(ve, "rt", b)
                R_.wait_free(ve, "rt_img", b)
                ch(nc.vector.tensor_reduce(negC[:, 0:TT], rt[:, 0:TT, 0:NE], AX.X, ALU.max, negate=True))
                ch.link(nc.vector.tensor_reduce(negC[0:NI, TT:TILES], rt[0:NI, TT:TILES, 0:NE], AX.X, ALU.max, negate=True))
                nc.vector.tensor_tensor(eC[:, 0:TT, :], rt[:, 0:TT, 0:NE], negC[:, 0:TT].unsqueeze(2).to_broadcast([P, TT, NE]), ALU.add)
                nc.vector.tensor_tensor(eC[0:NI, TT:TILES, :], rt[0:NI, TT:TILES, 0:NE],
                                        negC[0:NI, TT:TILES].unsqueeze(2).to_broadcast([NI, 1, NE]), ALU.add).then_inc(c_shift, 1)

            def tail4(b):
                ve.wait_ge(eD_in, b + 1)
                nc.vector.reciprocal(dstat[NE:P, 2:3], dstat[NE:P, 1:2]).then_inc(d_scale, 1)
                ve.wait_ge(eC_in, b + 1)
                ch(nc.vector.tensor_reduce(sumC[:, 0:TT], eC[:, 0:TT, :], AX.X, ALU.add))
                ch.link(nc.vector.tensor_reduce(sumC[0:NI, TT:TILES], eC[0:NI, TT:TILES, :], AX.X, ALU.add))
                at = c.rsum[:, bass.ds(b, 1), :].rearrange("p b k -> p (b k)")
                ch(nc.vector.reciprocal(at[:, 0:TT], sumC[:, 0:TT]))
                ch(nc.vector.reciprocal(at[0:NI, TT:TILES], sumC[0:NI, TT:TILES]))

            def tail5(b):
                R_.wait_full(ve, "xsT", b)
                ve.wait_ge(c_stored, DMA + b * 16)
                ch(nc.vector.tensor_copy(CT[:, 0:NI], one("xsT")[0:NE, 2 * P:2 * P + NI]))
                src = one("xsT")[0:K2, 0:2 * P].rearrange("p (e n) -> p e n", e=2)[:, :, NE:P]
                nc.vector.tensor_copy(c.xsT[0:K2, :, :, bass.ds(b, 1)].rearrange("p e n b -> p e (n b)"), src).then_inc(R_.free("xsT"), 1)

            def turn(b, front_, tail):
                if front_:
                    front(0, b + 1)
                    front(1, b + 1)
                if tail:
                    tail0(b)
                for k in range(2, TILES):
                    if front_:
                        front(k, b + 1)
                    if tail:
                        (tail2, tail3, tail4)[k - 2](b)
                if tail:
                    tail5(b)
                if front_:
                    out(b + 1)
            turn(-1, True, False)
            with ve.Fori(0, B - 1) as b:
                ch.enter(b, AT_DVE)
                turn(b, True, True)
                ch.leave(B - 1, "attention dve")
            turn(B - 1, False, True)


G = 4
GROUPS = NE // G
R32 = 2 * B


def experts(nc, c, t, sb, sem):
    w1 = sb("w1", [K2 + 1, 2, G, 2, F])
    w2 = sb("w2", [P, 2, G, FC, H])
    xg = sb("xg", [K2 + 1, 2, 2, G, R32])
    hs = sb("hs", [P, 2, F])
    hT = sb("hT", [P, 2, FC, P])
    ys = sb("ys", [P, 2, H])
    names = ("w1_in", "w2_in", "xg_in", "first", "gelu", "turned", "turned_in", "second", "ys_in", "ys_out")
    w1_in, w2_in, xg_in, first, gelu, turned, turned_in, second, ys_in, ys_out = ([sem(f"ex_{n}_{u}") for u in range(2)] for n in names)
    ps = c.psum
    hid = [ps[:, 2 * u:2 * u + 2, :].rearrange("p k n -> p (k n)") for u in range(2)]
    flip = ps[:, 4:6, :].rearrange("p k n -> p (k n)")
    turns = GROUPS // 2

    with nc.Block() as block:
        @block.sync
        def _(sp):
            give(sp, [*first, *second, *gelu, *turned_in, *ys_in], [*ys_out])
            def load(i, u):
                e0 = i * (2 * G) + G * u
                sp.wait_ge(first[u], ONE + i)
                sp.dma_start(w1[0:K2, u], t["L0_ffn_w1"][bass.ds(e0, G)].rearrange("n (p t) h -> p n t h", t=2)).then_inc(w1_in[u], 16)
                sp.dma_start(w1[K2:K2 + 1, u, :, 0, :], t["L0_ffn_b1"][bass.ds(e0, G)].rearrange("(a n) h -> a n h", a=1)
                             ).then_inc(w1_in[u], 16)
                sp.wait_ge(second[u], ONE + i)
                sp.dma_start(w2[:, u], t["L0_ffn_w2"][bass.ds(e0, G)].rearrange("n (p c) d -> p n c d", c=FC)).then_inc(w2_in[u], 16)

            def store(i, u):
                sp.wait_ge(ys_in[u], ONE + i + 1)
                for j in range(G):
                    sp.dma_start(c.y_dram[bass.ds(i * (2 * G) + (G * u + j), 1)].rearrange("n b d -> (n b) d"),
                                 ys[R32 * j:R32 * j + B, u, :]).then_inc(ys_out[u], 16)
            load(0, 0)
            load(0, 1)
            with sp.Fori(0, turns - 1) as i:
                for u in range(2):
                    load(i + 1, u)
                    store(i, u)
            for u in range(2):
                store(turns - 1, u)
            for u in range(2):
                sp.wait_ge(ys_out[u], DMA + 16 * G * turns)

        @block.gpsimd
        def _(gp):
            with gp.Fori(0, turns) as i:
                for u in range(2):
                    gp.wait_ge(first[u], ONE + i)
                    nc.gpsimd.tensor_copy(xg[:, u], c.xsT[:, :, bass.ds(i * (2 * G) + G * u, G), :]).then_inc(xg_in[u], 1)
                    gp.wait_ge(xg_in[u], i + 1)

        @block.tensor
        def _(te):
            def layer1(i, u):
                te.wait_ge(w1_in[u], i * 32 + 32)
                te.wait_ge(xg_in[u], i + 1)
                te.wait_ge(gelu[u], ONE + i)
                for c0, n in ((0, 512), (512, F - 512)):
                    for k in range(2):
                        rows = K2 + 1 - k
                        for j in range(G):
                            last = nc.tensor.matmul(hid[u][R32 * j:R32 * j + R32, c0:c0 + n], xg[0:rows, u, k, j, :],
                                                    w1[0:rows, u, j, k, c0:c0 + n], start=(k == 0), stop=(k == 1))
                last.then_inc(first[u], 1)

            def layer2(i, u):
                te.wait_ge(gelu[u], ONE + i + 1)
                if u:
                    te.wait_ge(turned_in[0], ONE + i + 1)
                else:
                    te.wait_ge(turned_in[1], ONE + i)
                for f in range(FC):
                    last = nc.tensor.transpose(flip[:, P * f:P * f + P], hs[:, u, f:F:FC], c.ident)
                last.then_inc(turned[u], 1)
                te.wait_ge(turned_in[u], ONE + i + 1)
                te.wait_ge(w2_in[u], i * 16 + 16)
                te.wait_ge(ys_in[u], ONE + i)
                for f in range(FC):
                    for j in range(G):
                        last = nc.tensor.matmul(ps[R32 * j:R32 * j + R32, 6 + u, 0:H], hT[:, u, f, R32 * j:R32 * j + R32],
                                                w2[:, u, j, f, :], start=(f == 0), stop=(f == FC - 1))
                last.then_inc(second[u], 1)
            with te.Fori(0, turns) as i:
                layer1(i, 0)
                layer1(i, 1)
                layer2(i, 0)
                layer2(i, 1)

        @block.scalar
        def _(sc):
            with sc.Fori(0, turns) as i:
                for u in range(2):
                    sc.wait_ge(first[u], ONE + i + 1)
                    nc.scalar.activation(hs[:, u, :], hid[u][:, 0:F], ACT.Gelu).then_inc(gelu[u], 1)

        @block.vector
        def _(ve):
            with ve.Fori(0, turns) as i:
                for u in range(2):
                    ve.wait_ge(turned[u], i + 1)
                    nc.vector.tensor_copy(hT[:, u].rearrange("p c n -> p (c n)"), flip[:, 0:F]).then_inc(turned_in[u], 1)
                    ve.wait_ge(second[u], ONE + i + 1)
                    ve.wait_ge(ys_out[u], DMA + i * (16 * G))
                    nc.vector.tensor_copy(ys[:, u, :], ps[:, 6 + u, 0:H]).then_inc(ys_in[u], 1)


def combine(nc, c, t, sb, sem):
    Y = sb("Y", [NE, B, H])
    b2 = sb("b2", [NE, H])
    CT = sb("CT", [NE, 2, N])
    yb = sb("yb", [NE, 2, H])
    y_in, b2_in, y_ready = sem("co_y_in"), sem("co_b2_in"), sem("co_y_ready")
    c_in, yb_in = ([sem(f"co_{n}_{u}") for u in range(2)] for n in ("c_in", "yb_in"))
    full, added, stored = sem("co_full"), sem("co_added"), sem("co_stored")
    parts = ((0, 2), (2, 4), (4, 5))
    tiles = [(P, NI + P * k) for k in range(TT)] + [(NI, 0)]
    ps = c.psum

    def bank(u, j):
        return ps[:, 3 * u + j, :]
    turns = B // 2

    with nc.Block() as block:
        @block.sync
        def _(sp):
            give(sp, [full, added], [])
            sp.dma_start(Y[:], c.y_dram).then_inc(y_in, 16)
            sp.dma_start(b2[:], t["L0_ffn_b2"]).then_inc(b2_in, 16)
            with sp.Fori(0, turns) as i:
                for u in range(2):
                    sp.wait_ge(full, ONE + i * 6)
                    sp.dma_start(CT[:, u], c.c_dram[bass.ds(i * 2 + u, 1)].rearrange("b n t -> (b n) t")).then_inc(c_in[u], 16)

        @block.scalar
        def _(sc):
            sc.wait_ge(y_ready, 1)
            with sc.Fori(0, turns) as i:
                for u in range(2):
                    sc.wait_ge(full, ONE + i * 6)
                    nc.scalar.activation(yb[:, u, :], Y[:, bass.ds(i * 2 + u, 1), :].rearrange("p b h -> p (b h)"), ACT.Copy
                                         ).then_inc(yb_in[u], 1)

        @block.gpsimd
        def _(gp):
            with gp.Fori(0, B) as b:
                gp.wait_ge(added, ONE + b * 5 + 4)
                dst = t["out"][bass.ds(b, 1), NI:N, :].rearrange("b (k p) h -> p (b k) h", p=P)
                gp.dma_start(dst, c.h[:, bass.ds(b * TT, TT), :]).then_inc(stored, 16)
                gp.wait_ge(added, ONE + b * 5 + 5)
                gp.dma_start(t["out"][bass.ds(b, 1), 0:NI, :].rearrange("b p h -> (b p) h"),
                             c.h_img[:, bass.ds(b, 1), :].rearrange("p b h -> p (b h)")).then_inc(stored, 16)
            gp.wait_ge(stored, 32 * B)

        @block.tensor
        def _(te):
            with te.Fori(0, turns) as i:
                for u in range(2):
                    te.wait_ge(c_in[u], i * 16 + 16)
                    te.wait_ge(yb_in[u], i + 1)
                    for j, (k0, k1) in enumerate(parts):
                        if j == 0:
                            te.wait_ge(added, ONE + i * 10)
                        for k in range(k0, k1):
                            n, c0 = tiles[k]
                            last = nc.tensor.matmul(bank(u, j)[0:n, H * (k - k0):H * (k - k0) + H], CT[:, u, c0:c0 + n], yb[:, u, :],
                                                    start=True, stop=True)
                        last.then_inc(full, 1)

        @block.vector
        def _(ve):
            ve.wait_ge(y_in, 16)
            ve.wait_ge(b2_in, 16)
            nc.vector.tensor_tensor(Y[:], Y[:], b2[:].unsqueeze(1).to_broadcast([NE, B, H]), ALU.add).then_inc(y_ready, 1)
            with ve.Fori(0, turns) as i:
                for u in range(2):
                    b = i * 2 + u
                    for j, (k0, k1) in enumerate(parts):
                        ve.wait_ge(full, ONE + i * 6 + (3 * u + j + 1))
                        for k in range(k0, k1):
                            n = tiles[k][0]
                            h = (c.h[:, bass.ds(i * (2 * TT) + (TT * u + k), 1), :] if k < TT else c.h_img[:, bass.ds(b, 1), :]
                                 ).rearrange("p a h -> p (a h)")
                            scale = c.rsum[0:n, bass.ds(b, 1), k:k + 1].rearrange("p a k -> p (a k)")
                            nc.vector.scalar_tensor_tensor(h, bank(u, j)[0:n, H * (k - k0):H * (k - k0) + H], scale, h,
                                                           ALU.mult, ALU.add).then_inc(added, 1)


INPUTS = ["x", "x_txt", "itok_BS_0_15", "itok_BS_0_3", "itok_BS_0_9999", "itok_BS_0_2047", "fside_BS_age_tau", "fside_BS_delays_tau",
          "L0_tok_W", "L0_tok_b", "L0_txt_word_table", "L0_txt_modalities_table", "L0_txt_seg_table", "L0_txt_npi_table",
          "L0_txt_posi_table", "L0_txt_age_w", "L0_txt_age_b", "L0_txt_age_w0", "L0_txt_age_b0", "L0_txt_delay_w", "L0_txt_delay_b",
          "L0_txt_delay_w0", "L0_txt_delay_b0", "L0_txt_ln_gamma", "L0_txt_ln_beta", "L0_attn_w_qkv", "L0_attn_w_proj",
          "L0_attn_b_proj", "L0_ffn_phi", "L0_ffn_scale", "L0_ffn_w1", "L0_ffn_b1", "L0_ffn_w2", "L0_ffn_b2"]


def kernel(**inputs):
    import concourse.bacc as bacc
    from concourse.bass_utils import run_bass_kernel_spmd

    nc = bacc.Bacc("TRN2", target_bir_lowering=False, num_devices=1)
    arrays = {f"in_{name}": np.ascontiguousarray(inputs[name]) for name in INPUTS}
    arrays["in_const"] = constants()
    t = {name[3:]: nc.dram_tensor(name, a.shape, mybir.dt.from_np(a.dtype), kind="ExternalInput").ap() for name, a in arrays.items()}
    t["out"] = nc.dram_tensor("out", (B, N, H), F32, kind="ExternalOutput").ap()
    build(nc, t)
    result = run_bass_kernel_spmd(nc, [arrays], core_ids=[0])
    return result.results[0]["out"]
```

```python
from contextlib import ExitStack

import numpy as np

import concourse.bass as bass
from concourse import mybir

F32 = mybir.dt.float32
I32 = mybir.dt.int32
U32 = mybir.dt.uint32
ALU = mybir.AluOpType
ACT = mybir.ActivationFunctionType
AX = mybir.AxisListType
RMAX = bass.bass_isa.ReduceOp.max

P = 128
B, S, H = 16, 512, 192
NI = 16
N = S + NI
M = 64
PAD = (M - N % M) % M
NP = N + PAD
L = NP // M
NH, D = 12, H // 12
PAIRS = NH // 2
TT = S // P
NT = B * TT
K2 = H // 2
HW = 2 * M
EV = HW + D
ITERS = 6
NE, F = 64, 768
FC = F // P
TWO_PI = 2.0 * np.pi
MAGIC = 1.5 * 2.0 ** 23
SEED = float(0x5F3759DF)
VOCAB, NPI, POS, MODAL, SEG = 8000, 2500, 512, 16, 4


def constants():
    ident = np.eye(P, dtype=np.float32)
    mask = np.zeros((P, 8, M), np.float32)
    for r in range(P):
        mask[r, r // D] = D ** -0.5
    ones_bd = np.zeros((P, 2, D), np.float32)
    ones_bd[:M, 0] = 1.0
    ones_bd[M:, 1] = 1.0
    pick = np.zeros((P, MODAL * SEG), np.float32)
    for m in range(MODAL):
        for s in range(SEG):
            pick[m, SEG * m + s] = 1.0
            pick[MODAL + s, SEG * m + s] = 1.0
    return np.concatenate([ident, mask.reshape(P, -1), ones_bd.reshape(P, -1), pick], axis=1)


C_ID, C_MASK, C_ONES, C_PICK, C_ALL = 0, P, P + 8 * M, P + 8 * M + 2 * D, P + 8 * M + 2 * D + M


class Chain:

    def __init__(self, eng, sem):
        self.eng, self.sem, self.base, self.n = eng, sem, 0, 0

    def __call__(self, ins):
        ins.then_inc(self.sem, 1)
        self.n += 1

    def wait(self, back=0):
        self.eng.wait_ge(self.sem, self.base + (self.n - back))

    def link(self, ins):
        self(ins)
        self.wait()

    def enter(self, i, per):
        self.start, self.per = self.base + self.n, per
        self.base, self.n = self.start + i * per, 0

    def leave(self, turns, what):
        assert self.n == self.per, f"{what}: {self.n} in a turn, {self.per} given"
        self.base, self.n = self.start + self.per * turns, 0


ONE, DMA = 1, 16


def give(eng, ones, transfers, *slots):
    for s in ones + [s for x in slots for s in (*x.full_sem.values(), *x.free_sem.values())]:
        eng.sem_inc(s, ONE)
    for s in transfers:
        eng.sem_inc(s, DMA)


class Slots:

    def __init__(self, sem, name, products):
        self.uses, self.at = {}, {}
        for product, slot in products:
            self.at[product] = (slot, self.uses.get(slot, 0))
            self.uses[slot] = self.uses.get(slot, 0) + 1
        self.full_sem = {s: sem(f"{name}_{s}_full") for s in self.uses}
        self.free_sem = {s: sem(f"{name}_{s}_free") for s in self.uses}

    def turn(self, product, i):
        slot, k = self.at[product]
        return i * self.uses[slot] + k

    def claim(self, eng, product, i):
        eng.wait_ge(self.free_sem[self.at[product][0]], ONE + self.turn(product, i))

    def full(self, product):
        return self.full_sem[self.at[product][0]]

    def free(self, product):
        return self.free_sem[self.at[product][0]]

    def wait_full(self, eng, product, i):
        eng.wait_ge(self.full(product), ONE + self.turn(product, i) + 1)

    def wait_free(self, eng, product, i):
        eng.wait_ge(self.free(product), ONE + self.turn(product, i) + 1)


def spread(ap, parts):
    return bass.AP(tensor=ap.tensor, offset=ap.offset, ap=[[0, parts]] + [list(x) for x in ap.ap])


def rsqrt(nc, ch, y, t, v):
    ch.link(nc.vector.tensor_scalar(t.bitcast(I32), v.bitcast(I32), 1, None, ALU.logical_shift_right))
    ch.link(nc.vector.tensor_scalar(y.bitcast(I32), t.bitcast(I32), -1.0, SEED, ALU.mult, ALU.add))
    for _ in range(3):
        ch.link(nc.vector.tensor_tensor(t, y, y, ALU.mult))
        ch.link(nc.vector.scalar_tensor_tensor(t, t, -0.5, v, ALU.mult, ALU.mult))
        ch.link(nc.vector.scalar_tensor_tensor(y, t, 1.5, y, ALU.add, ALU.mult))


class Core:
    pass


def build(nc, t):
    with ExitStack() as ctx:
        def sb(name, shape, dt=F32, where=ctx):
            return where.enter_context(nc.sbuf_tensor(name, shape, dt))

        def sem(name):
            return ctx.enter_context(nc.semaphore(name))

        c = Core()
        c.psum = ctx.enter_context(nc.psum_tensor("psum", [P, 8, 512], F32))
        c.const = sb("const", [P, C_ALL])
        c.ident = c.const[:, C_ID:C_ID + P]
        c.mask = c.const[:, C_MASK:C_MASK + 8 * M].rearrange("p (h m) -> p h m", m=M)
        c.ones_bd = c.const[:, C_ONES:C_ONES + 2 * D]
        c.h = sb("h", [P, NT, H])
        c.h_img = sb("h_img", [NI, B, H])
        c.rsum = sb("rsum", [P, B, TT + 1])
        c.late_room = sb("late_room", [P, 2 * NE * 2 * B])
        c.xsT = c.late_room[0:K2 + 1, :].rearrange("p (k n b) -> p k n b", k=2, n=NE)
        late = ctx.enter_context(ExitStack())
        c.V = sb("V", [P, B, PAIRS, D], where=late)
        c.landk = sb("landk", [P, B, 2, M], where=late)
        c.wprojT = sb("wprojT", [P, 2, H], where=late)
        c.phin = sb("phin", [K2, 2, 2 * NE], where=late)
        c.q_dram = nc.dram_tensor("q_rows", (B, P, 2, N), F32, kind="Internal").ap()
        c.c_dram = nc.dram_tensor("router_rows", (B, NE, N), F32, kind="Internal").ap()
        c.y_dram = nc.dram_tensor("expert_rows", (NE, B, H), F32, kind="Internal").ap()
        c.x_dram = nc.dram_tensor("attn2_rows", (B, P, PAIRS, HW), F32, kind="Internal").ap()
        c.pair_dram = nc.dram_tensor("modal_seg_table", (MODAL * SEG, H), F32, kind="Internal").ap()
        with ExitStack() as three:
            c.E = sb("E", [P, B, PAIRS, M], where=three)
            c.rows = sb("rows", [P, B, PAIRS], where=three)
            c.cols = sb("cols", [P, B, PAIRS], where=three)
            with ExitStack() as two:
                used = 0

                def early(parts, *shape):
                    nonlocal used
                    size = int(np.prod(shape))
                    a = c.late_room[0:parts, used:used + size]
                    used += size
                    return a.rearrange("p (a b) -> p a b", b=shape[1]) if len(shape) == 2 else a
                c.wT = early(K2, 2, 640)
                c.turns_w = early(P, 2, H)
                c.turns_b = early(P, 2, H)
                c.gamma = early(P, H)
                c.beta = early(P, H)
                c.tau = early(P, 2, NT)
                c.linear = early(P, NT)
                c.hnT_img = early(K2, 2, B * NI)
                c.idx = sb("idx", [P, 4, NT], U32, where=two)
                with ExitStack() as work:
                    setup(nc, c, t, lambda n, s, d=F32: sb(n, s, d, work), sem)
                with ExitStack() as work:
                    landmarks(nc, c, t, lambda n, s, d=F32: sb("lm_" + n, s, d, work), sem)
            with ExitStack() as work:
                pseudo_inverse(nc, c, lambda n, s, d=F32: sb("pi_" + n, s, d, work), sem)
        with ExitStack() as work:
            attention(nc, c, lambda n, s, d=F32: sb("at_" + n, s, d, work), sem)
        late.close()
        with ExitStack() as work:
            experts(nc, c, t, lambda n, s, d=F32: sb("ex_" + n, s, d, work), sem)
        with ExitStack() as work:
            combine(nc, c, t, lambda n, s, d=F32: sb("co_" + n, s, d, work), sem)


def setup(nc, c, t, sb, sem):
    tokw = sb("tokw", [K2, 2, F])
    wq = sb("wq", [K2, 6, H])
    wp = sb("wp", [K2, 2, H])
    phi = sb("phi", [K2, 2, NE])
    phi_sq = sb("phi_sq", [K2, 2, NE])
    tokwT = sb("tokwT", [P, 6, H])
    room = c.h[:].rearrange("p k h -> p (k h)")
    img = room[0:3 * B, 0:4096]
    regrouped = room[0:3 * B, 4096:8192].rearrange("p (i j r q) -> p i j r q", i=4, j=4, r=16)
    patches = sb("patches", [P, 16, 2, 3 * B])
    tok_b = sb("tok_b", [NI, H])
    ids = sb("ids", [NT, 5, P], I32)
    idf = sb("idf", [NT, 5, P])
    below = sb("below", [NT, 5, P])
    taus = sb("taus", [NT, 2, P])
    tables = sb("tables", [MODAL + SEG, H])
    pair_rows = sb("pair_rows", [MODAL * SEG, H])
    lin_w = sb("lin_w", [P, 4])
    scale = sb("scale", [P, 1])
    ones = sb("ones", [P, P])
    tmp = sb("tmp", [P, NE])
    tmp2 = sb("tmp2", [P, NE])
    stats = sb("stats_i", [NI, B, 6])
    mv = sb("mv_i", [NI, B, 2])
    rstd = sb("rstd_i", [NI, B])
    hn_img = sb("hn_img", [NI, B, H])
    loaded, gp_loaded = sem("setup_loaded"), sem("setup_gp_loaded")
    pe, dve, act = sem("setup_pe"), sem("setup_dve"), sem("setup_act")
    regroup = sem("setup_regrouped")
    zeroed, stored = sem("setup_zeroed"), sem("setup_stored")
    ps = c.psum

    with nc.Block() as block:
        @block.sync
        def _(sp):
            n = 0

            def load(dst, src):
                nonlocal n
                sp.dma_start(dst, src).then_inc(loaded, 16)
                n += 16
            load(c.const[:], t["const"])
            load(tokw[:], t["L0_tok_W"].rearrange("(k p) f -> p k f", k=2))
            load(wq[:], t["L0_attn_w_qkv"].rearrange("(k p) f -> p k f", k=6))
            load(wp[:], t["L0_attn_w_proj"].rearrange("(k p) f -> p k f", k=2))
            load(phi[:], t["L0_ffn_phi"].rearrange("(k p) n o -> p k (n o)", k=2))
            load(img, t["x"].rearrange("b c h w -> (b c) (h w)"))
            load(tok_b[:], spread(t["L0_tok_b"], NI))
            for k, name in enumerate(("x_txt", "itok_BS_0_9999", "itok_BS_0_2047", "itok_BS_0_15", "itok_BS_0_3")):
                load(ids[:, k, :], t[name].rearrange("b (t p) -> (b t) p", p=P))
            for k, name in enumerate(("fside_BS_age_tau", "fside_BS_delays_tau")):
                load(taus[:, k, :], t[name].rearrange("b (t p) -> (b t) p", p=P))
            load(tables[0:MODAL, :], t["L0_txt_modalities_table"])
            load(tables[MODAL:MODAL + SEG, :], t["L0_txt_seg_table"])
            for k, name in enumerate(("age", "delay")):
                load(lin_w[:, k:k + 1], spread(t[f"L0_txt_{name}_w0"][0], P))
                load(lin_w[:, 2 + k:3 + k], spread(t[f"L0_txt_{name}_b0"], P))
            load(scale[:], spread(t["L0_ffn_scale"], P))
            load(c.gamma[:], spread(t["L0_txt_ln_gamma"], P))
            load(c.beta[:], spread(t["L0_txt_ln_beta"], P))
            sp.wait_ge(zeroed, 3)
            for k, name in enumerate(("age", "delay")):
                load(c.turns_w[:, k, 0:H - 1], spread(t[f"L0_txt_{name}_w"][0], P))
                load(c.turns_b[:, k, 0:H - 1], spread(t[f"L0_txt_{name}_b"], P))
            assert n == LOADED
            sp.wait_ge(dve, SETUP_DVE["pair_rows"])
            sp.dma_start(c.pair_dram, pair_rows[:]).then_inc(stored, 16)
            sp.wait_ge(dve, SETUP_DVE["proj"])
            sp.dma_start(c.wprojT[M:M + 1, 1, :], t["L0_attn_b_proj"].rearrange("(a h) -> a h", a=1)).then_inc(stored, 16)
            sp.wait_ge(stored, 32)

        @block.gpsimd
        def _(gp):
            nc.gpsimd.memset(c.turns_w[:], 0.0).then_inc(zeroed, 1)
            nc.gpsimd.memset(c.turns_b[:], 0.0).then_inc(zeroed, 1)
            nc.gpsimd.memset(ones[:], 1.0).then_inc(zeroed, 1)

        @block.tensor
        def _(te):
            te.wait_ge(loaded, LOADED)
            for k in range(6):
                ch, half = k // 2, k % 2
                if k >= 2:
                    te.wait_ge(dve, k - 1)
                for e in range(2):
                    src = tokw[:, e, 384 * half + ch:384 * half + 384:3]
                    last = nc.tensor.transpose(ps[:, k % 2, K2 * e:K2 * e + K2], src, c.ident[0:K2, 0:K2])
                last.then_inc(pe, 1)
            for k in range(6):
                te.wait_ge(dve, 5 + k)
                for e in range(2):
                    last = nc.tensor.transpose(ps[0:K2, k % 2, K2 * e:K2 * e + K2], wq[:, k, K2 * e:K2 * e + K2],
                                               c.ident[0:K2, 0:K2])
                last.then_inc(pe, 1)
            te.wait_ge(dve, SETUP_DVE["qkv"])
            for e in range(2):
                nc.tensor.transpose(ps[:, 0, K2 * e:K2 * e + K2], wp[:, e, 0:P], c.ident[0:K2, 0:K2])
                last = nc.tensor.transpose(ps[0:M, 1, K2 * e:K2 * e + K2], wp[:, e, P:H], c.ident[0:K2, 0:K2])
            last.then_inc(pe, 1)
            te.wait_ge(dve, SETUP_DVE["proj"])
            te.wait_ge(dve, SETUP_DVE["ids"])
            for k in range(4):
                nc.tensor.transpose(ps[:, 2, M * k:M * k + M], idf[:, k, :], c.ident[0:NT, 0:NT])
            for k in range(2):
                last = nc.tensor.transpose(ps[:, 3, M * k:M * k + M], taus[:, k, :], c.ident[0:NT, 0:NT])
            last.then_inc(pe, 1)
            nc.tensor.matmul(ps[0:MODAL * SEG, 4, 0:H], c.const[0:MODAL + SEG, C_PICK:C_PICK + M], tables[:],
                             start=True, stop=True).then_inc(pe, 1)
            te.wait_ge(dve, SETUP_DVE["phi_sq"])
            te.wait_ge(zeroed, 3)
            for k in range(2):
                last = nc.tensor.matmul(ps[:, 5, 0:NE], ones[0:K2, :], phi_sq[:, k, :], start=(k == 0), stop=(k == 1))
            last.then_inc(pe, 1)
            for i in range(4):
                te.wait_ge(regroup, i + 1)
                for j in range(4):
                    g = 4 * i + j
                    if g >= 2:
                        te.wait_ge(act, g - 1)
                    for half in range(2):
                        src = regrouped[:, i, j, 8 * half:8 * half + 8, :].rearrange("p r q -> p (r q)")
                        last = nc.tensor.transpose(ps[:, 6 + g % 2, 48 * half:48 * half + 48], src, c.ident[0:48, 0:48])
                    last.then_inc(pe, 1)
            te.wait_ge(act, 16)
            for g in range(4):
                if g >= 2:
                    te.wait_ge(dve, SETUP_DVE["embed"] + 4 * (g - 1))
                for k in range(6):
                    ch, half = k // 2, k % 2
                    for j in range(4):
                        b = 4 * g + j
                        last = nc.tensor.matmul(ps[32 * j:32 * j + NI, g % 2, 0:H], patches[:, :, half, 3 * b + ch],
                                                tokwT[:, k, :], start=(k == 0), stop=(k == 5))
                last.then_inc(pe, 1)
            te.wait_ge(dve, SETUP_DVE["hn_img"])
            for b in range(B):
                for k in range(2):
                    last = nc.tensor.transpose(ps[0:K2, 2, 256 * k + NI * b:256 * k + NI * b + NI],
                                               hn_img[:, b, K2 * k:K2 * k + K2], c.ident[0:NI, 0:NI])
            last.then_inc(pe, 1)

        @block.scalar
        def _(sc):
            sc.wait_ge(loaded, LOADED)
            for i in range(4):
                src = img[:, 1024 * i:1024 * i + 1024].rearrange("p (r j q) -> p j r q", r=16, j=4)
                nc.scalar.activation(regrouped[:, i], src, ACT.Copy).then_inc(regroup, 1)
            for g in range(16):
                sc.wait_ge(pe, 17 + g)
                nc.scalar.activation(patches[:, g, :, :].rearrange("p h f -> p (h f)"), ps[:, 6 + g % 2, 0:96],
                                     ACT.Copy).then_inc(act, 1)
            sc.wait_ge(pe, 37)
            nc.scalar.activation(c.hnT_img[:], ps[0:K2, 2, 0:512].rearrange("p (k n) -> p k n", k=2),
                                 ACT.Copy).then_inc(act, 1)

        @block.vector
        def _(v):
            ch = Chain(v, dve)

            def mark(name):
                assert ch.n == SETUP_DVE[name], (name, ch.n)
            for k in range(6):
                v.wait_ge(pe, k + 1)
                ch(nc.vector.tensor_copy(tokwT[:, k, :], ps[:, k % 2, 0:H]))
            for k in range(6):
                v.wait_ge(pe, 7 + k)
                part, lo = k // 2, 96 * (k % 2)
                runs = []
                if part == 0:
                    runs = [(lo, lo + 96, 0)] + ([(128, 192, 128)] if lo else [])
                elif part == 1:
                    runs = [(0, 96, 320)] if lo == 0 else [(96, 128, 320), (128, 192, 64)]
                else:
                    runs = [(lo, lo + 96, 448)]
                for r0, r1, off in runs:
                    src = ps[0:K2, k % 2, 0:H].rearrange("p (e r) -> p e r", e=2)[:, :, r0 - lo:r1 - lo]
                    dst = c.wT[:, :, r0 + off:r1 + off]
                    ins = nc.vector.tensor_copy(dst, src)
                ch(ins)
            mark("qkv")
            v.wait_ge(pe, 13)
            ch(nc.vector.tensor_copy(c.wprojT[:, 0, :], ps[:, 0, 0:H]))
            ch(nc.vector.tensor_copy(c.wprojT[0:M, 1, :], ps[0:M, 1, 0:H]))
            mark("proj")
            v.wait_ge(loaded, LOADED)
            for k, size in enumerate((VOCAB, NPI, POS, MODAL, SEG)):
                ch(nc.vector.tensor_scalar(below[:, k, :], ids[:, k, :], 0.0, float(size), ALU.is_lt, ALU.mult))
            for k in range(5):
                ch.wait(4)
                ch(nc.vector.tensor_tensor(idf[:, k, :], ids[:, k, :], below[:, k, :], ALU.add))
            for k, size in enumerate((VOCAB, NPI, POS, MODAL, SEG)):
                ch.wait(4)
                ch(nc.vector.tensor_scalar(idf[:, k, :], idf[:, k, :], 0.0, float(size - 1), ALU.max, ALU.min))
            ch.wait()
            ch.link(nc.vector.scalar_tensor_tensor(idf[:, 3, :], idf[:, 3, :], float(SEG), idf[:, 4, :], ALU.mult, ALU.add))
            mark("ids")
            ch.link(nc.vector.tensor_tensor(phi_sq[:], phi[:], phi[:], ALU.mult))
            mark("phi_sq")
            v.wait_ge(pe, 14)
            ch(nc.vector.tensor_copy(c.idx[:], ps[:, 2, 0:4 * NT].rearrange("p (k n) -> p k n", k=4)))
            ch.link(nc.vector.tensor_copy(c.tau[:], ps[:, 3, 0:2 * NT].rearrange("p (k n) -> p k n", k=2)))
            v.wait_ge(pe, 15)
            ch(nc.vector.tensor_copy(pair_rows[:], ps[0:MODAL * SEG, 4, 0:H]))
            mark("pair_rows")
            ch.link(nc.vector.tensor_scalar(c.linear[:], c.tau[:, 0, :], lin_w[:, 0:1], lin_w[:, 2:3], ALU.mult, ALU.add))
            ch.link(nc.vector.scalar_tensor_tensor(c.linear[:], c.tau[:, 1, :], lin_w[:, 1:2], c.linear[:], ALU.mult, ALU.add))
            ch.link(nc.vector.tensor_scalar(c.linear[:], c.linear[:], lin_w[:, 3:4], None, ALU.add))
            ch(nc.vector.tensor_scalar(c.turns_w[:], c.turns_w[:], 1.0 / TWO_PI, None, ALU.mult))
            ch(nc.vector.tensor_scalar(c.turns_b[:], c.turns_b[:], 1.0 / TWO_PI, None, ALU.mult))
            v.wait_ge(pe, 16)
            ch.link(nc.vector.tensor_scalar(tmp2[:], ps[:, 5, 0:NE], 1e-24, None, ALU.max))
            y = sb("phi_rn", [P, NE])
            rsqrt(nc, ch, y[:], tmp[:], tmp2[:])
            ch.link(nc.vector.tensor_scalar(y[:], y[:], scale[:, 0:1], None, ALU.mult))
            for k in range(2):
                for j in range(2):
                    ch(nc.vector.tensor_tensor(c.phin[:, k, NE * j:NE * j + NE], phi[:, k, :], y[0:K2, :], ALU.mult))
            mark("embed")
            for g in range(4):
                v.wait_ge(pe, 33 + g)
                for j in range(4):
                    ch(nc.vector.tensor_tensor(c.h_img[:, 4 * g + j, :], ps[32 * j:32 * j + NI, g % 2, 0:H], tok_b[:], ALU.add))
            ch.wait()
            moments(nc, ch, c.h_img, stats, mv, rstd, sb("rt_i", [NI, B]), sb("ve_i", [NI, B]), B, 1e-5)
            for k in range(B):
                ch(nc.vector.tensor_scalar(hn_img[:, k, :], c.h_img[:, k, :], mv[:, k, 0:1], rstd[:, k:k + 1], ALU.subtract, ALU.mult))
            mark("hn_img")


LOADED = 16 * 27
SETUP_DVE = dict(qkv=12, proj=14, ids=30, phi_sq=31, pair_rows=34, embed=56, hn_img=132)


def moments(nc, ch, src, stats, mv, rstd, rt, ve, n, eps):
    for k in range(n):
        ch(nc.vector.bn_stats(stats[:, k, :], src[:, k, :]))
    ch.wait()
    nc.vector.tensor_copy(rt[:, 0:1], stats[:, 0, 0:1])
    for k in range(n):
        ch(nc.vector.bn_aggr(mv[:, k, :], stats[:, k, :]))
    ch.wait()
    ch.link(nc.vector.tensor_scalar(ve[:, 0:n], mv[:, 0:n, 1], eps, None, ALU.add))
    rsqrt(nc, ch, rstd[:, 0:n], rt[:, 0:n], ve[:, 0:n])


HALF = NP // 2
LM_ATTN2 = {1: "xT0", 2: "xT1", 4: "x0", 5: "x1"}
LM_PRODUCTS = [("hnT0", "A0"), ("hnT1", "A1"), ("hnT2", "A2"), ("hnT3", "A3"),
               ("k2a", "A0"), ("k2b", "A1"), ("land", "A2"), ("q1a", "A3"), ("q1b", "A0"), ("q0a", "A1"), ("q0b", "A2"),
               ("v01", "A0"), ("v23", "A1"), ("v4", "A2"), ("sim2", "A3")]
for _p in range(PAIRS):
    LM_PRODUCTS += [(f"sim3_{_p}", f"S{_p % 2}"), (f"p3T_{_p}", "A1" if _p % 2 else "A3"), (f"p3I_{_p}", "A2")]
    if _p in LM_ATTN2:
        LM_PRODUCTS.append((LM_ATTN2[_p], "A0"))
LM_PRODUCTS += [("u", "A0"), ("uT", "A1")]
LM_DVE = 70


def landmarks(nc, c, t, sb, sem):
    got = sb("got", [P, TT, 4, H])
    emb = sb("emb", [P, TT, H])
    turns = sb("turns", [P, TT, 2, H])
    whole = sb("whole", [P, TT, 2, H])
    hm = sb("hm", [P, TT, H])
    hn = sb("hn", [P, TT, H])
    hnT = sb("hnT", [K2, 2, NP])
    hnl = sb("hnl", [K2, 2, M])
    q0 = sb("q0", [P, 2, N])
    k1 = sb("k1", [P, NP])
    k2 = sb("k2", [P, NP])
    v = sb("v", [P, TT + 1, H])
    land = sb("land", [P, 4, M])
    ql = sb("ql", [P, 12, M])
    w2 = sb("w2", [P, PAIRS, M])
    e2 = w2
    small = sb("small", [P, 6, PAIRS])
    x2 = sb("x2", [P, PAIRS, HW])
    x2T = sb("x2T", [P, PAIRS, HW])
    p3 = sb("p3", [P, 3, NP])
    p3T = sb("p3T", [P, TT + 1, PAIRS, HW])
    u = sb("u", [P, 2, HW])
    stats, mv = sb("stats", [P, TT, 6]), sb("mv", [P, TT, 2])
    rstd, rt, ve = sb("rstd", [P, TT]), sb("rt", [P, TT]), sb("ve", [P, TT])
    S = Slots(sem, "lm", LM_PRODUCTS)
    slot = {"A0": 0, "A1": 1, "A2": 2, "A3": 3, "S0": 4, "S1": 6}

    def bank(product):
        return slot[S.at[product][0]]
    cleared = sem("lm_cleared")
    gathered, summed, paired, emb_in = sem("lm_gathered"), sem("lm_summed"), sem("lm_paired"), sem("lm_emb_in")
    turned, rounded, reduced, sined = sem("lm_turned"), sem("lm_rounded"), sem("lm_reduced"), sem("lm_sined")
    hn_ready, img_in, hnT_in = sem("lm_hn_ready"), sem("lm_img_in"), sem("lm_hnT_in")
    embedded, kept, halfway = sem("lm_embedded"), sem("lm_kept"), sem("lm_halfway")
    hnl_ready, ql_ready = sem("lm_hnl_ready"), sem("lm_ql_ready")
    sub2, exp2, x2_ready, max3, exp3 = sem("lm_sub2"), sem("lm_exp2"), sem("lm_x2_ready"), sem("lm_max3"), sem("lm_exp3")
    x2_stored = sem("lm_x2_stored")
    q_stored = sem("lm_q_stored")
    dve_done, act_done, gp_done = sem("lm_dve"), sem("lm_act"), sem("lm_gp")
    ps = c.psum

    with nc.Block() as block:
        @block.gpsimd
        def _(gp):
            nc.gpsimd.memset(hnT[:], 0.0).then_inc(cleared, 1)
            nc.gpsimd.memset(x2[:], 0.0).then_inc(cleared, 1)
            nc.gpsimd.memset(c.landk[:, :, 0:1, :], 0.0).then_inc(cleared, 1)

            idx_b, spare = sb("idx_b", [P, 4, TT], U32), sb("spare", [P, 1])

            def gathers(b):
                nc.gpsimd.tensor_copy(idx_b[:], c.idx[:, :, bass.ds(b * TT, TT)]).then_inc(gp_done, 1)
                gp.wait_ge(gp_done, b + 1)
                nc.gpsimd.tensor_tensor(spare[:], c.const[:, 0:1], c.const[:, 0:1], ALU.add)
                for k in range(TT):
                    for r, table in enumerate(("L0_txt_word_table", "L0_txt_npi_table", "L0_txt_posi_table", None)):
                        gp.indirect_dma_start(out=got[:, k, r, :], out_offset=None, in_=t[table] if table else c.pair_dram,
                                              in_offset=bass.IndirectOffsetOnAxis(ap=idx_b[:, r, k:k + 1], axis=0)
                                              ).then_inc(gathered, 16)

            with gp.Fori(0, B) as b:
                gp.wait_ge(emb_in, ONE + b)
                gathers(b)
                gp.wait_ge(gathered, b * (16 * 4 * TT) + 16 * 4 * TT)
                nc.gpsimd.tensor_tensor(got[:, :, 0:2, :], got[:, :, 0:2, :], got[:, :, 2:4, :], ALU.add).then_inc(paired, 1)
                gp.wait_ge(paired, b + 1)
                gp.wait_ge(summed, ONE + b)
                nc.gpsimd.tensor_tensor(emb[:], got[:, :, 0, :], got[:, :, 1, :], ALU.add).then_inc(halfway, 1)
                gp.wait_ge(sined, b + 1)
                gp.wait_ge(halfway, 2 * b + 1)
                nc.gpsimd.tensor_tensor(emb[:], emb[:], whole[:, :, 0, :], ALU.add).then_inc(halfway, 1)
                gp.wait_ge(halfway, 2 * b + 2)
                nc.gpsimd.tensor_tensor(emb[:], emb[:], whole[:, :, 1, :], ALU.add).then_inc(emb_in, 1)

        @block.sync
        def _(sp):
            give(sp, [emb_in, summed, exp3, kept], [q_stored, x2_stored], S)
            def store(b):
                S.wait_free(sp, "q0b", b)
                S.wait_free(sp, "q1b", b)
                S.wait_free(sp, "q0a", b)
                sp.dma_start(c.q_dram[b], q0[:]).then_inc(q_stored, 16)
                sp.wait_ge(x2_ready, b + 1)
                sp.dma_start(c.x_dram[b], x2[:]).then_inc(x2_stored, 16)
            with sp.Fori(0, B) as b:
                store(b)
            sp.wait_ge(q_stored, DMA + 16 * B)
            sp.wait_ge(x2_stored, DMA + 16 * B)

        @block.tensor
        def _(te):
            te.wait_ge(cleared, 3)

            def turn(b):
                te.wait_ge(hn_ready, b + 1)
                for k in range(TT):
                    S.claim(te, f"hnT{k}", b)
                    for e in range(2):
                        last = nc.tensor.transpose(ps[0:K2, bank(f"hnT{k}"), P * e:P * e + P],
                                                   hn[:, k, K2 * e:K2 * e + K2], c.ident)
                    last.then_inc(S.full(f"hnT{k}"), 1)
                for k in range(TT):
                    S.wait_free(te, f"hnT{k}", b)
                te.wait_ge(img_in, b + 1)

                def rows(product, lo, c0, width):
                    S.claim(te, product, b)
                    for e in range(2):
                        last = nc.tensor.matmul(ps[:, bank(product), 0:width], c.wT[:, e, lo:lo + P],
                                                hnT[:, e, c0:c0 + width], start=(e == 0), stop=(e == 1))
                    last.then_inc(S.full(product), 1)
                rows("k2a", 320, 0, HALF)
                rows("k2b", 320, HALF, HALF)
                te.wait_ge(hnl_ready, b + 1)
                S.claim(te, "land", b)
                for k, lo in enumerate((0, 128, 192, 320)):
                    for e in range(2):
                        last = nc.tensor.matmul(ps[:, bank("land"), M * k:M * k + M], c.wT[:, e, lo:lo + P], hnl[:, e, :],
                                                start=(e == 0), stop=(e == 1))
                last.then_inc(S.full("land"), 1)
                rows("q1a", 128, 0, HALF)
                rows("q1b", 128, HALF, HALF)
                rows("q0a", 0, PAD, N // 2)
                rows("q0b", 0, PAD + N // 2, N // 2)
                for k in range(TT + 1):
                    product = ("v01", "v23", "v4")[k // 2]
                    rows_n, c0 = (P, PAD + NI + P * k) if k < TT else (NI, PAD)
                    if k % 2 == 0:
                        S.claim(te, product, b)
                    for e in range(2):
                        last = nc.tensor.matmul(ps[0:rows_n, bank(product), H * (k % 2):H * (k % 2) + H],
                                                hnT[:, e, c0:c0 + rows_n], c.wT[:, e, 448:640],
                                                start=(e == 0), stop=(e == 1))
                    if k % 2 or k == TT:
                        last.then_inc(S.full(product), 1)

                te.wait_ge(ql_ready, b + 1)
                S.claim(te, "sim2", b)
                for p in range(PAIRS):
                    last = nc.tensor.matmul(ps[:, bank("sim2"), M * p:M * p + M], ql[:, 2 * p:2 * p + 2, :],
                                            land[:, 3 if p < 4 else 1, :], start=True, stop=True)
                last.then_inc(S.full("sim2"), 1)
                def scores(p):
                    product = f"sim3_{p}"
                    if p == 0:
                        S.wait_free(te, "k2b", b)
                    if p == 4:
                        S.wait_free(te, "q1b", b)
                    te.wait_ge(exp3, ONE + b * PAIRS + max(p - 1, 0))
                    src = k2 if p < 4 else k1
                    nc.tensor.matmul(ps[:, bank(product), 0:512], ql[:, 2 * p:2 * p + 2, :], src[:, 0:512], start=True, stop=True)
                    nc.tensor.matmul(ps[:, bank(product) + 1, 0:NP - 512], ql[:, 2 * p:2 * p + 2, :], src[:, 512:NP],
                                     start=True, stop=True).then_inc(S.full(product), 1)

                def turn_probs(p):
                    te.wait_ge(exp3, ONE + b * PAIRS + (p + 1))
                    S.claim(te, f"p3T_{p}", b)
                    S.claim(te, f"p3I_{p}", b)
                    for k in range(TT):
                        c0 = PAD + NI + P * k
                        last = nc.tensor.transpose(ps[:, bank(f"p3T_{p}"), HW * k:HW * k + HW], p3[:, p % 3, c0:c0 + P], c.ident)
                    last.then_inc(S.full(f"p3T_{p}"), 1)
                    nc.tensor.transpose(ps[0:NI, bank(f"p3I_{p}"), 0:HW], p3[:, p % 3, PAD:PAD + NI], c.ident
                                        ).then_inc(S.full(f"p3I_{p}"), 1)

                def attn2_turned(g):
                    te.wait_ge(x2_ready, b + 1)
                    S.claim(te, f"xT{g}", b)
                    for k in range(3):
                        last = nc.tensor.transpose(ps[:, bank(f"xT{g}"), HW * k:HW * k + HW], x2[:, 3 * g + k, :], c.ident)
                    last.then_inc(S.full(f"xT{g}"), 1)

                def attn2_squared(g):
                    S.claim(te, f"x{g}", b)
                    for k in range(3):
                        last = nc.tensor.matmul(ps[:, bank(f"x{g}"), HW * k:HW * k + HW], x2T[:, 3 * g + k, :],
                                                x2T[:, 3 * g + k, :], start=True, stop=True)
                    last.then_inc(S.full(f"x{g}"), 1)
                scores(0)
                scores(1)
                for p in range(PAIRS):
                    if p + 2 < PAIRS:
                        scores(p + 2)
                    turn_probs(p)
                    if p in LM_ATTN2:
                        (attn2_turned if p < 4 else attn2_squared)(int(LM_ATTN2[p][-1]))
                S.claim(te, "u", b)
                for g in range(2):
                    S.wait_free(te, f"p3T_{3 + 2 * g}", b)
                    if g:
                        S.wait_free(te, "p3T_4", b)
                    S.wait_free(te, f"p3I_{3 + 2 * g}", b)
                    for k in range(TT + 1):
                        n = P if k < TT else NI
                        for p in range(4 * g, min(4 * g + 4, PAIRS)):
                            j = p % 4
                            last = nc.tensor.matmul(ps[32 * j:32 * j + 32, bank("u"), HW * g:HW * g + HW],
                                                    v[0:n, k, 32 * p:32 * p + 32], p3T[0:n, k, p, :],
                                                    start=(k == 0), stop=(k == TT))
                last.then_inc(S.full("u"), 1)
                S.wait_free(te, "u", b)
                S.claim(te, "uT", b)
                nc.tensor.transpose(ps[:, bank("uT"), 0:P], u[:, 0, :], c.ident)
                nc.tensor.transpose(ps[:, bank("uT"), P:P + M], u[0:M, 1, :], c.ident[0:M, 0:M]).then_inc(S.full("uT"), 1)
            with te.Fori(0, B) as b:
                turn(b)

        @block.scalar
        def _(sc):
            def copy(dst, src, scale=1.0):
                return nc.scalar.activation(dst, src, ACT.Copy, scale=scale)

            def rounds(b):
                sc.wait_ge(emb_in, ONE + b)
                sc.wait_ge(turned, b + 1)
                nc.scalar.activation(whole[:], turns[:], ACT.Copy, bias=MAGIC).then_inc(rounded, 1)

            def sines(b):
                sc.wait_ge(reduced, b + 1)
                nc.scalar.activation(whole[:], turns[:], ACT.Sin, scale=-TWO_PI).then_inc(sined, 1)

            def keep(b):
                sc.wait_ge(embedded, b + 1)
                copy(c.h[:, bass.ds(b * TT, TT), :], hm[:]).then_inc(kept, 1)

            def turn(b, following, second):
                sc.wait_ge(S.full("v4"), ONE + b * S.uses["A2"])
                copy(hnT[:, :, PAD:PAD + NI], c.hnT_img[:, :, bass.ds(b * NI, NI)]).then_inc(img_in, 1)
                for k in range(TT):
                    S.wait_full(sc, f"hnT{k}", b)
                    c0 = PAD + NI + P * k
                    copy(hnT[:, :, c0:c0 + P], ps[0:K2, bank(f"hnT{k}"), 0:2 * P].rearrange("p (e n) -> p e n", e=2)
                         ).then_inc(S.free(f"hnT{k}"), 1)
                for part, half in (("k2a", 0), ("k2b", 1)):
                    S.wait_full(sc, part, b)
                    copy(k2[:, HALF * half:HALF * half + HALF], ps[:, bank(part), 0:HALF]).then_inc(S.free(part), 1)
                S.wait_full(sc, "land", b)
                copy(land[:], ps[:, bank("land"), 0:4 * M].rearrange("p (k m) -> p k m", k=4), 1.0 / L
                     ).then_inc(S.free("land"), 1)
                if second:
                    rounds(b + 2)
                sc.wait_ge(q_stored, DMA + b * 16)
                for part, half in (("q1a", 0), ("q1b", 1)):
                    S.wait_full(sc, part, b)
                    copy(k1[:, HALF * half:HALF * half + HALF], ps[:, bank(part), 0:HALF]).then_inc(act_done, 1)
                    if half == 0:
                        copy(q0[:, 1, 0:HALF - PAD], ps[:, bank(part), PAD:HALF]).then_inc(S.free(part), 1)
                    else:
                        copy(q0[:, 1, HALF - PAD:N], ps[:, bank(part), 0:HALF]).then_inc(S.free(part), 1)
                for part, half in (("q0a", 0), ("q0b", 1)):
                    S.wait_full(sc, part, b)
                    copy(q0[:, 0, N // 2 * half:N // 2 * half + N // 2], ps[:, bank(part), 0:N // 2]).then_inc(S.free(part), 1)
                if second:
                    sines(b + 2)
                for k, part in enumerate(("v01", "v23", "v4")):
                    S.wait_full(sc, part, b)
                    if k < 2:
                        copy(v[:, 2 * k:2 * k + 2, :], ps[:, bank(part), 0:2 * H].rearrange("p (k h) -> p k h", k=2)).then_inc(S.free(part), 1)
                    else:
                        copy(v[0:NI, TT, :], ps[0:NI, bank(part), 0:H]).then_inc(S.free(part), 1)
                if following:
                    keep(b + 1)
                sc.wait_ge(sub2, b + 1)
                nc.scalar.activation(e2[:], w2[:], ACT.Exp).then_inc(exp2, 1)
                for p in range(PAIRS + 1):
                    if p < PAIRS:
                        sc.wait_ge(max3, b * PAIRS + (p + 1))
                        if p >= 3:
                            S.wait_full(sc, f"p3I_{p - 3}", b)
                        src = ps[:, bank(f"sim3_{p}"):bank(f"sim3_{p}") + 2, :].rearrange("p k n -> p (k n)")[:, 0:NP]
                        nc.scalar.activation(p3[:, p % 3, :], src, ACT.Exp, bias=small[:, 3, p:p + 1],
                                             accum_out=small[:, 4, p:p + 1]).then_inc(exp3, 1)
                    if p:
                        q = p - 1
                        S.wait_full(sc, f"p3I_{q}", b)
                        copy(p3T[0:NI, TT, q, :], ps[0:NI, bank(f"p3I_{q}"), 0:HW]).then_inc(S.free(f"p3I_{q}"), 1)
                        if q in (1, 2):
                            g = q - 1
                            S.wait_full(sc, f"xT{g}", b)
                            copy(x2T[:, 3 * g:3 * g + 3, :], ps[:, bank(f"xT{g}"), 0:3 * HW].rearrange("p (k m) -> p k m", k=3)
                                 ).then_inc(S.free(f"xT{g}"), 1)
            rounds(0)
            sines(0)
            rounds(1)
            sines(1)
            keep(0)
            with sc.Fori(0, B - 2) as b:
                turn(b, True, True)
            turn(B - 2, True, False)
            turn(B - 1, False, False)

        @block.vector
        def _(ve_):
            ch = Chain(ve_, dve_done)

            def angles(b):
                for k in range(TT):
                    for j in range(2):
                        ch(nc.vector.scalar_tensor_tensor(turns[:, k, j, :], c.turns_w[:, j, :],
                                                          c.tau[:, j, bass.ds(b * TT + k, 1)], c.turns_b[:, j, :], ALU.mult, ALU.add)) \
                            if (k, j) != (TT - 1, 1) else \
                            nc.vector.scalar_tensor_tensor(turns[:, k, j, :], c.turns_w[:, j, :],
                                                           c.tau[:, j, bass.ds(b * TT + k, 1)], c.turns_b[:, j, :],
                                                           ALU.mult, ALU.add).then_inc(turned, 1)

            def fractions(b):
                ve_.wait_ge(rounded, b + 1)
                ve_.wait_ge(turned, b + 1)
                nc.vector.scalar_tensor_tensor(turns[:].rearrange("p a j h -> p (a j h)"), whole[:].rearrange("p a j h -> p (a j h)"),
                                               MAGIC, turns[:].rearrange("p a j h -> p (a j h)"), ALU.subtract, ALU.subtract
                                               ).then_inc(reduced, 1)

            def embed_moments(b):
                ve_.wait_ge(emb_in, ONE + b + 1)
                ch.link(nc.vector.tensor_tensor(emb[:, :, H - 1], emb[:, :, H - 1], c.linear[:, bass.ds(b * TT, TT)], ALU.add))
                moments(nc, ch, emb, stats, mv, rstd, rt, ve, TT, 1e-12)

            def embed(b):
                ve_.wait_ge(kept, ONE + b)
                for k in range(TT):
                    ins = nc.vector.scalar_tensor_tensor(hm[:, k, :], emb[:, k, :], mv[:, k, 0:1], c.gamma, ALU.subtract, ALU.mult)
                    ch(ins) if k < TT - 1 else ins.then_inc(summed, 1)
                ve_.wait_ge(summed, ONE + b + 1)
                for k in range(TT):
                    ins = nc.vector.scalar_tensor_tensor(hm[:, k, :], hm[:, k, :], rstd[:, k:k + 1], c.beta, ALU.mult, ALU.add)
                    ch(ins) if k < TT - 1 else ins.then_inc(embedded, 1)
                ve_.wait_ge(embedded, b + 1)

            def normalise(b):
                moments(nc, ch, hm, stats, mv, rstd, rt, ve, TT, 1e-5)
                for k in range(TT):
                    ins = nc.vector.tensor_scalar(hn[:, k, :], hm[:, k, :], mv[:, k, 0:1], rstd[:, k:k + 1], ALU.subtract, ALU.mult)
                    ch(ins) if k < TT - 1 else ins.then_inc(hn_ready, 1)

            def turn(b, following, second):
                S.wait_free(ve_, "hnT3", b)
                ve_.wait_ge(img_in, b + 1)
                nc.vector.tensor_reduce(hnl[:], hnT[:].rearrange("p e (m l) -> p e m l", l=L), AX.X, ALU.add
                                        ).then_inc(hnl_ready, 1)
                if second:
                    ve_.wait_ge(sined, b + 2)
                    angles(b + 2)
                if following:
                    embed_moments(b + 1)
                S.wait_free(ve_, "land", b)
                ch(nc.vector.tensor_tensor(ql[:, 0:8, :], c.mask, land[:, 0:1, :].to_broadcast([P, 8, M]), ALU.mult))
                nc.vector.tensor_tensor(ql[:, 8:12, :], c.mask[:, 4:8, :], land[:, 2:3, :].to_broadcast([P, 4, M]), ALU.mult
                                        ).then_inc(ql_ready, 1)
                ch(nc.vector.tensor_copy(c.landk[:, bass.ds(b, 1), :, :].rearrange("p b k m -> p (b k) m"), land[:, 2:4, :]))
                if following:
                    embed(b + 1)
                if second:
                    fractions(b + 2)
                S.wait_full(ve_, "sim2", b)
                sim2 = ps[:, bank("sim2"), 0:PAIRS * M].rearrange("p (k m) -> p k m", m=M)
                ch.link(nc.vector.tensor_reduce(small[:, 0, :], sim2, AX.X, ALU.max, negate=True))
                nc.vector.tensor_tensor(w2[:], sim2, small[:, 0, :].unsqueeze(2).to_broadcast([P, PAIRS, M]), ALU.add
                                        ).then_inc(sub2, 1)
                ve_.wait_ge(sub2, b + 1)
                nc.vector.tensor_copy(small[:, 2, 0:1], small[:, 0, 0:1]).then_inc(S.free("sim2"), 1)
                for p in range(PAIRS):
                    S.wait_full(ve_, f"sim3_{p}", b)
                    src = ps[:, bank(f"sim3_{p}"):bank(f"sim3_{p}") + 2, :].rearrange("p k n -> p (k n)")[:, 0:NP]
                    nc.vector.tensor_reduce(small[:, 3, p:p + 1], src, AX.X, ALU.max, negate=True).then_inc(max3, 1)
                    if p == 1:
                        attn2(b)
                    if p >= 2:
                        probs_out(p - 2, b)
                squares(0, b)
                probs_out(PAIRS - 2, b)
                probs_out(PAIRS - 1, b)
                squares(1, b)
                if following:
                    normalise(b + 1)
                S.wait_full(ve_, "u", b)
                ch(nc.vector.tensor_copy(u[:, 0, :], ps[:, bank("u"), 0:HW]))
                nc.vector.tensor_copy(u[0:M, 1, :], ps[0:M, bank("u"), HW:2 * HW]).then_inc(S.free("u"), 1)
                ch.link(nc.vector.reciprocal(small[:, 5, :], small[:, 4, :]))
                S.wait_full(ve_, "uT", b)
                uT = ps[:, bank("uT"), 0:H].rearrange("p (k e d) -> p k e d", e=2, d=D)
                at = c.V[:, bass.ds(b, 1), :, :].rearrange("p b k d -> p (b k) d")
                ch(nc.vector.tensor_tensor(at[0:M], uT[0:M, :, 0, :], small[0:M, 5, :].unsqueeze(2).to_broadcast([M, PAIRS, D]), ALU.mult))
                nc.vector.tensor_tensor(at[M:P], uT[M:P, :, 1, :], small[M:P, 5, :].unsqueeze(2).to_broadcast([M, PAIRS, D]),
                                        ALU.mult).then_inc(S.free("uT"), 1)
                ch(nc.vector.tensor_reduce(c.rows[:, bass.ds(b, 1), :].rearrange("p b k -> p (b k)"), x2[:], AX.X, ALU.add))
                S.wait_free(ve_, "xT1", b)
                ch(nc.vector.tensor_reduce(c.cols[:, bass.ds(b, 1), :].rearrange("p b k -> p (b k)"), x2T[:], AX.X, ALU.add))

            def squares(g, b):
                S.wait_full(ve_, f"x{g}", b)
                x = ps[:, bank(f"x{g}"), 0:3 * HW].rearrange("p (k w) -> p k w", w=HW)
                for half in range(2):
                    r0 = M * half
                    at = c.E[r0:r0 + M, bass.ds(b, 1), 3 * g:3 * g + 3, :].rearrange("p b k w -> p (b k) w")
                    ins = nc.vector.tensor_copy(at, x[r0:r0 + M, :, r0:r0 + M])
                    ins.then_inc(S.free(f"x{g}"), 1) if half else ch(ins)

            def attn2(b):
                ve_.wait_ge(exp2, b + 1)
                S.wait_free(ve_, "sim2", b)
                ch.link(nc.vector.tensor_reduce(small[:, 1, :], e2[:], AX.X, ALU.add))
                ch.link(nc.vector.reciprocal(small[:, 2, :], small[:, 1, :]))
                ve_.wait_ge(x2_stored, DMA + b * 16)
                ch(nc.vector.tensor_tensor(x2[0:M, :, 0:M], e2[0:M], small[0:M, 2, :].unsqueeze(2).to_broadcast([M, PAIRS, M]), ALU.mult))
                nc.vector.tensor_tensor(x2[M:P, :, M:HW], e2[M:P], small[M:P, 2, :].unsqueeze(2).to_broadcast([M, PAIRS, M]), ALU.mult
                                        ).then_inc(x2_ready, 1)

            def probs_out(p, b):
                S.wait_full(ve_, f"p3T_{p}", b)
                nc.vector.tensor_copy(p3T[:, 0:TT, p, :], ps[:, bank(f"p3T_{p}"), :].rearrange("p (k m) -> p k m", m=HW)
                                      ).then_inc(S.free(f"p3T_{p}"), 1)
            ve_.wait_ge(cleared, 3)
            angles(0)
            fractions(0)
            embed_moments(0)
            embed(0)
            angles(1)
            fractions(1)
            normalise(0)
            with ve_.Fori(0, B - 2) as b:
                ch.enter(b, LM_DVE)
                turn(b, True, True)
                ch.leave(B - 2, "landmarks dve")
            turn(B - 2, True, False)
            turn(B - 1, False, False)


STREAMS = 4
PI_GP = 5 * STREAMS
PI_V = ITERS + 1


def pseudo_inverse(nc, c, sb, sem):
    peak = sb("peak", [P, 2])
    peak_all = sb("peak_all", [P, 2])
    inv_c = sb("inv_c", [P, 2])
    start = sb("start", [P, STREAMS, 3, EV])
    ev = sb("ev", [P, STREAMS, 3, EV])
    q = sb("q", [P, STREAMS, 3, EV])
    r = sb("r", [P, STREAMS, 3, EV])
    w = sb("w", [P, STREAMS, 3, D])
    x2 = sb("x2_in", [P, STREAMS, 3, HW])
    streams = range(STREAMS)
    peaks, peaked, scaled, prep = sem("pi_peaks"), sem("pi_peaked"), sem("pi_scaled"), sem("pi_prep")
    cleared = sem("pi_cleared")
    p1, p2, q_in, r_in, e_in, v_in = ([sem(f"pi_{n}_{s}") for s in streams] for n in ("p1", "p2", "q_in", "r_in", "e_in", "v_in"))
    a = [c.psum[:, 2 * s, 0:3 * EV].rearrange("p (k w) -> p k w", k=3) for s in streams]
    bb = [c.psum[:, 2 * s + 1, 0:3 * EV].rearrange("p (k w) -> p k w", k=3) for s in streams]
    turns = B // 2

    x2_in = sem("pi_x2_in")

    with nc.Block() as block:
        @block.sync
        def _(sp):
            give(sp, [*p1, *r_in, *v_in], [])
            with sp.Fori(0, turns) as i:
                for s in streams:
                    sp.wait_ge(p1[s], ONE + i * PI_V)
                    g = s % 2
                    src = c.x_dram[bass.ds(i * 2 + s // 2, 1), :, 3 * g:3 * g + 3, :].rearrange("b p k m -> (b p) k m")
                    sp.dma_start(x2[:, s], src).then_inc(x2_in, 16)

        @block.gpsimd
        def _(gp):
            ch = Chain(gp, prep)
            nc.gpsimd.memset(start[:], 0.0).then_inc(cleared, 1)
            nc.gpsimd.memset(ev[:], 0.0).then_inc(cleared, 1)
            gp.wait_ge(peaks, 2)
            nc.gpsimd.partition_all_reduce(peak_all[:], peak[:], channels=P, reduce_op=RMAX).then_inc(peaked, 1)
            gp.wait_ge(scaled, 2)
            gp.wait_ge(cleared, 2)

            with gp.Fori(0, turns) as i:
                ch.enter(i, PI_GP)
                for s in streams:
                    gp.wait_ge(r_in[s], ONE + i * ITERS)
                    g = s % 2
                    bx = bass.ds(i * 2 + s // 2, 1)
                    for half in range(2):
                        r0 = M * half
                        src = c.E[r0:r0 + M, bx, 3 * g:3 * g + 3, :].rearrange("p b k m -> p (b k) m")
                        ch.link(nc.gpsimd.tensor_tensor(start[r0:r0 + M, s, :, r0:r0 + M], src,
                                                        inv_c[r0:r0 + M, 1:2].unsqueeze(2).to_broadcast([M, 3, M]), ALU.mult))
                    src = c.V[:, bx, 3 * g:3 * g + 3, :].rearrange("p b k d -> p (b k) d")
                    ch.link(nc.gpsimd.tensor_copy(start[:, s, :, HW:EV], src))
                    for half in range(2):
                        r0 = M * half
                        at = start[r0:r0 + M, s, :, r0:r0 + M]
                        one = c.ident[r0:r0 + M, r0:r0 + M].unsqueeze(1).to_broadcast([M, 3, M])
                        ch.link(nc.gpsimd.tensor_tensor(at, at, one, ALU.add))
                ch.leave(turns, "pseudo-inverse pool")

        @block.tensor
        def _(te):
            te.wait_ge(cleared, 2)

            def turn(i):
                for k in range(ITERS):
                    for s in streams:
                        if k == 0:
                            te.wait_ge(prep, i * PI_GP + 5 * (s + 1))
                        te.wait_ge(v_in[s], ONE + i * PI_V + k)
                        x = start if k == 0 else ev
                        for p in range(3):
                            last = nc.tensor.matmul(a[s][:, p, :], x[:, s, p, 0:HW], x[:, s, p, :], start=True, stop=True)
                        last.then_inc(p1[s], 1)
                    for s in streams:
                        te.wait_ge(r_in[s], ONE + i * ITERS + (k + 1))
                        lo = 0 if k < ITERS - 1 else HW
                        for p in range(3):
                            last = nc.tensor.matmul(bb[s][:, p, lo:EV], q[:, s, p, 0:HW], r[:, s, p, lo:EV], start=True, stop=True)
                        last.then_inc(p2[s], 1)
                te.wait_ge(x2_in, i * (16 * STREAMS) + 16 * STREAMS)
                for s in streams:
                    te.wait_ge(v_in[s], ONE + i * PI_V + ITERS)
                    for p in range(3):
                        last = nc.tensor.matmul(a[s][:, p, HW:EV], x2[:, s, p, :], ev[:, s, p, HW:EV], start=True, stop=True)
                    last.then_inc(p1[s], 1)
            with te.Fori(0, turns) as i:
                turn(i)

        @block.scalar
        def _(sc):
            def turn(i):
                for k in range(ITERS):
                    for s in streams:
                        sc.wait_ge(p1[s], ONE + i * PI_V + (k + 1))
                        nc.scalar.activation(q[:, s], a[s], ACT.Copy).then_inc(q_in[s], 1)
                    if k < ITERS - 1:
                        for s in streams:
                            sc.wait_ge(p2[s], i * ITERS + (k + 1))
                            nc.scalar.activation(ev[:, s, :, 0:HW], bb[s][:, :, 0:HW], ACT.Copy, scale=0.25).then_inc(e_in[s], 1)
            with sc.Fori(0, turns) as i:
                turn(i)

        @block.vector
        def _(ve):
            nc.vector.tensor_reduce(peak[:, 0:1], c.rows[:].rearrange("p b k -> p (b k)"), AX.X, ALU.max).then_inc(peaks, 1)
            nc.vector.tensor_reduce(peak[:, 1:2], c.cols[:].rearrange("p b k -> p (b k)"), AX.X, ALU.max).then_inc(peaks, 1)
            ve.wait_ge(peaked, 1)
            nc.vector.tensor_tensor(peak[:, 0:1], peak_all[:, 0:1], peak_all[:, 1:2], ALU.mult).then_inc(peaks, 1)
            ve.wait_ge(peaks, 3)
            nc.vector.reciprocal(inv_c[:, 0:1], peak[:, 0:1]).then_inc(scaled, 1)
            ve.wait_ge(scaled, 1)
            nc.vector.tensor_scalar(inv_c[:, 1:2], inv_c[:, 0:1], -1.0, None, ALU.mult).then_inc(scaled, 1)

            def turn(i):
                for k in range(ITERS):
                    x = start if k == 0 else ev
                    for s in streams:
                        ve.wait_ge(q_in[s], i * ITERS + (k + 1))
                        ve.wait_ge(v_in[s], ONE + i * PI_V + k)
                        nc.vector.tensor_tensor(w[:, s], x[:, s, :, HW:EV], q[:, s, :, HW:EV], ALU.add)
                        nc.vector.scalar_tensor_tensor(r[:, s, :, HW:EV], x[:, s, :, HW:EV], 4.0, q[:, s, :, HW:EV], ALU.mult, ALU.add)
                        nc.vector.scalar_tensor_tensor(r[:, s, :, 0:HW], x[:, s, :, 0:HW], 3.0, q[:, s, :, 0:HW], ALU.mult, ALU.add
                                                       ).then_inc(r_in[s], 1)
                    for s in streams:
                        ve.wait_ge(p2[s], i * ITERS + (k + 1))
                        if k < ITERS - 1:
                            ve.wait_ge(e_in[s], i * (ITERS - 1) + (k + 1))
                        dst = ev[:, s, :, HW:EV]
                        ve.wait_ge(r_in[s], ONE + i * ITERS + (k + 1))
                        nc.vector.scalar_tensor_tensor(dst, bb[s][:, :, HW:EV], 0.25, w[:, s], ALU.mult, ALU.add).then_inc(v_in[s], 1)
                for s in streams:
                    g = s % 2
                    dst = c.V[:, bass.ds(i * 2 + s // 2, 1), 3 * g:3 * g + 3, :].rearrange("p b k d -> p (b k) d")
                    ve.wait_ge(p1[s], ONE + i * PI_V + PI_V)
                    nc.vector.tensor_scalar(dst, a[s][:, :, HW:EV], inv_c[:, 0:1], None, ALU.mult).then_inc(v_in[s], 1)
            with ve.Fori(0, turns) as i:
                turn(i)


AT_FRONT = [(f"scores{k}", f"S{k % 2}") if q == 0 else (f"probs{k}", "T") for k in range(TT + 1) for q in range(2)]
AT_FRONT += [("outA", "T"), ("out_img", "I"), ("outB", "O")]
AT_TAIL = [("proj0", "R1"), ("proj1", "R0"), ("proj2", "R1")]
AT_TAIL += [(f"xnT{k}", f"R{k % 2}") for k in range(TT + 1)]
AT_TAIL += [("lgT", "R0"), ("lgT_img", "R1"), ("rt", "R0"), ("rt_img", "R1"), ("xs", "R0"), ("xsT", "R0"), ("eCT", "R1")]
AT_DVE, AT_GP = 37, 3
TILES = TT + 1


def attention(nc, c, sb, sem):
    qb = sb("qb", [P, 2, N])
    kl = sb("kl", [P, 12, M])
    zb = sb("zb", [P, PAIRS, 2 * D])
    e1 = sb("e1", [P, 3, NH * M])
    p1T = sb("p1T", [P, PAIRS, N])
    neg = sb("neg", [P, 2, NH])
    den = sb("den", [P, 2, S])
    rden_img = sb("rden_img", [P, 2 * NI])
    oA = sb("oA", [P, N])
    oB = sb("oB", [M + 1, N])
    stats, mv = sb("stats", [P, TILES, 6]), sb("mv", [P, TILES, 2])
    v192, t1, rn = sb("v192", [P, TILES]), sb("t1", [P, TILES]), sb("rn", [P, TILES])
    shift = sb("shift", [P, TILES])
    hw = sb("hw", [P, TILES, H])
    xn = sb("xn", [P, TILES, H])
    xnT = sb("xnT", [K2, 2, N])
    rT = sb("rT", [P, N])
    rt = sb("rt", [P, TILES, 2 * NE])
    dstat = sb("dstat", [P, 4])
    eC = sb("eC", [P, TILES, NE])
    negC = sb("negC", [P, TILES])
    sumC = sb("sumC", [P, TILES])
    xs = sb("xs", [P, H])
    CT = sb("CT", [NE, N])
    F_ = Slots(sem, "at", AT_FRONT)
    R_ = Slots(sem, "at", AT_TAIL)
    banks = {"S0": 0, "I": 0, "S1": 2, "O": 2, "T": 4, "R0": 6, "R1": 7}
    ps = c.psum

    def two(product):
        b0 = banks[F_.at[product][0]]
        return ps[:, b0:b0 + 2, :].rearrange("p k n -> p (k n)")

    def one(product):
        return ps[:, banks[R_.at[product][0]], :]

    q_in, kl_in, zb_in, cleared = sem("at_q_in"), sem("at_kl_in"), sem("at_zb_in"), sem("at_cleared")
    shifted, exp_in = sem("at_shifted"), sem("at_exp_in")
    h_in, den_in, ln_in = sem("at_h_in"), sem("at_den_in"), sem("at_ln_in")
    normed, xn_in = sem("at_normed"), sem("at_xn_in")
    d_shift, eD_in, c_shift, eC_in, d_scale = (sem("at_" + n) for n in ("d_shift", "eD_in", "c_shift", "eC_in", "d_scale"))
    dve_done, gp_done, c_stored = sem("at_dve"), sem("at_gp"), sem("at_c_stored")

    chunks = [(0, NI)] + [(NI + P * k, P) for k in range(TT)]
    tiles = [(P, NI + P * k) for k in range(TT)] + [(NI, 0)]

    with nc.Block() as block:
        @block.sync
        def _(sp):
            give(sp, [shifted, h_in], [c_stored], F_, R_)
            def load(b):
                sp.wait_ge(F_.full("scores4"), ONE + b * F_.uses["S0"])
                sp.dma_start(qb[:], c.q_dram[bass.ds(b, 1)].rearrange("b p k n -> (b p) k n")).then_inc(q_in, 16)

            def store(b):
                R_.wait_free(sp, "eCT", b)
                R_.wait_free(sp, "xsT", b)
                sp.dma_start(c.c_dram[bass.ds(b, 1)].rearrange("b n t -> (b n) t"), CT[:]).then_inc(c_stored, 16)
            load(0)
            load(1)
            with sp.Fori(0, B - 2) as b:
                load(b + 2)
                store(b)
            store(B - 2)
            store(B - 1)
            sp.wait_ge(c_stored, DMA + 16 * B)

        @block.gpsimd
        def _(gp):
            ch = Chain(gp, gp_done)
            for k, (tile, value) in enumerate(((zb[:], 0.0), (mv[:], 0.0), (e1[:], 0.0), (xn[:, TT, :], 0.0), (xs[:], 0.0), (oB[M:M + 1, :], 1.0), (c.xsT[:], 0.0),
                                               (c.xsT[K2:K2 + 1, 0:1], 1.0), (c.rsum[:], 1.0))):
                nc.gpsimd.memset(tile, value).then_inc(cleared, 1)
                gp.wait_ge(cleared, k + 1)

            def keys(b):
                gp.wait_ge(F_.full("scores4"), ONE + b * F_.uses["S0"])
                ch.link(nc.gpsimd.tensor_tensor(kl[:, 0:8, :], c.mask, c.landk[:, bass.ds(b, 1), 1, :].to_broadcast([P, 8, M]), ALU.mult))
                nc.gpsimd.tensor_tensor(kl[:, 8:12, :], c.mask[:, 0:4, :], c.landk[:, bass.ds(b, 1), 0, :].to_broadcast([P, 4, M]), ALU.mult
                                        ).then_inc(kl_in, 1)
                gp.wait_ge(kl_in, b + 1)

            def values(b):
                gp.wait_ge(F_.full("outB"), ONE + b)
                for half in range(2):
                    r0 = M * half
                    src = c.V[r0:r0 + M, bass.ds(b, 1), :, :].rearrange("p b k d -> p (b k) d")
                    ins = nc.gpsimd.tensor_copy(zb[r0:r0 + M, :, D * half:D * half + D], src)
                    if half:
                        ins.then_inc(zb_in, 1)
                        gp.wait_ge(zb_in, b + 1)
                    else:
                        ch.link(ins)

            def residual(b):
                R_.wait_free(gp, "proj1", b)
                R_.wait_free(gp, "proj2", b)
                ch.link(nc.gpsimd.tensor_copy(c.h[:, bass.ds(b * TT, TT), :], hw[:, 0:TT, :]))
                nc.gpsimd.tensor_copy(c.h_img[:, bass.ds(b, 1), :], hw[0:NI, TT:TILES, :]).then_inc(h_in, 1)
                gp.wait_ge(h_in, b + 1)
            keys(0)
            values(0)
            keys(1)
            with gp.Fori(0, B - 2) as b:
                ch.enter(b, AT_GP)
                values(b + 1)
                residual(b)
                keys(b + 2)
                ch.leave(B - 2, "attention pool")
            values(B - 1)
            residual(B - 2)
            residual(B - 1)

        @block.tensor
        def _(te):
            te.wait_ge(cleared, 9)

            def scores(k, b):
                c0, n = chunks[k]
                if k == 1:
                    te.wait_ge(F_.free("outB"), ONE + b)
                if k == 0:
                    te.wait_ge(q_in, b * 16 + 16)
                    te.wait_ge(kl_in, b + 1)
                    te.wait_ge(F_.free("out_img"), ONE + b)
                te.wait_ge(shifted, ONE + b * TILES + max(k - 1, 0))
                out = two(f"scores{k}")
                klf = kl[:].rearrange("p h m -> p (h m)")
                nc.tensor.matmul(out[0:n, 0:512], qb[:, 0, c0:c0 + n], klf[:, 0:512], start=True, stop=True)
                nc.tensor.matmul(out[0:n, 512:768], qb[:, 1, c0:c0 + n], klf[:, 512:768], start=True, stop=True
                                 ).then_inc(F_.full(f"scores{k}"), 1)

            def probs(k, b):
                c0, n = chunks[k]
                te.wait_ge(exp_in, b * TILES + (k + 1))
                F_.claim(te, f"probs{k}", b)
                out = two(f"probs{k}")
                for p in range(PAIRS):
                    last = nc.tensor.transpose(out[:, P * p:P * p + P], e1[:, k % 3, HW * p:HW * p + HW], c.ident)
                last.then_inc(F_.full(f"probs{k}"), 1)

            def out(g, b):
                product = ("outA", "outB")[g]
                if g == 0:
                    te.wait_ge(zb_in, b + 1)
                    F_.claim(te, product, b)
                else:
                    te.wait_ge(shifted, ONE + b * TILES + TILES)
                for q in range(2):
                    for p in range(4 * g, min(4 * g + 4, PAIRS)):
                        j = p % 4
                        lhsT = c.ones_bd if q else zb[:, p, :]
                        last = nc.tensor.matmul(two(product)[32 * j:32 * j + 32, 512 * q:512 * q + S], lhsT,
                                                p1T[:, p, NI:N], start=True, stop=True)
                last.then_inc(F_.full(product), 1)

            def out_img(b):
                te.wait_ge(shifted, ONE + b * TILES + TILES)
                for p in range(PAIRS):
                    j = p % 4
                    for q in range(2):
                        c0 = 2 * NI * (p // 4) + NI * q
                        last = nc.tensor.matmul(two("out_img")[32 * j:32 * j + 32, c0:c0 + NI], c.ones_bd if q else zb[:, p, :],
                                                p1T[:, p, 0:NI], start=True, stop=True)
                last.then_inc(F_.full("out_img"), 1)

            def tail0(b):
                for product in ("outA", "out_img", "outB"):
                    F_.wait_free(te, product, b)
                for k in (4, 0, 1, 2, 3):
                    n, c0 = tiles[k]
                    product = "proj0" if k == 4 else f"proj{1 + k // 2}"
                    lo = H * (k % 2) if k < 4 else 0
                    if k in (4, 0, 2):
                        R_.claim(te, product, b)
                    nc.tensor.matmul(one(product)[0:n, lo:lo + H], oA[:, c0:c0 + n], c.wprojT[:, 0, :], start=True, stop=False)
                    last = nc.tensor.matmul(one(product)[0:n, lo:lo + H], oB[:, c0:c0 + n], c.wprojT[0:M + 1, 1, :],
                                            start=False, stop=True)
                    if k in (4, 1, 3):
                        last.then_inc(R_.full(product), 1)

            def tail1(b):
                te.wait_ge(xn_in, b + 1)
                for k, (n, c0) in enumerate(tiles):
                    R_.claim(te, f"xnT{k}", b)
                    for e in range(2):
                        last = nc.tensor.transpose(one(f"xnT{k}")[0:K2, P * e:P * e + P], xn[:, k, K2 * e:K2 * e + K2], c.ident)
                    last.then_inc(R_.full(f"xnT{k}"), 1)

            def tail2(b):
                R_.wait_free(te, "xnT3", b)
                R_.wait_free(te, "xnT4", b)
                for product, c0, n in (("lgT", NI, S), ("lgT_img", 0, NI)):
                    R_.claim(te, product, b)
                    for e in range(2):
                        last = nc.tensor.matmul(one(product)[:, 0:n], c.phin[:, e, :], xnT[:, e, c0:c0 + n], start=(e == 0), stop=(e == 1))
                    last.then_inc(R_.full(product), 1)

            def tail3(b):
                te.wait_ge(eD_in, b + 1)
                R_.claim(te, "rt", b)
                R_.claim(te, "rt_img", b)
                for k in range(TT):
                    last = nc.tensor.transpose(one("rt")[:, P * k:P * k + P], rT[:, NI + P * k:NI + P * k + P], c.ident)
                last.then_inc(R_.full("rt"), 1)
                nc.tensor.transpose(one("rt_img")[0:NI, 0:P], rT[:, 0:NI], c.ident).then_inc(R_.full("rt_img"), 1)

            def tail4(b):
                R_.wait_free(te, "rt", b)
                R_.wait_free(te, "rt_img", b)
                R_.claim(te, "xs", b)
                for k, (n, c0) in enumerate(tiles):
                    last = nc.tensor.matmul(one("xs")[NE:P, 0:H], rt[0:n, k, NE:P], xn[0:n, k, :], start=(k == 0), stop=(k == TT))
                last.then_inc(R_.full("xs"), 1)

            def tail5(b):
                R_.wait_free(te, "xs", b)
                R_.claim(te, "xsT", b)
                R_.claim(te, "eCT", b)
                te.wait_ge(eC_in, b + 1)
                for e in range(2):
                    nc.tensor.transpose(one("xsT")[0:K2, P * e:P * e + P], xs[:, e:H:2], c.ident)
                nc.tensor.transpose(one("xsT")[0:NE, 2 * P:2 * P + NI], eC[0:NI, TT, :], c.ident[0:NI, 0:NI]).then_inc(R_.full("xsT"), 1)
                for k in range(TT):
                    last = nc.tensor.transpose(one("eCT")[0:NE, P * k:P * k + P], eC[:, k, :], c.ident)
                last.then_inc(R_.full("eCT"), 1)

            def turn(b, front, tail):
                if front:
                    scores(0, b + 1)
                    scores(1, b + 1)
                if tail:
                    tail0(b)
                if front:
                    probs(0, b + 1)
                    scores(2, b + 1)
                    probs(1, b + 1)
                    scores(3, b + 1)
                    probs(2, b + 1)
                    scores(4, b + 1)
                    probs(3, b + 1)
                if tail:
                    tail1(b)
                    tail2(b)
                if front:
                    probs(4, b + 1)
                if tail:
                    tail3(b)
                if front:
                    out(0, b + 1)
                if tail:
                    tail4(b)
                if front:
                    out_img(b + 1)
                    out(1, b + 1)
                if tail:
                    tail5(b)
            turn(-1, True, False)
            with te.Fori(0, B - 1) as b:
                turn(b, True, True)
            turn(B - 1, False, True)

        @block.scalar
        def _(sc):
            def copy(dst, src, scale=1.0):
                return nc.scalar.activation(dst, src, ACT.Copy, scale=scale)

            def exps(k, b):
                n = chunks[k][1]
                sc.wait_ge(shifted, ONE + b * TILES + (k + 1))
                nc.scalar.activation(e1[0:n, k % 3, :], e1[0:n, k % 3, :], ACT.Exp).then_inc(exp_in, 1)

            def evac(k, b):
                c0, n = chunks[k]
                F_.wait_full(sc, f"probs{k}", b)
                src = two(f"probs{k}").rearrange("p (k n) -> p k n", n=P)
                copy(p1T[:, 0:4, c0:c0 + n], src[:, 0:4, 0:n])
                copy(p1T[:, 4:6, c0:c0 + n], src[:, 4:6, 0:n]).then_inc(F_.free(f"probs{k}"), 1)

            def tail0(b):
                sc.wait_ge(normed, b + 1)
                for k, (n, c0) in enumerate(tiles):
                    ins = nc.scalar.activation(xn[0:n, k, :], hw[0:n, k, :], ACT.Identity, bias=shift[0:n, k:k + 1], scale=rn[0:n, k:k + 1])
                ins.then_inc(xn_in, 1)

            def tail1(b):
                for k, (n, c0) in enumerate(tiles):
                    R_.wait_full(sc, f"xnT{k}", b)
                    ins = copy(xnT[:, :, c0:c0 + n], one(f"xnT{k}")[0:K2, 0:2 * P].rearrange("p (e n) -> p e n", e=2)[:, :, 0:n])
                    ins.then_inc(R_.free(f"xnT{k}"), 1)

            def tail2(b):
                for product, c0, n in (("lgT", NI, S), ("lgT_img", 0, NI)):
                    R_.wait_full(sc, product, b)
                    copy(rT[:, c0:c0 + n], one(product)[:, 0:n]).then_inc(R_.free(product), 1)

            def tail3(b):
                sc.wait_ge(d_shift, b + 1)
                nc.scalar.activation(rT[NE:P], rT[NE:P], ACT.Exp, bias=dstat[NE:P, 0:1], accum_out=dstat[NE:P, 1:2]).then_inc(eD_in, 1)
                R_.wait_full(sc, "rt", b)
                copy(rt[:, 0:TT, :], one("rt").rearrange("p (k n) -> p k n", n=P)).then_inc(R_.free("rt"), 1)
                R_.wait_full(sc, "rt_img", b)
                copy(rt[0:NI, TT, :], one("rt_img")[0:NI, 0:P]).then_inc(R_.free("rt_img"), 1)

            def tail4(b):
                sc.wait_ge(c_shift, b + 1)
                nc.scalar.activation(eC[:, 0:TT, :], eC[:, 0:TT, :], ACT.Exp)
                nc.scalar.activation(eC[0:NI, TT, :], eC[0:NI, TT, :], ACT.Exp).then_inc(eC_in, 1)
                R_.wait_full(sc, "xs", b)
                sc.wait_ge(d_scale, b + 1)
                copy(xs[NE:P], one("xs")[NE:P, 0:H], dstat[NE:P, 2:3]).then_inc(R_.free("xs"), 1)

            def tail5(b):
                R_.wait_full(sc, "eCT", b)
                sc.wait_ge(c_stored, DMA + b * 16)
                copy(CT[:, NI:N], one("eCT")[0:NE, 0:S]).then_inc(R_.free("eCT"), 1)

            def out(g, b):
                product, n = (("outA", P), ("outB", M))[g]
                F_.wait_full(sc, product, b)
                nc.scalar.activation(den[0:n, g, :], two(product)[0:n, 512:512 + S], ACT.Ln).then_inc(ln_in, 1)
                sc.wait_ge(ln_in, 2 * b + (g + 1))
                nc.scalar.activation(den[0:n, g, :], den[0:n, g, :], ACT.Exp, scale=-1.0).then_inc(den_in, 1)

            def turn(b, front_, tail):
                if front_:
                    exps(0, b + 1)
                    exps(1, b + 1)
                    evac(0, b + 1)
                    evac(1, b + 1)
                    exps(2, b + 1)
                    evac(2, b + 1)
                    exps(3, b + 1)
                    evac(3, b + 1)
                if tail:
                    tail0(b)
                if front_:
                    exps(4, b + 1)
                if tail:
                    tail1(b)
                    tail2(b)
                if front_:
                    evac(4, b + 1)
                if tail:
                    tail3(b)
                if front_:
                    out(0, b + 1)
                if tail:
                    tail4(b)
                if front_:
                    out(1, b + 1)
                if tail:
                    tail5(b)
            turn(-1, True, False)
            with sc.Fori(0, B - 1) as b:
                turn(b, True, True)
            turn(B - 1, False, True)

        @block.vector
        def _(ve):
            ch = Chain(ve, dve_done)
            ve.wait_ge(cleared, 9)

            def front(k, b):
                c0, n = chunks[k]
                F_.wait_full(ve, f"scores{k}", b)
                src = two(f"scores{k}")[0:n, 0:NH * M].rearrange("p (h m) -> p h m", m=M)
                ve.wait_ge(shifted, ONE + b * TILES + max(k - 1, 0))
                ch.link(nc.vector.tensor_reduce(neg[0:n, k % 2, :], src, AX.X, ALU.max, negate=True))
                if k >= 3:
                    F_.wait_full(ve, f"probs{k - 3}", b)
                nc.vector.tensor_tensor(e1[0:n, k % 3, :].rearrange("p (h m) -> p h m", m=M), src,
                                        neg[0:n, k % 2, :].unsqueeze(2).to_broadcast([n, NH, M]), ALU.add).then_inc(shifted, 1)

            def out(g, b):
                product, o, n = (("outA", oA, P), ("outB", oB, M))[g]
                ve.wait_ge(den_in, 2 * b + (g + 1))
                nc.vector.tensor_tensor(o[0:n, NI:N], two(product)[0:n, 0:S], den[0:n, g, :], ALU.mult).then_inc(F_.free(product), 1)

            def out_img(b):
                F_.wait_full(ve, "out_img", b)
                for g, (o, n) in enumerate(((oA, P), (oB, M))):
                    ch(nc.vector.reciprocal(rden_img[0:n, NI * g:NI * g + NI], two("out_img")[0:n, 2 * NI * g + NI:2 * NI * g + 2 * NI]))
                ch.wait()
                for g, (o, n) in enumerate(((oA, P), (oB, M))):
                    ins = nc.vector.tensor_tensor(o[0:n, 0:NI], two("out_img")[0:n, 2 * NI * g:2 * NI * g + NI],
                                                  rden_img[0:n, NI * g:NI * g + NI], ALU.mult)
                ins.then_inc(F_.free("out_img"), 1)

            def tail0(b):
                R_.wait_full(ve, "proj0", b)
                h = c.h_img[:, bass.ds(b, 1), :].rearrange("p a h -> p (a h)")
                ve.wait_ge(h_in, ONE + b)
                nc.vector.tensor_tensor(hw[0:NI, TT, :], one("proj0")[0:NI, 0:H], h, ALU.add).then_inc(R_.free("proj0"), 1)
                for j in range(2):
                    R_.wait_full(ve, f"proj{1 + j}", b)
                    h = c.h[:, bass.ds(b * TT + 2 * j, 2), :]
                    nc.vector.tensor_tensor(hw[:, 2 * j:2 * j + 2, :], one(f"proj{1 + j}")[:, 0:2 * H].rearrange("p (a h) -> p a h", h=H), h, ALU.add
                                            ).then_inc(R_.free(f"proj{1 + j}"), 1)

            def statistics(b):
                R_.wait_free(ve, "proj1", b)
                R_.wait_free(ve, "proj2", b)
                for k in range(TT):
                    ch(nc.vector.bn_stats(stats[:, k, :], hw[:, k, :]))
                ch(nc.vector.bn_stats(stats[0:NI, TT, :], hw[0:NI, TT, :]))
                ch.wait()
                nc.vector.tensor_copy(t1[:, 0:1], stats[:, 0, 0:1])
                for k in range(TILES):
                    n = tiles[k][0]
                    ch(nc.vector.bn_aggr(mv[0:n, k, :], stats[0:n, k, :]))
                ch.wait()

            def norms(b):
                ch.link(nc.vector.tensor_scalar(t1[:], mv[:, :, 1], 1e-24, 1e-29, ALU.mult, ALU.add))
                ch.link(nc.vector.scalar_tensor_tensor(v192[:], mv[:, :, 1], float(H), t1[:], ALU.mult, ALU.max))
                rsqrt(nc, ch, rn[:], t1[:], v192[:])
                nc.vector.scalar_tensor_tensor(shift[:], mv[:, :, 0], -1.0, rn[:], ALU.mult, ALU.mult).then_inc(normed, 1)

            def tail2(b):
                R_.wait_free(ve, "lgT", b)
                R_.wait_free(ve, "lgT_img", b)
                nc.vector.tensor_reduce(dstat[:, 0:1], rT[:], AX.X, ALU.max, negate=True).then_inc(d_shift, 1)

            def tail3(b):
                R_.wait_free(ve, "rt", b)
                R_.wait_free(ve, "rt_img", b)
                nc.vector.reciprocal(dstat[NE:P, 2:3], dstat[NE:P, 1:2]).then_inc(d_scale, 1)
                ch(nc.vector.tensor_reduce(negC[:, 0:TT], rt[:, 0:TT, 0:NE], AX.X, ALU.max, negate=True))
                ch.link(nc.vector.tensor_reduce(negC[0:NI, TT:TILES], rt[0:NI, TT:TILES, 0:NE], AX.X, ALU.max, negate=True))
                nc.vector.tensor_tensor(eC[:, 0:TT, :], rt[:, 0:TT, 0:NE], negC[:, 0:TT].unsqueeze(2).to_broadcast([P, TT, NE]), ALU.add)
                nc.vector.tensor_tensor(eC[0:NI, TT:TILES, :], rt[0:NI, TT:TILES, 0:NE],
                                        negC[0:NI, TT:TILES].unsqueeze(2).to_broadcast([NI, 1, NE]), ALU.add).then_inc(c_shift, 1)

            def tail4(b):
                ve.wait_ge(eC_in, b + 1)
                ch(nc.vector.tensor_reduce(sumC[:, 0:TT], eC[:, 0:TT, :], AX.X, ALU.add))
                ch.link(nc.vector.tensor_reduce(sumC[0:NI, TT:TILES], eC[0:NI, TT:TILES, :], AX.X, ALU.add))
                at = c.rsum[:, bass.ds(b, 1), :].rearrange("p b k -> p (b k)")
                ch(nc.vector.reciprocal(at[:, 0:TT], sumC[:, 0:TT]))
                ch(nc.vector.reciprocal(at[0:NI, TT:TILES], sumC[0:NI, TT:TILES]))

            def tail5(b):
                R_.wait_full(ve, "xsT", b)
                ve.wait_ge(c_stored, DMA + b * 16)
                ch(nc.vector.tensor_copy(CT[:, 0:NI], one("xsT")[0:NE, 2 * P:2 * P + NI]))
                src = one("xsT")[0:K2, 0:2 * P].rearrange("p (e n) -> p e n", e=2)[:, :, NE:P]
                nc.vector.tensor_copy(c.xsT[0:K2, :, :, bass.ds(b, 1)].rearrange("p e n b -> p e (n b)"), src).then_inc(R_.free("xsT"), 1)

            def turn(b, front_, tail):
                if front_:
                    front(0, b + 1)
                    front(1, b + 1)
                if tail:
                    tail0(b)
                if front_:
                    front(2, b + 1)
                if tail:
                    statistics(b)
                if front_:
                    front(3, b + 1)
                if tail:
                    norms(b)
                if front_:
                    front(4, b + 1)
                if tail:
                    tail2(b)
                    tail3(b)
                if front_:
                    out(0, b + 1)
                    out_img(b + 1)
                    out(1, b + 1)
                if tail:
                    tail4(b)
                    tail5(b)
            turn(-1, True, False)
            with ve.Fori(0, B - 1) as b:
                ch.enter(b, AT_DVE)
                turn(b, True, True)
                ch.leave(B - 1, "attention dve")
            turn(B - 1, False, True)


G = 4
GROUPS = NE // G
R32 = 2 * B


def experts(nc, c, t, sb, sem):
    w1 = sb("w1", [K2 + 1, 2, G, 2, F])
    w2 = sb("w2", [P, 2, G, FC, H])
    xg = sb("xg", [K2 + 1, 2, 2, G, R32])
    hs = sb("hs", [P, 2, F])
    hT = sb("hT", [P, 2, FC, P])
    ys = sb("ys", [P, 2, H])
    names = ("w1_in", "w2_in", "xg_in", "first", "gelu", "turned", "turned_in", "second", "ys_in", "ys_out")
    w1_in, w2_in, xg_in, first, gelu, turned, turned_in, second, ys_in, ys_out = ([sem(f"ex_{n}_{u}") for u in range(2)] for n in names)
    ps = c.psum
    hid = [ps[:, 2 * u:2 * u + 2, :].rearrange("p k n -> p (k n)") for u in range(2)]
    flip = ps[:, 4:6, :].rearrange("p k n -> p (k n)")
    turns = GROUPS // 2

    with nc.Block() as block:
        @block.sync
        def _(sp):
            give(sp, [*first, *second, *gelu, *turned_in, *ys_in], [*ys_out])
            def load(i, u):
                e0 = i * (2 * G) + G * u
                sp.wait_ge(first[u], ONE + i)
                sp.dma_start(w1[0:K2, u], t["L0_ffn_w1"][bass.ds(e0, G)].rearrange("n (p t) h -> p n t h", t=2)).then_inc(w1_in[u], 16)
                sp.dma_start(w1[K2:K2 + 1, u, :, 0, :], t["L0_ffn_b1"][bass.ds(e0, G)].rearrange("(a n) h -> a n h", a=1)
                             ).then_inc(w1_in[u], 16)
                sp.wait_ge(second[u], ONE + i)
                sp.dma_start(w2[:, u], t["L0_ffn_w2"][bass.ds(e0, G)].rearrange("n (p c) d -> p n c d", c=FC)).then_inc(w2_in[u], 16)

            def store(i, u):
                sp.wait_ge(ys_in[u], ONE + i + 1)
                for j in range(G):
                    sp.dma_start(c.y_dram[bass.ds(i * (2 * G) + (G * u + j), 1)].rearrange("n b d -> (n b) d"),
                                 ys[R32 * j:R32 * j + B, u, :]).then_inc(ys_out[u], 16)
            load(0, 0)
            load(0, 1)
            with sp.Fori(0, turns - 1) as i:
                for u in range(2):
                    load(i + 1, u)
                    store(i, u)
            for u in range(2):
                store(turns - 1, u)
            for u in range(2):
                sp.wait_ge(ys_out[u], DMA + 16 * G * turns)

        @block.gpsimd
        def _(gp):
            with gp.Fori(0, turns) as i:
                for u in range(2):
                    gp.wait_ge(first[u], ONE + i)
                    nc.gpsimd.tensor_copy(xg[:, u], c.xsT[:, :, bass.ds(i * (2 * G) + G * u, G), :]).then_inc(xg_in[u], 1)
                    gp.wait_ge(xg_in[u], i + 1)

        @block.tensor
        def _(te):
            def layer1(i, u):
                te.wait_ge(w1_in[u], i * 32 + 32)
                te.wait_ge(xg_in[u], i + 1)
                te.wait_ge(gelu[u], ONE + i)
                for c0, n in ((0, 512), (512, F - 512)):
                    for k in range(2):
                        rows = K2 + 1 - k
                        for j in range(G):
                            last = nc.tensor.matmul(hid[u][R32 * j:R32 * j + R32, c0:c0 + n], xg[0:rows, u, k, j, :],
                                                    w1[0:rows, u, j, k, c0:c0 + n], start=(k == 0), stop=(k == 1))
                last.then_inc(first[u], 1)

            def layer2(i, u):
                te.wait_ge(gelu[u], ONE + i + 1)
                if u:
                    te.wait_ge(turned_in[0], ONE + i + 1)
                else:
                    te.wait_ge(turned_in[1], ONE + i)
                for f in range(FC):
                    last = nc.tensor.transpose(flip[:, P * f:P * f + P], hs[:, u, f:F:FC], c.ident)
                last.then_inc(turned[u], 1)
                te.wait_ge(turned_in[u], ONE + i + 1)
                te.wait_ge(w2_in[u], i * 16 + 16)
                te.wait_ge(ys_in[u], ONE + i)
                for f in range(FC):
                    for j in range(G):
                        last = nc.tensor.matmul(ps[R32 * j:R32 * j + R32, 6 + u, 0:H], hT[:, u, f, R32 * j:R32 * j + R32],
                                                w2[:, u, j, f, :], start=(f == 0), stop=(f == FC - 1))
                last.then_inc(second[u], 1)
            with te.Fori(0, turns) as i:
                layer1(i, 0)
                layer1(i, 1)
                layer2(i, 0)
                layer2(i, 1)

        @block.scalar
        def _(sc):
            with sc.Fori(0, turns) as i:
                for u in range(2):
                    sc.wait_ge(first[u], ONE + i + 1)
                    nc.scalar.activation(hs[:, u, :], hid[u][:, 0:F], ACT.Gelu).then_inc(gelu[u], 1)

        @block.vector
        def _(ve):
            with ve.Fori(0, turns) as i:
                for u in range(2):
                    ve.wait_ge(turned[u], i + 1)
                    nc.vector.tensor_copy(hT[:, u].rearrange("p c n -> p (c n)"), flip[:, 0:F]).then_inc(turned_in[u], 1)
                    ve.wait_ge(second[u], ONE + i + 1)
                    ve.wait_ge(ys_out[u], DMA + i * (16 * G))
                    nc.vector.tensor_copy(ys[:, u, :], ps[:, 6 + u, 0:H]).then_inc(ys_in[u], 1)


def combine(nc, c, t, sb, sem):
    Y = sb("Y", [NE, B, H])
    b2 = sb("b2", [NE, H])
    CT = sb("CT", [NE, 2, N])
    yb = sb("yb", [NE, 2, H])
    y_in, b2_in, y_ready = sem("co_y_in"), sem("co_b2_in"), sem("co_y_ready")
    c_in, yb_in = ([sem(f"co_{n}_{u}") for u in range(2)] for n in ("c_in", "yb_in"))
    full, added, stored = sem("co_full"), sem("co_added"), sem("co_stored")
    parts = ((0, 2), (2, 4), (4, 5))
    tiles = [(P, NI + P * k) for k in range(TT)] + [(NI, 0)]
    ps = c.psum

    def bank(u, j):
        return ps[:, 3 * u + j, :]
    turns = B // 2

    with nc.Block() as block:
        @block.sync
        def _(sp):
            give(sp, [full, added], [])
            sp.dma_start(Y[:], c.y_dram).then_inc(y_in, 16)
            sp.dma_start(b2[:], t["L0_ffn_b2"]).then_inc(b2_in, 16)
            with sp.Fori(0, turns) as i:
                for u in range(2):
                    sp.wait_ge(full, ONE + i * 6)
                    sp.dma_start(CT[:, u], c.c_dram[bass.ds(i * 2 + u, 1)].rearrange("b n t -> (b n) t")).then_inc(c_in[u], 16)

        @block.scalar
        def _(sc):
            sc.wait_ge(y_ready, 1)
            with sc.Fori(0, turns) as i:
                for u in range(2):
                    sc.wait_ge(full, ONE + i * 6)
                    nc.scalar.activation(yb[:, u, :], Y[:, bass.ds(i * 2 + u, 1), :].rearrange("p b h -> p (b h)"), ACT.Copy
                                         ).then_inc(yb_in[u], 1)

        @block.gpsimd
        def _(gp):
            with gp.Fori(0, B) as b:
                gp.wait_ge(added, ONE + b * 5 + 4)
                dst = t["out"][bass.ds(b, 1), NI:N, :].rearrange("b (k p) h -> p (b k) h", p=P)
                gp.dma_start(dst, c.h[:, bass.ds(b * TT, TT), :]).then_inc(stored, 16)
                gp.wait_ge(added, ONE + b * 5 + 5)
                gp.dma_start(t["out"][bass.ds(b, 1), 0:NI, :].rearrange("b p h -> (b p) h"),
                             c.h_img[:, bass.ds(b, 1), :].rearrange("p b h -> p (b h)")).then_inc(stored, 16)
            gp.wait_ge(stored, 32 * B)

        @block.tensor
        def _(te):
            with te.Fori(0, turns) as i:
                for u in range(2):
                    te.wait_ge(c_in[u], i * 16 + 16)
                    te.wait_ge(yb_in[u], i + 1)
                    for j, (k0, k1) in enumerate(parts):
                        if j == 0:
                            te.wait_ge(added, ONE + i * 10)
                        for k in range(k0, k1):
                            n, c0 = tiles[k]
                            last = nc.tensor.matmul(bank(u, j)[0:n, H * (k - k0):H * (k - k0) + H], CT[:, u, c0:c0 + n], yb[:, u, :],
                                                    start=True, stop=True)
                        last.then_inc(full, 1)

        @block.vector
        def _(ve):
            ve.wait_ge(y_in, 16)
            ve.wait_ge(b2_in, 16)
            nc.vector.tensor_tensor(Y[:], Y[:], b2[:].unsqueeze(1).to_broadcast([NE, B, H]), ALU.add).then_inc(y_ready, 1)
            with ve.Fori(0, turns) as i:
                for u in range(2):
                    b = i * 2 + u
                    for j, (k0, k1) in enumerate(parts):
                        ve.wait_ge(full, ONE + i * 6 + (3 * u + j + 1))
                        for k in range(k0, k1):
                            n = tiles[k][0]
                            h = (c.h[:, bass.ds(i * (2 * TT) + (TT * u + k), 1), :] if k < TT else c.h_img[:, bass.ds(b, 1), :]
                                 ).rearrange("p a h -> p (a h)")
                            scale = c.rsum[0:n, bass.ds(b, 1), k:k + 1].rearrange("p a k -> p (a k)")
                            nc.vector.scalar_tensor_tensor(h, bank(u, j)[0:n, H * (k - k0):H * (k - k0) + H], scale, h,
                                                           ALU.mult, ALU.add).then_inc(added, 1)


INPUTS = ["x", "x_txt", "itok_BS_0_15", "itok_BS_0_3", "itok_BS_0_9999", "itok_BS_0_2047", "fside_BS_age_tau", "fside_BS_delays_tau",
          "L0_tok_W", "L0_tok_b", "L0_txt_word_table", "L0_txt_modalities_table", "L0_txt_seg_table", "L0_txt_npi_table",
          "L0_txt_posi_table", "L0_txt_age_w", "L0_txt_age_b", "L0_txt_age_w0", "L0_txt_age_b0", "L0_txt_delay_w", "L0_txt_delay_b",
          "L0_txt_delay_w0", "L0_txt_delay_b0", "L0_txt_ln_gamma", "L0_txt_ln_beta", "L0_attn_w_qkv", "L0_attn_w_proj",
          "L0_attn_b_proj", "L0_ffn_phi", "L0_ffn_scale", "L0_ffn_w1", "L0_ffn_b1", "L0_ffn_w2", "L0_ffn_b2"]


def kernel(**inputs):
    import concourse.bacc as bacc
    from concourse.bass_utils import run_bass_kernel_spmd

    nc = bacc.Bacc("TRN2", target_bir_lowering=False, num_devices=1)
    arrays = {f"in_{name}": np.ascontiguousarray(inputs[name]) for name in INPUTS}
    arrays["in_const"] = constants()
    t = {name[3:]: nc.dram_tensor(name, a.shape, mybir.dt.from_np(a.dtype), kind="ExternalInput").ap() for name, a in arrays.items()}
    t["out"] = nc.dram_tensor("out", (B, N, H), F32, kind="ExternalOutput").ap()
    build(nc, t)
    result = run_bass_kernel_spmd(nc, [arrays], core_ids=[0])
    return result.results[0]["out"]
```

```python
from contextlib import ExitStack

import numpy as np

import concourse.bass as bass
from concourse import mybir

F32 = mybir.dt.float32
I32 = mybir.dt.int32
U32 = mybir.dt.uint32
ALU = mybir.AluOpType
ACT = mybir.ActivationFunctionType
AX = mybir.AxisListType
RMAX = bass.bass_isa.ReduceOp.max

P = 128
B, S, H = 16, 512, 192
NI = 16
N = S + NI
M = 64
PAD = (M - N % M) % M
NP = N + PAD
L = NP // M
NH, D = 12, H // 12
PAIRS = NH // 2
TT = S // P
NT = B * TT
K2 = H // 2
HW = 2 * M
EV = HW + D
ITERS = 6
NE, F = 64, 768
FC = F // P
TWO_PI = 2.0 * np.pi
MAGIC = 1.5 * 2.0 ** 23
SEED = float(0x5F3759DF)
VOCAB, NPI, POS, MODAL, SEG = 8000, 2500, 512, 16, 4


def constants():
    ident = np.eye(P, dtype=np.float32)
    mask = np.zeros((P, 8, M), np.float32)
    for r in range(P):
        mask[r, r // D] = D ** -0.5
    ones_bd = np.zeros((P, 2, D), np.float32)
    ones_bd[:M, 0] = 1.0
    ones_bd[M:, 1] = 1.0
    pick = np.zeros((P, MODAL * SEG), np.float32)
    for m in range(MODAL):
        for s in range(SEG):
            pick[m, SEG * m + s] = 1.0
            pick[MODAL + s, SEG * m + s] = 1.0
    return np.concatenate([ident, mask.reshape(P, -1), ones_bd.reshape(P, -1), pick], axis=1)


C_ID, C_MASK, C_ONES, C_PICK, C_ALL = 0, P, P + 8 * M, P + 8 * M + 2 * D, P + 8 * M + 2 * D + M


class Chain:

    def __init__(self, eng, sem):
        self.eng, self.sem, self.base, self.n = eng, sem, 0, 0

    def __call__(self, ins):
        ins.then_inc(self.sem, 1)
        self.n += 1

    def wait(self, back=0):
        self.eng.wait_ge(self.sem, self.base + (self.n - back))

    def link(self, ins):
        self(ins)
        self.wait()

    def enter(self, i, per):
        self.start, self.per = self.base + self.n, per
        self.base, self.n = self.start + i * per, 0

    def leave(self, turns, what):
        assert self.n == self.per, f"{what}: {self.n} in a turn, {self.per} given"
        self.base, self.n = self.start + self.per * turns, 0


ONE, DMA = 1, 16


def give(eng, ones, transfers, *slots):
    for s in ones + [s for x in slots for s in (*x.full_sem.values(), *x.free_sem.values())]:
        eng.sem_inc(s, ONE)
    for s in transfers:
        eng.sem_inc(s, DMA)


class Slots:

    def __init__(self, sem, name, products):
        self.uses, self.at = {}, {}
        for product, slot in products:
            self.at[product] = (slot, self.uses.get(slot, 0))
            self.uses[slot] = self.uses.get(slot, 0) + 1
        self.full_sem = {s: sem(f"{name}_{s}_full") for s in self.uses}
        self.free_sem = {s: sem(f"{name}_{s}_free") for s in self.uses}

    def turn(self, product, i):
        slot, k = self.at[product]
        return i * self.uses[slot] + k

    def claim(self, eng, product, i):
        eng.wait_ge(self.free_sem[self.at[product][0]], ONE + self.turn(product, i))

    def full(self, product):
        return self.full_sem[self.at[product][0]]

    def free(self, product):
        return self.free_sem[self.at[product][0]]

    def wait_full(self, eng, product, i):
        eng.wait_ge(self.full(product), ONE + self.turn(product, i) + 1)

    def wait_free(self, eng, product, i):
        eng.wait_ge(self.free(product), ONE + self.turn(product, i) + 1)


def spread(ap, parts):
    return bass.AP(tensor=ap.tensor, offset=ap.offset, ap=[[0, parts]] + [list(x) for x in ap.ap])


RSQRT_STEPS = 11


def rsqrt_step(nc, ch, y, t, v, j):
    if j:
        ch.wait()
    if j == 0:
        ch(nc.vector.tensor_scalar(t.bitcast(I32), v.bitcast(I32), 1, None, ALU.logical_shift_right))
    elif j == 1:
        ch(nc.vector.tensor_scalar(y.bitcast(I32), t.bitcast(I32), -1.0, SEED, ALU.mult, ALU.add))
    elif j % 3 == 2:
        ch(nc.vector.tensor_tensor(t, y, y, ALU.mult))
    elif j % 3 == 0:
        ch(nc.vector.scalar_tensor_tensor(t, t, -0.5, v, ALU.mult, ALU.mult))
    else:
        ch(nc.vector.scalar_tensor_tensor(y, t, 1.5, y, ALU.add, ALU.mult))


def rsqrt(nc, ch, y, t, v):
    for j in range(RSQRT_STEPS):
        rsqrt_step(nc, ch, y, t, v, j)
    ch.wait()


G = 4
R32 = 2 * B


class Core:
    pass


def build(nc, t):
    with ExitStack() as ctx:
        def sb(name, shape, dt=F32, where=ctx):
            return where.enter_context(nc.sbuf_tensor(name, shape, dt))

        def sem(name):
            return ctx.enter_context(nc.semaphore(name))

        c = Core()
        c.psum = ctx.enter_context(nc.psum_tensor("psum", [P, 8, 512], F32))
        c.const = sb("const", [P, C_ALL])
        c.ident = c.const[:, C_ID:C_ID + P]
        c.mask = c.const[:, C_MASK:C_MASK + 8 * M].rearrange("p (h m) -> p h m", m=M)
        c.ones_bd = c.const[:, C_ONES:C_ONES + 2 * D]
        c.h = sb("h", [P, NT, H])
        c.h_img = sb("h_img", [NI, B, H])
        c.rsum = sb("rsum", [P, B, TT + 1])
        c.late_room = sb("late_room", [P, 2 * NE * 2 * B])
        c.xsT = c.late_room[0:K2 + 1, :].rearrange("p (k n b) -> p k n b", k=2, n=NE)
        c.V = sb("V", [P, B, PAIRS, D])
        c.landk = sb("landk", [P, B, 2, M])
        c.wprojT = sb("wprojT", [P, 2, H])
        c.phin = sb("phin", [K2, 2, 2 * NE])
        c.q_dram = nc.dram_tensor("q_rows", (B, P, 2, N), F32, kind="Internal").ap()
        c.c_dram = nc.dram_tensor("router_rows", (B, NE, N), F32, kind="Internal").ap()
        c.y_dram = nc.dram_tensor("expert_rows", (NE, B, H), F32, kind="Internal").ap()
        c.x_dram = nc.dram_tensor("attn2_rows", (B, P, PAIRS, HW), F32, kind="Internal").ap()
        c.pair_dram = nc.dram_tensor("modal_seg_table", (MODAL * SEG, H), F32, kind="Internal").ap()
        with ExitStack() as three:
            c.E = sb("E", [P, B, PAIRS, M], where=three)
            c.rows = sb("rows", [P, B, PAIRS], where=three)
            c.cols = sb("cols", [P, B, PAIRS], where=three)
            with ExitStack() as two:
                used = 0

                def early(parts, *shape):
                    nonlocal used
                    size = int(np.prod(shape))
                    a = c.late_room[0:parts, used:used + size]
                    used += size
                    return a.rearrange("p (a b) -> p a b", b=shape[1]) if len(shape) == 2 else a
                c.wT = early(K2, 2, 640)
                c.turns_w = early(P, 2, H)
                c.turns_b = early(P, 2, H)
                c.gamma = early(P, H)
                c.beta = early(P, H)
                c.tau = early(P, 2, NT)
                c.linear = early(P, NT)
                c.hnT_img = early(K2, 2, B * NI)
                c.idx = sb("idx", [P, 4, NT], U32, where=two)
                c.idx_b = sb("idx_b", [P, 4, TT], U32, where=two)
                c.got = sb("got", [P, TT, 4, H], where=two)
                c.gathered = sem("gathered")
                with ExitStack() as work:
                    setup(nc, c, t, lambda n, s, d=F32: sb(n, s, d, work), sem)
                with ExitStack() as work:
                    landmarks(nc, c, t, lambda n, s, d=F32: sb("lm_" + n, s, d, work), sem)
            with ExitStack() as work:
                pseudo_inverse(nc, c, lambda n, s, d=F32: sb("pi_" + n, s, d, work), sem)
        names = ("w1_in", "w2_in", "first", "second")
        c.w1_in, c.w2_in, c.first, c.second = ([sem(f"ex_{n}_{u}") for u in range(2)] for n in names)
        c.w1 = [sb("ex_w1_0", [K2 + 1, G, 2, F])]
        c.w2 = [sb("ex_w2_0", [P, G, FC, H])]
        with ExitStack() as work:
            attention(nc, c, t, lambda n, s, d=F32: sb("at_" + n, s, d, work), sem)
        c.w1.append(sb("ex_w1_1", [K2 + 1, G, 2, F]))
        c.w2.append(sb("ex_w2_1", [P, G, FC, H]))
        with ExitStack() as work:
            experts(nc, c, t, lambda n, s, d=F32: sb("ex_" + n, s, d, work), sem)
        with ExitStack() as work:
            combine(nc, c, t, lambda n, s, d=F32: sb("co_" + n, s, d, work), sem)


def gather_rows(gp, c, t):
    for k in range(TT):
        for r, table in enumerate(("L0_txt_word_table", "L0_txt_npi_table", "L0_txt_posi_table", None)):
            gp.indirect_dma_start(out=c.got[:, k, r, :], out_offset=None, in_=t[table] if table else c.pair_dram,
                                  in_offset=bass.IndirectOffsetOnAxis(ap=c.idx_b[:, r, k:k + 1], axis=0)
                                  ).then_inc(c.gathered, 16)


def setup(nc, c, t, sb, sem):
    tokw = sb("tokw", [K2, 2, F])
    wq = sb("wq", [K2, 6, H])
    wp = sb("wp", [K2, 2, H])
    phi = sb("phi", [K2, 2, NE])
    phi_sq = sb("phi_sq", [K2, 2, NE])
    tokwT = sb("tokwT", [P, 6, H])
    room = c.h[:].rearrange("p k h -> p (k h)")
    img = room[0:3 * B, 0:4096]
    regrouped = room[0:3 * B, 4096:8192].rearrange("p (i j r q) -> p i j r q", i=4, j=4, r=16)
    patches = sb("patches", [P, 16, 2, 3 * B])
    tok_b = sb("tok_b", [NI, H])
    ids = sb("ids", [NT, 5, P], I32)
    idf = sb("idf", [NT, 5, P])
    below = sb("below", [NT, 5, P])
    taus = sb("taus", [NT, 2, P])
    tables = sb("tables", [MODAL + SEG, H])
    pair_rows = sb("pair_rows", [MODAL * SEG, H])
    lin_w = sb("lin_w", [P, 4])
    scale = sb("scale", [P, 1])
    ones = sb("ones", [P, P])
    tmp = sb("tmp", [P, NE])
    tmp2 = sb("tmp2", [P, NE])
    stats = sb("stats_i", [NI, B, 6])
    mv = sb("mv_i", [NI, B, 2])
    rstd = sb("rstd_i", [NI, B])
    hn_img = sb("hn_img", [NI, B, H])
    weights_in = sem("setup_weights_in")
    loaded, pairs_stored, first_idx = sem("setup_loaded"), sem("setup_pairs_stored"), sem("setup_first_idx")
    pe, dve, act = sem("setup_pe"), sem("setup_dve"), sem("setup_act")
    regroup = sem("setup_regrouped")
    zeroed, stored = sem("setup_zeroed"), sem("setup_stored")
    ps = c.psum

    with nc.Block() as block:
        @block.sync
        def _(sp):
            def load(dst, src):
                sp.dma_start(dst, src).then_inc(loaded, 16)
            for dst, src in ((c.const[:], t["const"]), (tokw[:], t["L0_tok_W"].rearrange("(k p) f -> p k f", k=2)),
                             (wq[:], t["L0_attn_w_qkv"].rearrange("(k p) f -> p k f", k=6)),
                             (wp[:], t["L0_attn_w_proj"].rearrange("(k p) f -> p k f", k=2))):
                sp.dma_start(dst, src).then_inc(weights_in, 16)
            load(phi[:], t["L0_ffn_phi"].rearrange("(k p) n o -> p k (n o)", k=2))
            load(img, t["x"].rearrange("b c h w -> (b c) (h w)"))
            load(tok_b[:], spread(t["L0_tok_b"], NI))
            load(scale[:], spread(t["L0_ffn_scale"], P))
            load(c.gamma[:], spread(t["L0_txt_ln_gamma"], P))
            load(c.beta[:], spread(t["L0_txt_ln_beta"], P))
            sp.wait_ge(zeroed, 3)
            for k, name in enumerate(("age", "delay")):
                load(c.turns_w[:, k, 0:H - 1], spread(t[f"L0_txt_{name}_w"][0], P))
                load(c.turns_b[:, k, 0:H - 1], spread(t[f"L0_txt_{name}_b"], P))
            sp.wait_ge(dve, SETUP_DVE["pair_rows"])
            sp.dma_start(c.pair_dram, pair_rows[:]).then_inc(pairs_stored, 16)
            sp.wait_ge(dve, SETUP_DVE["proj"])
            sp.dma_start(c.wprojT[M:M + 1, 1, :], t["L0_attn_b_proj"].rearrange("(a h) -> a h", a=1)).then_inc(stored, 16)
            sp.wait_ge(stored, 16)

        @block.gpsimd
        def _(gp):
            nc.gpsimd.memset(c.turns_w[:], 0.0).then_inc(zeroed, 1)
            nc.gpsimd.memset(c.turns_b[:], 0.0).then_inc(zeroed, 1)
            nc.gpsimd.memset(ones[:], 1.0).then_inc(zeroed, 1)
            gp.wait_ge(dve, SETUP_DVE["pair_rows"])
            nc.gpsimd.tensor_copy(c.idx_b[:], c.idx[:, :, 0:TT]).then_inc(first_idx, 1)
            gp.wait_ge(first_idx, 1)
            gp.wait_ge(pairs_stored, 16)
            gather_rows(gp, c, t)

        @block.tensor
        def _(te):
            te.wait_ge(weights_in, 16 * 4)
            for k in range(6):
                ch, half = k // 2, k % 2
                if k >= 2:
                    te.wait_ge(dve, k - 1)
                for e in range(2):
                    src = tokw[:, e, 384 * half + ch:384 * half + 384:3]
                    last = nc.tensor.transpose(ps[:, k % 2, K2 * e:K2 * e + K2], src, c.ident[0:K2, 0:K2])
                last.then_inc(pe, 1)
            for k in range(6):
                te.wait_ge(dve, 5 + k)
                for e in range(2):
                    last = nc.tensor.transpose(ps[0:K2, k % 2, K2 * e:K2 * e + K2], wq[:, k, K2 * e:K2 * e + K2],
                                               c.ident[0:K2, 0:K2])
                last.then_inc(pe, 1)
            te.wait_ge(dve, SETUP_DVE["qkv"])
            for e in range(2):
                nc.tensor.transpose(ps[:, 0, K2 * e:K2 * e + K2], wp[:, e, 0:P], c.ident[0:K2, 0:K2])
                last = nc.tensor.transpose(ps[0:M, 1, K2 * e:K2 * e + K2], wp[:, e, P:H], c.ident[0:K2, 0:K2])
            last.then_inc(pe, 1)
            te.wait_ge(dve, SETUP_DVE["proj"])
            te.wait_ge(dve, SETUP_DVE["ids"])
            for k in range(4):
                nc.tensor.transpose(ps[:, 2, M * k:M * k + M], idf[:, k, :], c.ident[0:NT, 0:NT])
            for k in range(2):
                last = nc.tensor.transpose(ps[:, 3, M * k:M * k + M], taus[:, k, :], c.ident[0:NT, 0:NT])
            last.then_inc(pe, 1)
            nc.tensor.matmul(ps[0:MODAL * SEG, 4, 0:H], c.const[0:MODAL + SEG, C_PICK:C_PICK + M], tables[:],
                             start=True, stop=True).then_inc(pe, 1)
            te.wait_ge(dve, SETUP_DVE["phi_sq"])
            te.wait_ge(zeroed, 3)
            for k in range(2):
                last = nc.tensor.matmul(ps[:, 5, 0:NE], ones[0:K2, :], phi_sq[:, k, :], start=(k == 0), stop=(k == 1))
            last.then_inc(pe, 1)
            for i in range(4):
                te.wait_ge(regroup, i + 1)
                for j in range(4):
                    g = 4 * i + j
                    if g >= 2:
                        te.wait_ge(act, g - 1)
                    for half in range(2):
                        src = regrouped[:, i, j, 8 * half:8 * half + 8, :].rearrange("p r q -> p (r q)")
                        last = nc.tensor.transpose(ps[:, 6 + g % 2, 48 * half:48 * half + 48], src, c.ident[0:48, 0:48])
                    last.then_inc(pe, 1)
            te.wait_ge(act, 16)
            for g in range(4):
                if g >= 2:
                    te.wait_ge(dve, SETUP_DVE["embed"] + 4 * (g - 1))
                for k in range(6):
                    ch, half = k // 2, k % 2
                    for j in range(4):
                        b = 4 * g + j
                        last = nc.tensor.matmul(ps[32 * j:32 * j + NI, g % 2, 0:H], patches[:, :, half, 3 * b + ch],
                                                tokwT[:, k, :], start=(k == 0), stop=(k == 5))
                last.then_inc(pe, 1)
            te.wait_ge(dve, SETUP_DVE["hn_img"])
            for b in range(B):
                for k in range(2):
                    last = nc.tensor.transpose(ps[0:K2, 2, 256 * k + NI * b:256 * k + NI * b + NI],
                                               hn_img[:, b, K2 * k:K2 * k + K2], c.ident[0:NI, 0:NI])
            last.then_inc(pe, 1)

        @block.scalar
        def _(sc):
            def load(dst, src):
                sc.dma_start(dst, src).then_inc(loaded, 16)
            for k, name in enumerate(("x_txt", "itok_BS_0_9999", "itok_BS_0_2047", "itok_BS_0_15", "itok_BS_0_3")):
                load(ids[:, k, :], t[name].rearrange("b (t p) -> (b t) p", p=P))
            for k, name in enumerate(("fside_BS_age_tau", "fside_BS_delays_tau")):
                load(taus[:, k, :], t[name].rearrange("b (t p) -> (b t) p", p=P))
            load(tables[0:MODAL, :], t["L0_txt_modalities_table"])
            load(tables[MODAL:MODAL + SEG, :], t["L0_txt_seg_table"])
            for k, name in enumerate(("age", "delay")):
                load(lin_w[:, k:k + 1], spread(t[f"L0_txt_{name}_w0"][0], P))
                load(lin_w[:, 2 + k:3 + k], spread(t[f"L0_txt_{name}_b0"], P))
            sc.wait_ge(loaded, LOADED)
            for i in range(4):
                src = img[:, 1024 * i:1024 * i + 1024].rearrange("p (r j q) -> p j r q", r=16, j=4)
                nc.scalar.activation(regrouped[:, i], src, ACT.Copy).then_inc(regroup, 1)
            for g in range(16):
                sc.wait_ge(pe, 17 + g)
                nc.scalar.activation(patches[:, g, :, :].rearrange("p h f -> p (h f)"), ps[:, 6 + g % 2, 0:96],
                                     ACT.Copy).then_inc(act, 1)
            sc.wait_ge(pe, 37)
            nc.scalar.activation(c.hnT_img[:], ps[0:K2, 2, 0:512].rearrange("p (k n) -> p k n", k=2),
                                 ACT.Copy).then_inc(act, 1)

        @block.vector
        def _(v):
            ch = Chain(v, dve)

            def mark(name):
                assert ch.n == SETUP_DVE[name], (name, ch.n)
            for k in range(6):
                v.wait_ge(pe, k + 1)
                ch(nc.vector.tensor_copy(tokwT[:, k, :], ps[:, k % 2, 0:H]))
            for k in range(6):
                v.wait_ge(pe, 7 + k)
                part, lo = k // 2, 96 * (k % 2)
                runs = []
                if part == 0:
                    runs = [(lo, lo + 96, 0)] + ([(128, 192, 128)] if lo else [])
                elif part == 1:
                    runs = [(0, 96, 320)] if lo == 0 else [(96, 128, 320), (128, 192, 64)]
                else:
                    runs = [(lo, lo + 96, 448)]
                for r0, r1, off in runs:
                    src = ps[0:K2, k % 2, 0:H].rearrange("p (e r) -> p e r", e=2)[:, :, r0 - lo:r1 - lo]
                    dst = c.wT[:, :, r0 + off:r1 + off]
                    ins = nc.vector.tensor_copy(dst, src)
                ch(ins)
            mark("qkv")
            v.wait_ge(pe, 13)
            ch(nc.vector.tensor_copy(c.wprojT[:, 0, :], ps[:, 0, 0:H]))
            ch(nc.vector.tensor_copy(c.wprojT[0:M, 1, :], ps[0:M, 1, 0:H]))
            mark("proj")
            v.wait_ge(loaded, LOADED)
            for k, size in enumerate((VOCAB, NPI, POS, MODAL, SEG)):
                ch(nc.vector.tensor_scalar(below[:, k, :], ids[:, k, :], 0.0, float(size), ALU.is_lt, ALU.mult))
            for k in range(5):
                ch.wait(4)
                ch(nc.vector.tensor_tensor(idf[:, k, :], ids[:, k, :], below[:, k, :], ALU.add))
            for k, size in enumerate((VOCAB, NPI, POS, MODAL, SEG)):
                ch.wait(4)
                ch(nc.vector.tensor_scalar(idf[:, k, :], idf[:, k, :], 0.0, float(size - 1), ALU.max, ALU.min))
            ch.wait()
            ch.link(nc.vector.scalar_tensor_tensor(idf[:, 3, :], idf[:, 3, :], float(SEG), idf[:, 4, :], ALU.mult, ALU.add))
            mark("ids")
            ch.link(nc.vector.tensor_tensor(phi_sq[:], phi[:], phi[:], ALU.mult))
            mark("phi_sq")
            v.wait_ge(pe, 14)
            ch(nc.vector.tensor_copy(c.idx[:], ps[:, 2, 0:4 * NT].rearrange("p (k n) -> p k n", k=4)))
            ch.link(nc.vector.tensor_copy(c.tau[:], ps[:, 3, 0:2 * NT].rearrange("p (k n) -> p k n", k=2)))
            v.wait_ge(pe, 15)
            ch(nc.vector.tensor_copy(pair_rows[:], ps[0:MODAL * SEG, 4, 0:H]))
            mark("pair_rows")
            ch.link(nc.vector.tensor_scalar(c.linear[:], c.tau[:, 0, :], lin_w[:, 0:1], lin_w[:, 2:3], ALU.mult, ALU.add))
            ch.link(nc.vector.scalar_tensor_tensor(c.linear[:], c.tau[:, 1, :], lin_w[:, 1:2], c.linear[:], ALU.mult, ALU.add))
            ch.link(nc.vector.tensor_scalar(c.linear[:], c.linear[:], lin_w[:, 3:4], None, ALU.add))
            ch(nc.vector.tensor_scalar(c.turns_w[:], c.turns_w[:], 1.0 / TWO_PI, None, ALU.mult))
            ch(nc.vector.tensor_scalar(c.turns_b[:], c.turns_b[:], 1.0 / TWO_PI, None, ALU.mult))
            v.wait_ge(pe, 16)
            ch.link(nc.vector.tensor_scalar(tmp2[:], ps[:, 5, 0:NE], 1e-24, None, ALU.max))
            y = sb("phi_rn", [P, NE])
            rsqrt(nc, ch, y[:], tmp[:], tmp2[:])
            ch.link(nc.vector.tensor_scalar(y[:], y[:], scale[:, 0:1], None, ALU.mult))
            for k in range(2):
                for j in range(2):
                    ch(nc.vector.tensor_tensor(c.phin[:, k, NE * j:NE * j + NE], phi[:, k, :], y[0:K2, :], ALU.mult))
            mark("embed")
            rt, ve = sb("rt_i", [NI, B]), sb("ve_i", [NI, B])

            def group_stats(g):
                for b in range(4 * g, 4 * g + 4):
                    ch(nc.vector.bn_stats(stats[:, b, :], c.h_img[:, b, :]))
            for g in range(4):
                v.wait_ge(pe, 33 + g)
                for j in range(4):
                    ch(nc.vector.tensor_tensor(c.h_img[:, 4 * g + j, :], ps[32 * j:32 * j + NI, g % 2, 0:H], tok_b[:], ALU.add))
                if g:
                    ch.wait(4)
                    group_stats(g - 1)
            ch.wait()
            group_stats(3)
            from_stats(nc, ch, stats, mv, rt, ve, B, 1e-5)
            rsqrt(nc, ch, rstd[:], rt[:], ve[:])
            for k in range(B):
                ch(nc.vector.tensor_scalar(hn_img[:, k, :], c.h_img[:, k, :], mv[:, k, 0:1], rstd[:, k:k + 1], ALU.subtract, ALU.mult))
            mark("hn_img")


LOADED = 16 * 23
SETUP_DVE = dict(qkv=12, proj=14, ids=30, phi_sq=31, pair_rows=34, embed=56, hn_img=132)


def variances(nc, ch, src, stats, mv, rt, ve, n, eps):
    for k in range(n):
        ch(nc.vector.bn_stats(stats[:, k, :], src[:, k, :]))
    from_stats(nc, ch, stats, mv, rt, ve, n, eps)


def from_stats(nc, ch, stats, mv, rt, ve, n, eps):
    ch.wait()
    nc.vector.tensor_copy(rt[:, 0:1], stats[:, 0, 0:1])
    for k in range(n):
        ch(nc.vector.bn_aggr(mv[:, k, :], stats[:, k, :]))
    ch.wait()
    ch.link(nc.vector.tensor_scalar(ve[:, 0:n], mv[:, 0:n, 1], eps, None, ALU.add))


def moments(nc, ch, src, stats, mv, rstd, rt, ve, n, eps):
    variances(nc, ch, src, stats, mv, rt, ve, n, eps)
    rsqrt(nc, ch, rstd[:, 0:n], rt[:, 0:n], ve[:, 0:n])


HALF = NP // 2
LM_ATTN2 = {1: "xT0", 2: "xT1", 4: "x0", 5: "x1"}
LM_PRODUCTS = [("hnT0", "A0"), ("hnT1", "A1"), ("hnT2", "A2"), ("hnT3", "A3"),
               ("k2a", "A0"), ("k2b", "A1"), ("land", "A2"), ("q1a", "A3"), ("q1b", "A0"), ("q0a", "A1"), ("q0b", "A2"),
               ("v01", "A0"), ("v23", "A1"), ("v4", "A2"), ("sim2", "A3")]
for _p in range(PAIRS):
    LM_PRODUCTS += [(f"sim3_{_p}", f"S{_p % 2}"), (f"p3T_{_p}", "A1" if _p % 2 else "A3"), (f"p3I_{_p}", "A2")]
    if _p in LM_ATTN2:
        LM_PRODUCTS.append((LM_ATTN2[_p], "A0"))
LM_PRODUCTS += [("u", "A0"), ("uT", "A1")]
LM_DVE = 65


def landmarks(nc, c, t, sb, sem):
    emb = sb("emb", [P, TT, H])
    turns = sb("turns", [P, TT, 2, H])
    whole = sb("whole", [P, TT, 2, H])
    hm = sb("hm", [P, TT, H])
    hn = sb("hn", [P, TT, H])
    hnT = sb("hnT", [K2, 2, NP])
    hnl = sb("hnl", [K2, 2, M])
    q0 = sb("q0", [P, 2, N])
    k1 = sb("k1", [P, NP])
    k2 = sb("k2", [P, NP])
    v = sb("v", [P, TT + 1, H])
    land = sb("land", [P, 4, M])
    ql = sb("ql", [P, 12, M])
    w2 = sb("w2", [P, PAIRS, M])
    small = sb("small", [P, 6, PAIRS])
    x2 = sb("x2", [P, PAIRS, HW])
    x2T = sb("x2T", [P, PAIRS, HW])
    p3 = sb("p3", [P, 3, NP])
    p3T = sb("p3T", [P, TT + 1, PAIRS, HW])
    u = sb("u", [P, 2, HW])
    stats, mv = sb("stats", [P, TT, 6]), sb("mv", [P, TT, 2])
    rstd, rt, ve = sb("rstd", [P, TT]), sb("rt", [P, TT]), sb("ve", [P, TT])
    nshift = sb("nshift", [P, TT])
    S = Slots(sem, "lm", LM_PRODUCTS)
    slot = {"A0": 0, "A1": 1, "A2": 2, "A3": 3, "S0": 4, "S1": 6}

    def bank(product):
        return slot[S.at[product][0]]
    cleared = sem("lm_cleared")
    summed, paired, emb_in = sem("lm_summed"), sem("lm_paired"), sem("lm_emb_in")
    turned, rounded, reduced, sined = sem("lm_turned"), sem("lm_rounded"), sem("lm_reduced"), sem("lm_sined")
    hn_ready, img_in, moments_in = sem("lm_hn_ready"), sem("lm_img_in"), sem("lm_moments_in")
    embedded, kept, halfway = sem("lm_embedded"), sem("lm_kept"), sem("lm_halfway")
    hnl_ready, ql_ready = sem("lm_hnl_ready"), sem("lm_ql_ready")
    sub2, exp2, x2_ready, max3, exp3 = sem("lm_sub2"), sem("lm_exp2"), sem("lm_x2_ready"), sem("lm_max3"), sem("lm_exp3")
    x2_stored = sem("lm_x2_stored")
    q_stored = sem("lm_q_stored")
    dve_done, gp_done = sem("lm_dve"), sem("lm_gp")
    ps = c.psum

    with nc.Block() as block:
        @block.gpsimd
        def _(gp):
            spare = sb("spare", [P, 1])

            def gathers(b):
                nc.gpsimd.tensor_copy(c.idx_b[:], c.idx[:, :, bass.ds(b * TT, TT)]).then_inc(gp_done, 1)
                gp.wait_ge(gp_done, b)
                nc.gpsimd.tensor_tensor(spare[:], c.const[:, 0:1], c.const[:, 0:1], ALU.add)
                gather_rows(gp, c, t)

            def sum_rows(b):
                gp.wait_ge(c.gathered, b * (16 * 4 * TT) + 16 * 4 * TT)
                nc.gpsimd.tensor_tensor(c.got[:, :, 0:2, :], c.got[:, :, 0:2, :], c.got[:, :, 2:4, :], ALU.add).then_inc(paired, 1)
                gp.wait_ge(paired, b + 1)
                gp.wait_ge(summed, ONE + b)
                nc.gpsimd.tensor_tensor(emb[:], c.got[:, :, 0, :], c.got[:, :, 1, :], ALU.add).then_inc(halfway, 1)
                gp.wait_ge(sined, b + 1)
                gp.wait_ge(halfway, 2 * b + 1)
                nc.gpsimd.tensor_tensor(emb[:], emb[:], whole[:, :, 0, :], ALU.add).then_inc(halfway, 1)
                gp.wait_ge(halfway, 2 * b + 2)
                nc.gpsimd.tensor_tensor(emb[:], emb[:], whole[:, :, 1, :], ALU.add).then_inc(emb_in, 1)
                gp.wait_ge(emb_in, ONE + b + 1)
            with gp.Fori(0, B - 1) as b:
                sum_rows(b)
                gathers(b + 1)
            sum_rows(B - 1)

        @block.sync
        def _(sp):
            give(sp, [emb_in, summed, exp3, kept], [q_stored, x2_stored], S)
            def store(b):
                S.wait_free(sp, "q0b", b)
                S.wait_free(sp, "q1b", b)
                S.wait_free(sp, "q0a", b)
                sp.dma_start(c.q_dram[b], q0[:]).then_inc(q_stored, 16)
                sp.wait_ge(x2_ready, b + 1)
                sp.dma_start(c.x_dram[b], x2[:]).then_inc(x2_stored, 16)
            with sp.Fori(0, B) as b:
                store(b)
            sp.wait_ge(q_stored, DMA + 16 * B)
            sp.wait_ge(x2_stored, DMA + 16 * B)

        @block.tensor
        def _(te):
            te.wait_ge(cleared, 3)

            def turn(b):
                te.wait_ge(hn_ready, b + 1)
                for k in range(TT):
                    S.claim(te, f"hnT{k}", b)
                    for e in range(2):
                        last = nc.tensor.transpose(ps[0:K2, bank(f"hnT{k}"), P * e:P * e + P],
                                                   hn[:, k, K2 * e:K2 * e + K2], c.ident)
                    last.then_inc(S.full(f"hnT{k}"), 1)
                for k in range(TT):
                    S.wait_free(te, f"hnT{k}", b)
                te.wait_ge(img_in, b + 1)

                def rows(product, lo, c0, width):
                    S.claim(te, product, b)
                    for e in range(2):
                        last = nc.tensor.matmul(ps[:, bank(product), 0:width], c.wT[:, e, lo:lo + P],
                                                hnT[:, e, c0:c0 + width], start=(e == 0), stop=(e == 1))
                    last.then_inc(S.full(product), 1)
                rows("k2a", 320, 0, HALF)
                rows("k2b", 320, HALF, HALF)
                te.wait_ge(hnl_ready, b + 1)
                S.claim(te, "land", b)
                for k, lo in enumerate((0, 128, 192, 320)):
                    for e in range(2):
                        last = nc.tensor.matmul(ps[:, bank("land"), M * k:M * k + M], c.wT[:, e, lo:lo + P], hnl[:, e, :],
                                                start=(e == 0), stop=(e == 1))
                last.then_inc(S.full("land"), 1)
                rows("q1a", 128, 0, HALF)
                rows("q1b", 128, HALF, HALF)
                rows("q0a", 0, PAD, N // 2)
                rows("q0b", 0, PAD + N // 2, N // 2)
                for k in range(TT + 1):
                    product = ("v01", "v23", "v4")[k // 2]
                    rows_n, c0 = (P, PAD + NI + P * k) if k < TT else (NI, PAD)
                    if k % 2 == 0:
                        S.claim(te, product, b)
                    for e in range(2):
                        last = nc.tensor.matmul(ps[0:rows_n, bank(product), H * (k % 2):H * (k % 2) + H],
                                                hnT[:, e, c0:c0 + rows_n], c.wT[:, e, 448:640],
                                                start=(e == 0), stop=(e == 1))
                    if k % 2 or k == TT:
                        last.then_inc(S.full(product), 1)

                te.wait_ge(ql_ready, b + 1)
                S.claim(te, "sim2", b)
                for p in range(PAIRS):
                    last = nc.tensor.matmul(ps[:, bank("sim2"), M * p:M * p + M], ql[:, 2 * p:2 * p + 2, :],
                                            land[:, 3 if p < 4 else 1, :], start=True, stop=True)
                last.then_inc(S.full("sim2"), 1)
                def scores(p):
                    product = f"sim3_{p}"
                    if p == 0:
                        S.wait_free(te, "k2b", b)
                    if p == 4:
                        S.wait_free(te, "q1b", b)
                    te.wait_ge(exp3, ONE + b * PAIRS + max(p - 1, 0))
                    src = k2 if p < 4 else k1
                    nc.tensor.matmul(ps[:, bank(product), 0:512], ql[:, 2 * p:2 * p + 2, :], src[:, 0:512], start=True, stop=True)
                    nc.tensor.matmul(ps[:, bank(product) + 1, 0:NP - 512], ql[:, 2 * p:2 * p + 2, :], src[:, 512:NP],
                                     start=True, stop=True).then_inc(S.full(product), 1)

                def turn_probs(p):
                    te.wait_ge(exp3, ONE + b * PAIRS + (p + 1))
                    S.claim(te, f"p3T_{p}", b)
                    S.claim(te, f"p3I_{p}", b)
                    for k in range(TT):
                        c0 = PAD + NI + P * k
                        last = nc.tensor.transpose(ps[:, bank(f"p3T_{p}"), HW * k:HW * k + HW], p3[:, p % 3, c0:c0 + P], c.ident)
                    last.then_inc(S.full(f"p3T_{p}"), 1)
                    nc.tensor.transpose(ps[0:NI, bank(f"p3I_{p}"), 0:HW], p3[:, p % 3, PAD:PAD + NI], c.ident
                                        ).then_inc(S.full(f"p3I_{p}"), 1)

                def attn2_turned(g):
                    te.wait_ge(x2_ready, b + 1)
                    S.claim(te, f"xT{g}", b)
                    for k in range(3):
                        last = nc.tensor.transpose(ps[:, bank(f"xT{g}"), HW * k:HW * k + HW], x2[:, 3 * g + k, :], c.ident)
                    last.then_inc(S.full(f"xT{g}"), 1)

                def attn2_squared(g):
                    S.claim(te, f"x{g}", b)
                    for k in range(3):
                        last = nc.tensor.matmul(ps[:, bank(f"x{g}"), HW * k:HW * k + HW], x2T[:, 3 * g + k, :],
                                                x2T[:, 3 * g + k, :], start=True, stop=True)
                    last.then_inc(S.full(f"x{g}"), 1)
                scores(0)
                scores(1)
                for p in range(PAIRS):
                    if p + 2 < PAIRS:
                        scores(p + 2)
                    turn_probs(p)
                    if p in LM_ATTN2:
                        (attn2_turned if p < 4 else attn2_squared)(int(LM_ATTN2[p][-1]))
                S.claim(te, "u", b)
                for g in range(2):
                    S.wait_free(te, f"p3T_{3 + 2 * g}", b)
                    if g:
                        S.wait_free(te, "p3T_4", b)
                    S.wait_free(te, f"p3I_{3 + 2 * g}", b)
                    for k in range(TT + 1):
                        n = P if k < TT else NI
                        for p in range(4 * g, min(4 * g + 4, PAIRS)):
                            j = p % 4
                            last = nc.tensor.matmul(ps[32 * j:32 * j + 32, bank("u"), HW * g:HW * g + HW],
                                                    v[0:n, k, 32 * p:32 * p + 32], p3T[0:n, k, p, :],
                                                    start=(k == 0), stop=(k == TT))
                last.then_inc(S.full("u"), 1)
                S.wait_free(te, "u", b)
                S.claim(te, "uT", b)
                nc.tensor.transpose(ps[:, bank("uT"), 0:P], u[:, 0, :], c.ident)
                nc.tensor.transpose(ps[:, bank("uT"), P:P + M], u[0:M, 1, :], c.ident[0:M, 0:M]).then_inc(S.full("uT"), 1)
            with te.Fori(0, B) as b:
                turn(b)

        @block.scalar
        def _(sc):
            def copy(dst, src, scale=1.0):
                return nc.scalar.activation(dst, src, ACT.Copy, scale=scale)

            def rounds(b):
                sc.wait_ge(emb_in, ONE + b)
                sc.wait_ge(turned, b + 1)
                nc.scalar.activation(whole[:], turns[:], ACT.Copy, bias=MAGIC).then_inc(rounded, 1)

            def sines(b):
                sc.wait_ge(reduced, b + 1)
                nc.scalar.activation(whole[:], turns[:], ACT.Sin, scale=-TWO_PI).then_inc(sined, 1)

            def keep(b):
                sc.wait_ge(embedded, b + 1)
                copy(c.h[:, bass.ds(b * TT, TT), :], hm[:]).then_inc(kept, 1)

            def normalise(b):
                sc.wait_ge(moments_in, b + 1)
                for k in range(TT):
                    ins = nc.scalar.activation(hn[:, k, :], hm[:, k, :], ACT.Identity, bias=nshift[:, k:k + 1], scale=rstd[:, k:k + 1])
                ins.then_inc(hn_ready, 1)

            def squares(g, b):
                S.wait_full(sc, f"x{g}", b)
                x = ps[:, bank(f"x{g}"), 0:3 * HW].rearrange("p (k w) -> p k w", w=HW)
                for half in range(2):
                    r0 = M * half
                    at = c.E[r0:r0 + M, bass.ds(b, 1), 3 * g:3 * g + 3, :].rearrange("p b k w -> p (b k) w")
                    ins = copy(at, x[r0:r0 + M, :, r0:r0 + M])
                ins.then_inc(S.free(f"x{g}"), 1)

            def turn(b, following, second, third, first=False):
                sc.wait_ge(S.full("v4"), ONE + b * S.uses["A2"])
                copy(hnT[:, :, PAD:PAD + NI], c.hnT_img[:, :, bass.ds(b * NI, NI)]).then_inc(img_in, 1)
                for k in range(TT):
                    S.wait_full(sc, f"hnT{k}", b)
                    c0 = PAD + NI + P * k
                    copy(hnT[:, :, c0:c0 + P], ps[0:K2, bank(f"hnT{k}"), 0:2 * P].rearrange("p (e n) -> p e n", e=2)
                         ).then_inc(S.free(f"hnT{k}"), 1)
                for part, half in (("k2a", 0), ("k2b", 1)):
                    S.wait_full(sc, part, b)
                    copy(k2[:, HALF * half:HALF * half + HALF], ps[:, bank(part), 0:HALF]).then_inc(S.free(part), 1)
                S.wait_full(sc, "land", b)
                copy(land[:], ps[:, bank("land"), 0:4 * M].rearrange("p (k m) -> p k m", k=4), 1.0 / L
                     ).then_inc(S.free("land"), 1)
                sc.wait_ge(q_stored, DMA + b * 16)
                for part, half in (("q1a", 0), ("q1b", 1)):
                    S.wait_full(sc, part, b)
                    copy(k1[:, HALF * half:HALF * half + HALF], ps[:, bank(part), 0:HALF])
                    if half == 0:
                        copy(q0[:, 1, 0:HALF - PAD], ps[:, bank(part), PAD:HALF]).then_inc(S.free(part), 1)
                    else:
                        copy(q0[:, 1, HALF - PAD:N], ps[:, bank(part), 0:HALF]).then_inc(S.free(part), 1)
                for part, half in (("q0a", 0), ("q0b", 1)):
                    S.wait_full(sc, part, b)
                    copy(q0[:, 0, N // 2 * half:N // 2 * half + N // 2], ps[:, bank(part), 0:N // 2]).then_inc(S.free(part), 1)
                if first:
                    rounds(b + 2)
                if second:
                    sines(b + 2)
                for k, part in enumerate(("v01", "v23", "v4")):
                    S.wait_full(sc, part, b)
                    if k < 2:
                        copy(v[:, 2 * k:2 * k + 2, :], ps[:, bank(part), 0:2 * H].rearrange("p (k h) -> p k h", k=2)).then_inc(S.free(part), 1)
                    else:
                        copy(v[0:NI, TT, :], ps[0:NI, bank(part), 0:H]).then_inc(S.free(part), 1)
                sc.wait_ge(sub2, b + 1)
                nc.scalar.activation(w2[:], w2[:], ACT.Exp).then_inc(exp2, 1)
                for p in range(PAIRS + 1):
                    if p < PAIRS:
                        sc.wait_ge(max3, b * PAIRS + (p + 1))
                        if p >= 3:
                            S.wait_full(sc, f"p3I_{p - 3}", b)
                        src = ps[:, bank(f"sim3_{p}"):bank(f"sim3_{p}") + 2, :].rearrange("p k n -> p (k n)")[:, 0:NP]
                        nc.scalar.activation(p3[:, p % 3, :], src, ACT.Exp, bias=small[:, 3, p:p + 1],
                                             accum_out=small[:, 4, p:p + 1]).then_inc(exp3, 1)
                    if p:
                        q = p - 1
                        S.wait_full(sc, f"p3I_{q}", b)
                        copy(p3T[0:NI, TT, q, :], ps[0:NI, bank(f"p3I_{q}"), 0:HW]).then_inc(S.free(f"p3I_{q}"), 1)
                        if q in (1, 2):
                            g = q - 1
                            S.wait_full(sc, f"xT{g}", b)
                            copy(x2T[:, 3 * g:3 * g + 3, :], ps[:, bank(f"xT{g}"), 0:3 * HW].rearrange("p (k m) -> p k m", k=3)
                                 ).then_inc(S.free(f"xT{g}"), 1)
                        if q >= 4:
                            squares(q - 4, b)
                if following:
                    normalise(b + 1)
                if third:
                    rounds(b + 3)
                if following:
                    keep(b + 1)
            rounds(0)
            sines(0)
            rounds(1)
            normalise(0)
            sines(1)
            keep(0)
            turn(0, True, True, True, first=True)
            with sc.Fori(1, B - 3) as b:
                turn(b, True, True, True)
            turn(B - 3, True, True, False)
            turn(B - 2, True, False, False)
            turn(B - 1, False, False, False)

        @block.vector
        def _(ve_):
            ch = Chain(ve_, dve_done)

            def angle(b, k, j):
                ins = nc.vector.scalar_tensor_tensor(turns[:, k, j, :], c.turns_w[:, j, :],
                                                     c.tau[:, j, bass.ds(b * TT + k, 1)], c.turns_b[:, j, :], ALU.mult, ALU.add)
                ins.then_inc(turned, 1) if (k, j) == (TT - 1, 1) else ch(ins)

            def angles(b):
                for k in range(TT):
                    for j in range(2):
                        angle(b, k, j)

            def fractions(b):
                ve_.wait_ge(rounded, b + 1)
                ve_.wait_ge(turned, b + 1)
                nc.vector.scalar_tensor_tensor(turns[:].rearrange("p a j h -> p (a j h)"), whole[:].rearrange("p a j h -> p (a j h)"),
                                               MAGIC, turns[:].rearrange("p a j h -> p (a j h)"), ALU.subtract, ALU.subtract
                                               ).then_inc(reduced, 1)

            def embed_moments(b):
                ve_.wait_ge(emb_in, ONE + b + 1)
                ch.link(nc.vector.tensor_tensor(emb[:, :, H - 1], emb[:, :, H - 1], c.linear[:, bass.ds(b * TT, TT)], ALU.add))
                moments(nc, ch, emb, stats, mv, rstd, rt, ve, TT, 1e-12)

            def embed(b):
                ve_.wait_ge(kept, ONE + b)
                for k in range(TT):
                    ins = nc.vector.scalar_tensor_tensor(hm[:, k, :], emb[:, k, :], mv[:, k, 0:1], c.gamma, ALU.subtract, ALU.mult)
                    ch(ins) if k < TT - 1 else ins.then_inc(summed, 1)
                ve_.wait_ge(summed, ONE + b + 1)
                for k in range(TT):
                    ins = nc.vector.scalar_tensor_tensor(hm[:, k, :], hm[:, k, :], rstd[:, k:k + 1], c.beta, ALU.mult, ALU.add)
                    ch(ins) if k < TT - 1 else ins.then_inc(embedded, 1)
                ve_.wait_ge(embedded, b + 1)

            def shift_mean(b):
                ch.wait()
                nc.vector.scalar_tensor_tensor(nshift[:], mv[:, :, 0], -1.0, rstd[:], ALU.mult, ALU.mult).then_inc(moments_in, 1)

            def turn(b, following, second, third):
                S.wait_free(ve_, "hnT3", b)
                ve_.wait_ge(img_in, b + 1)
                nc.vector.tensor_reduce(hnl[:], hnT[:].rearrange("p e (m l) -> p e m l", l=L), AX.X, ALU.add
                                        ).then_inc(hnl_ready, 1)
                if second:
                    fractions(b + 2)
                if following:
                    embed_moments(b + 1)
                S.wait_free(ve_, "land", b)
                ch(nc.vector.tensor_tensor(ql[:, 0:8, :], c.mask, land[:, 0:1, :].to_broadcast([P, 8, M]), ALU.mult))
                nc.vector.tensor_tensor(ql[:, 8:12, :], c.mask[:, 4:8, :], land[:, 2:3, :].to_broadcast([P, 4, M]), ALU.mult
                                        ).then_inc(ql_ready, 1)
                ch(nc.vector.tensor_copy(c.landk[:, bass.ds(b, 1), :, :].rearrange("p b k m -> p (b k) m"), land[:, 2:4, :]))
                if following:
                    embed(b + 1)
                S.wait_full(ve_, "sim2", b)
                sim2 = ps[:, bank("sim2"), 0:PAIRS * M].rearrange("p (k m) -> p k m", m=M)
                ch.link(nc.vector.tensor_reduce(small[:, 0, :], sim2, AX.X, ALU.max, negate=True))
                nc.vector.tensor_tensor(w2[:], sim2, small[:, 0, :].unsqueeze(2).to_broadcast([P, PAIRS, M]), ALU.add
                                        ).then_inc(sub2, 1)
                ve_.wait_ge(sub2, b + 1)
                nc.vector.tensor_copy(small[:, 2, 0:1], small[:, 0, 0:1]).then_inc(S.free("sim2"), 1)
                for p in range(PAIRS):
                    S.wait_full(ve_, f"sim3_{p}", b)
                    src = ps[:, bank(f"sim3_{p}"):bank(f"sim3_{p}") + 2, :].rearrange("p k n -> p (k n)")[:, 0:NP]
                    nc.vector.tensor_reduce(small[:, 3, p:p + 1], src, AX.X, ALU.max, negate=True).then_inc(max3, 1)
                    if following:
                        if p:
                            rsqrt_step(nc, ch, rstd[:], rt[:], ve[:], 2 * p - 2)
                    if p == 1:
                        attn2(b)
                    if p >= 2:
                        probs_out(p - 2, b)
                    if following:
                        if p:
                            rsqrt_step(nc, ch, rstd[:], rt[:], ve[:], 2 * p - 1)
                        else:
                            variances(nc, ch, hm, stats, mv, rt, ve, TT, 1e-5)
                    if p and third:
                        if p == 1:
                            ve_.wait_ge(sined, b + 3)
                        angle(b + 3, (p - 1) // 2, (p - 1) % 2)
                probs_out(PAIRS - 2, b)
                if following:
                    rsqrt_step(nc, ch, rstd[:], rt[:], ve[:], RSQRT_STEPS - 1)
                    shift_mean(b + 1)
                probs_out(PAIRS - 1, b)
                if third:
                    for j in range(PAIRS - 1, 2 * TT):
                        angle(b + 3, j // 2, j % 2)
                ch(nc.vector.tensor_reduce(c.rows[:, bass.ds(b, 1), :].rearrange("p b k -> p (b k)"), x2[:], AX.X, ALU.add))
                S.wait_free(ve_, "xT1", b)
                ch(nc.vector.tensor_reduce(c.cols[:, bass.ds(b, 1), :].rearrange("p b k -> p (b k)"), x2T[:], AX.X, ALU.add))
                S.wait_full(ve_, "u", b)
                ch(nc.vector.tensor_copy(u[:, 0, :], ps[:, bank("u"), 0:HW]))
                nc.vector.tensor_copy(u[0:M, 1, :], ps[0:M, bank("u"), HW:2 * HW]).then_inc(S.free("u"), 1)
                ch.link(nc.vector.reciprocal(small[:, 5, :], small[:, 4, :]))
                S.wait_full(ve_, "uT", b)
                uT = ps[:, bank("uT"), 0:H].rearrange("p (k e d) -> p k e d", e=2, d=D)
                at = c.V[:, bass.ds(b, 1), :, :].rearrange("p b k d -> p (b k) d")
                ch(nc.vector.tensor_tensor(at[0:M], uT[0:M, :, 0, :], small[0:M, 5, :].unsqueeze(2).to_broadcast([M, PAIRS, D]), ALU.mult))
                nc.vector.tensor_tensor(at[M:P], uT[M:P, :, 1, :], small[M:P, 5, :].unsqueeze(2).to_broadcast([M, PAIRS, D]),
                                        ALU.mult).then_inc(S.free("uT"), 1)

            def attn2(b):
                ve_.wait_ge(exp2, b + 1)
                S.wait_free(ve_, "sim2", b)
                ch.link(nc.vector.tensor_reduce(small[:, 1, :], w2[:], AX.X, ALU.add))
                ch.link(nc.vector.reciprocal(small[:, 2, :], small[:, 1, :]))
                ve_.wait_ge(x2_stored, DMA + b * 16)
                ch(nc.vector.tensor_tensor(x2[0:M, :, 0:M], w2[0:M], small[0:M, 2, :].unsqueeze(2).to_broadcast([M, PAIRS, M]), ALU.mult))
                nc.vector.tensor_tensor(x2[M:P, :, M:HW], w2[M:P], small[M:P, 2, :].unsqueeze(2).to_broadcast([M, PAIRS, M]), ALU.mult
                                        ).then_inc(x2_ready, 1)

            def probs_out(p, b):
                S.wait_full(ve_, f"p3T_{p}", b)
                nc.vector.tensor_copy(p3T[:, 0:TT, p, :], ps[:, bank(f"p3T_{p}"), :].rearrange("p (k m) -> p k m", m=HW)
                                      ).then_inc(S.free(f"p3T_{p}"), 1)
            angles(0)
            fractions(0)
            nc.vector.memset(hnT[:], 0.0).then_inc(cleared, 1)
            nc.vector.memset(x2[:], 0.0).then_inc(cleared, 1)
            nc.vector.memset(c.landk[:, :, 0:1, :], 0.0).then_inc(cleared, 1)
            ve_.wait_ge(sined, 1)
            angles(1)
            embed_moments(0)
            embed(0)
            moments(nc, ch, hm, stats, mv, rstd, rt, ve, TT, 1e-5)
            shift_mean(0)
            fractions(1)
            ve_.wait_ge(sined, 2)
            angles(2)
            ve_.wait_ge(cleared, 3)
            with ve_.Fori(0, B - 3) as b:
                ch.enter(b, LM_DVE)
                turn(b, True, True, True)
                ch.leave(B - 3, "landmarks dve")
            turn(B - 3, True, True, False)
            turn(B - 2, True, False, False)
            turn(B - 1, False, False, False)


STREAMS = 4
PI_GP = 5 * STREAMS
PI_V = ITERS + 1


def pseudo_inverse(nc, c, sb, sem):
    peak = sb("peak", [P, 2])
    peak_all = sb("peak_all", [P, 2])
    inv_c = sb("inv_c", [P, 2])
    start = sb("start", [P, STREAMS, 3, EV])
    ev = sb("ev", [P, STREAMS, 3, EV])
    q = sb("q", [P, STREAMS, 3, EV])
    r = sb("r", [P, STREAMS, 3, EV])
    w = sb("w", [P, STREAMS, 3, D])
    x2 = sb("x2_in", [P, STREAMS, 3, HW])
    streams = range(STREAMS)
    peaks, peaked, scaled, prep = sem("pi_peaks"), sem("pi_peaked"), sem("pi_scaled"), sem("pi_prep")
    cleared = sem("pi_cleared")
    p1, p2, q_in, r_in, e_in, v_in = ([sem(f"pi_{n}_{s}") for s in streams] for n in ("p1", "p2", "q_in", "r_in", "e_in", "v_in"))
    a = [c.psum[:, 2 * s, 0:3 * EV].rearrange("p (k w) -> p k w", k=3) for s in streams]
    bb = [c.psum[:, 2 * s + 1, 0:3 * EV].rearrange("p (k w) -> p k w", k=3) for s in streams]
    turns = B // 2

    x2_in = sem("pi_x2_in")

    def put_start(engine, ch, i, s):
        g = s % 2
        bx = bass.ds(i * 2 + s // 2, 1)
        for half in range(2):
            r0 = M * half
            src = c.E[r0:r0 + M, bx, 3 * g:3 * g + 3, :].rearrange("p b k m -> p (b k) m")
            ch.link(engine.tensor_tensor(start[r0:r0 + M, s, :, r0:r0 + M], src,
                                         inv_c[r0:r0 + M, 1:2].unsqueeze(2).to_broadcast([M, 3, M]), ALU.mult))
        src = c.V[:, bx, 3 * g:3 * g + 3, :].rearrange("p b k d -> p (b k) d")
        ch.link(engine.tensor_copy(start[:, s, :, HW:EV], src))
        for half in range(2):
            r0 = M * half
            at = start[r0:r0 + M, s, :, r0:r0 + M]
            one = c.ident[r0:r0 + M, r0:r0 + M].unsqueeze(1).to_broadcast([M, 3, M])
            ch.link(engine.tensor_tensor(at, at, one, ALU.add))

    with nc.Block() as block:
        @block.sync
        def _(sp):
            give(sp, [*p1, *r_in, *v_in], [])
            with sp.Fori(0, turns) as i:
                for s in streams:
                    sp.wait_ge(p1[s], ONE + i * PI_V)
                    g = s % 2
                    src = c.x_dram[bass.ds(i * 2 + s // 2, 1), :, 3 * g:3 * g + 3, :].rearrange("b p k m -> (b p) k m")
                    sp.dma_start(x2[:, s], src).then_inc(x2_in, 16)

        @block.gpsimd
        def _(gp):
            ch = Chain(gp, prep)
            gp.wait_ge(peaks, 2)
            nc.gpsimd.partition_all_reduce(peak_all[:], peak[:], channels=P, reduce_op=RMAX).then_inc(peaked, 1)
            ch.n = PI_GP
            with gp.Fori(0, turns - 1) as i:
                ch.enter(i, PI_GP)
                for s in streams:
                    gp.wait_ge(r_in[s], ONE + i * ITERS + 1)
                    put_start(nc.gpsimd, ch, i + 1, s)
                ch.leave(turns - 1, "pseudo-inverse pool")

        @block.tensor
        def _(te):
            te.wait_ge(cleared, 2)

            def turn(i):
                for k in range(ITERS):
                    for s in streams:
                        if k == 0:
                            te.wait_ge(prep, i * PI_GP + 5 * (s + 1))
                        te.wait_ge(v_in[s], ONE + i * PI_V + k)
                        x = start if k == 0 else ev
                        for p in range(3):
                            last = nc.tensor.matmul(a[s][:, p, :], x[:, s, p, 0:HW], x[:, s, p, :], start=True, stop=True)
                        last.then_inc(p1[s], 1)
                    for s in streams:
                        te.wait_ge(r_in[s], ONE + i * ITERS + (k + 1))
                        lo = 0 if k < ITERS - 1 else HW
                        for p in range(3):
                            last = nc.tensor.matmul(bb[s][:, p, lo:EV], q[:, s, p, 0:HW], r[:, s, p, lo:EV], start=True, stop=True)
                        last.then_inc(p2[s], 1)
                te.wait_ge(x2_in, i * (16 * STREAMS) + 16 * STREAMS)
                for s in streams:
                    te.wait_ge(v_in[s], ONE + i * PI_V + ITERS)
                    for p in range(3):
                        last = nc.tensor.matmul(a[s][:, p, HW:EV], x2[:, s, p, :], ev[:, s, p, HW:EV], start=True, stop=True)
                    last.then_inc(p1[s], 1)
            with te.Fori(0, turns) as i:
                turn(i)

        @block.scalar
        def _(sc):
            def turn(i):
                for k in range(ITERS):
                    for s in streams:
                        sc.wait_ge(p1[s], ONE + i * PI_V + (k + 1))
                        nc.scalar.activation(q[:, s], a[s], ACT.Copy).then_inc(q_in[s], 1)
                    if k < ITERS - 1:
                        for s in streams:
                            sc.wait_ge(p2[s], i * ITERS + (k + 1))
                            nc.scalar.activation(ev[:, s, :, 0:HW], bb[s][:, :, 0:HW], ACT.Copy, scale=0.25).then_inc(e_in[s], 1)
            with sc.Fori(0, turns) as i:
                turn(i)

        @block.vector
        def _(ve):
            nc.vector.tensor_reduce(peak[:, 0:1], c.rows[:].rearrange("p b k -> p (b k)"), AX.X, ALU.max).then_inc(peaks, 1)
            nc.vector.tensor_reduce(peak[:, 1:2], c.cols[:].rearrange("p b k -> p (b k)"), AX.X, ALU.max).then_inc(peaks, 1)
            nc.vector.memset(start[:], 0.0).then_inc(cleared, 1)
            nc.vector.memset(ev[:], 0.0).then_inc(cleared, 1)
            ve.wait_ge(peaked, 1)
            nc.vector.tensor_tensor(peak[:, 0:1], peak_all[:, 0:1], peak_all[:, 1:2], ALU.mult).then_inc(peaks, 1)
            ve.wait_ge(peaks, 3)
            nc.vector.reciprocal(inv_c[:, 0:1], peak[:, 0:1]).then_inc(scaled, 1)
            ve.wait_ge(scaled, 1)
            nc.vector.tensor_scalar(inv_c[:, 1:2], inv_c[:, 0:1], -1.0, None, ALU.mult).then_inc(scaled, 1)
            ve.wait_ge(scaled, 2)
            ve.wait_ge(cleared, 2)
            first = Chain(ve, prep)
            for s in streams:
                put_start(nc.vector, first, 0, s)

            def turn(i):
                for k in range(ITERS):
                    x = start if k == 0 else ev
                    for s in streams:
                        ve.wait_ge(q_in[s], i * ITERS + (k + 1))
                        ve.wait_ge(v_in[s], ONE + i * PI_V + k)
                        nc.vector.tensor_tensor(w[:, s], x[:, s, :, HW:EV], q[:, s, :, HW:EV], ALU.add)
                        nc.vector.scalar_tensor_tensor(r[:, s, :, HW:EV], x[:, s, :, HW:EV], 4.0, q[:, s, :, HW:EV], ALU.mult, ALU.add)
                        nc.vector.scalar_tensor_tensor(r[:, s, :, 0:HW], x[:, s, :, 0:HW], 3.0, q[:, s, :, 0:HW], ALU.mult, ALU.add
                                                       ).then_inc(r_in[s], 1)
                    for s in streams:
                        ve.wait_ge(p2[s], i * ITERS + (k + 1))
                        if k < ITERS - 1:
                            ve.wait_ge(e_in[s], i * (ITERS - 1) + (k + 1))
                        dst = ev[:, s, :, HW:EV]
                        ve.wait_ge(r_in[s], ONE + i * ITERS + (k + 1))
                        nc.vector.scalar_tensor_tensor(dst, bb[s][:, :, HW:EV], 0.25, w[:, s], ALU.mult, ALU.add).then_inc(v_in[s], 1)
                for s in streams:
                    g = s % 2
                    dst = c.V[:, bass.ds(i * 2 + s // 2, 1), 3 * g:3 * g + 3, :].rearrange("p b k d -> p (b k) d")
                    ve.wait_ge(p1[s], ONE + i * PI_V + PI_V)
                    nc.vector.tensor_scalar(dst, a[s][:, :, HW:EV], inv_c[:, 0:1], None, ALU.mult).then_inc(v_in[s], 1)
            with ve.Fori(0, turns) as i:
                turn(i)


AT_FRONT = [(f"scores{k}", f"S{k % 2}") if q == 0 else (f"probs{k}", "T") for k in range(TT + 1) for q in range(2)]
AT_FRONT += [("outA", "T"), ("out_img", "I"), ("outB", "O")]
AT_ROUTER = ("rt", "rt_img", "xs", "xsT", "eCT")
AT_TAIL = [("proj0", "R0"), ("proj1", "R1"), ("proj2", "R0"), ("rt", "R1"), ("rt_img", "R0"), ("xs", "R1"), ("xsT", "R0"), ("eCT", "R1")]
AT_TAIL += [(f"xnT{k}", f"R{k % 2}") for k in range(TT + 1)] + [("lgT", "R1"), ("lgT_img", "R0")]
AT_DVE, AT_GP = 37, 3
TILES = TT + 1


def attention(nc, c, t, sb, sem):
    qb = sb("qb", [P, 2, N])
    kl = sb("kl", [P, 12, M])
    zb = sb("zb", [P, PAIRS, 2 * D])
    e1 = sb("e1", [P, TILES, NH * M])
    p1T = sb("p1T", [P, PAIRS, N])
    neg = sb("neg", [P, 2, NH])
    den = sb("den", [P, 2, S])
    rden_img = sb("rden_img", [P, 2 * NI])
    oA = sb("oA", [P, N])
    oB = sb("oB", [M + 1, N])
    stats, mv = sb("stats", [P, TILES, 6]), sb("mv", [P, TILES, 2])
    v192, t1, rn = sb("v192", [P, TILES]), sb("t1", [P, TILES]), sb("rn", [P, TILES])
    shift = sb("shift", [P, TILES])
    hw = sb("hw", [P, TILES, H])
    xn = sb("xn", [P, TILES, H])
    xnT = sb("xnT", [K2, 2, N])
    rT = sb("rT", [P, N])
    rt = sb("rt", [P, TILES, 2 * NE])
    dstat = sb("dstat", [P, 4])
    eC = sb("eC", [P, TILES, NE])
    negC = sb("negC", [P, TILES])
    sumC = sb("sumC", [P, TILES])
    xs = sb("xs", [P, H])
    CT = sb("CT", [NE, N])
    F_ = Slots(sem, "at", AT_FRONT)
    R_ = Slots(sem, "at", AT_TAIL)
    banks = {"S0": 0, "I": 0, "S1": 2, "O": 2, "T": 4, "R0": 6, "R1": 7}
    ps = c.psum

    def two(product):
        b0 = banks[F_.at[product][0]]
        return ps[:, b0:b0 + 2, :].rearrange("p k n -> p (k n)")

    def one(product):
        return ps[:, banks[R_.at[product][0]], :]

    q_in, kl_in, zb_in = sem("at_q_in"), sem("at_kl_in"), sem("at_zb_in")
    cleared, room_cleared = sem("at_cleared"), sem("at_room_cleared")
    shifted, exp_in = sem("at_shifted"), sem("at_exp_in")
    h_in, den_in, ln_in = sem("at_h_in"), sem("at_den_in"), sem("at_ln_in")
    normed, xn_in = sem("at_normed"), sem("at_xn_in")
    d_shift, eD_in, c_shift, eC_in, d_scale = (sem("at_" + n) for n in ("d_shift", "eD_in", "c_shift", "eC_in", "d_scale"))
    dve_done, gp_done, c_stored = sem("at_dve"), sem("at_gp"), sem("at_c_stored")

    chunks = [(0, NI)] + [(NI + P * k, P) for k in range(TT)]
    tiles = [(P, NI + P * k) for k in range(TT)] + [(NI, 0)]

    with nc.Block() as block:
        @block.sync
        def _(sp):
            give(sp, [shifted, h_in], [c_stored], F_, R_)
            def load(b):
                sp.wait_ge(F_.full("scores4"), ONE + b * F_.uses["S0"])
                sp.dma_start(qb[:], c.q_dram[bass.ds(b, 1)].rearrange("b p k n -> (b p) k n")).then_inc(q_in, 16)

            def store(b):
                R_.wait_free(sp, "eCT", b + 1)
                R_.wait_free(sp, "xsT", b + 1)
                sp.dma_start(c.c_dram[bass.ds(b, 1)].rearrange("b n t -> (b n) t"), CT[:]).then_inc(c_stored, 16)
            load(0)
            load(1)
            load_experts(sp, c, t, 0, 0)
            load(2)
            with sp.Fori(0, B - 3) as b:
                load(b + 3)
                store(b)
            store(B - 3)
            store(B - 2)
            store(B - 1)
            sp.wait_ge(c_stored, DMA + 16 * B)

        @block.gpsimd
        def _(gp):
            ch = Chain(gp, gp_done)
            def keys(b):
                gp.wait_ge(F_.full("scores4"), ONE + b * F_.uses["S0"])
                ch.link(nc.gpsimd.tensor_tensor(kl[:, 0:8, :], c.mask, c.landk[:, bass.ds(b, 1), 1, :].to_broadcast([P, 8, M]), ALU.mult))
                nc.gpsimd.tensor_tensor(kl[:, 8:12, :], c.mask[:, 0:4, :], c.landk[:, bass.ds(b, 1), 0, :].to_broadcast([P, 4, M]), ALU.mult
                                        ).then_inc(kl_in, 1)
                gp.wait_ge(kl_in, b + 1)

            def values(b):
                gp.wait_ge(F_.full("out_img"), ONE + b)
                for half in range(2):
                    r0 = M * half
                    src = c.V[r0:r0 + M, bass.ds(b, 1), :, :].rearrange("p b k d -> p (b k) d")
                    ins = nc.gpsimd.tensor_copy(zb[r0:r0 + M, :, D * half:D * half + D], src)
                    if half:
                        ins.then_inc(zb_in, 1)
                        gp.wait_ge(zb_in, b + 1)
                    else:
                        ch.link(ins)

            def residual(b):
                R_.wait_free(gp, "proj1", b)
                R_.wait_free(gp, "proj2", b)
                ch.link(nc.gpsimd.tensor_copy(c.h[:, bass.ds(b * TT, TT), :], hw[:, 0:TT, :]))
                nc.gpsimd.tensor_copy(c.h_img[:, bass.ds(b, 1), :], hw[0:NI, TT:TILES, :]).then_inc(h_in, 1)
                gp.wait_ge(h_in, b + 1)
            keys(0)
            ch.link(nc.gpsimd.memset(zb[:], 0.0))
            values(0)
            keys(1)
            ch.link(nc.gpsimd.memset(c.xsT[:], 0.0))
            ch.link(nc.gpsimd.memset(c.xsT[K2:K2 + 1, 0:1], 1.0))
            nc.gpsimd.memset(c.rsum[:], 1.0).then_inc(room_cleared, 1)
            with gp.Fori(0, B - 2) as b:
                ch.enter(b, AT_GP)
                values(b + 1)
                residual(b)
                keys(b + 2)
                ch.leave(B - 2, "attention pool")
            values(B - 1)
            residual(B - 2)
            residual(B - 1)

        @block.tensor
        def _(te):
            def scores(k, b):
                c0, n = chunks[k]
                if k == 1:
                    te.wait_ge(F_.free("outB"), ONE + b)
                if k == 0:
                    te.wait_ge(q_in, b * 16 + 16)
                    te.wait_ge(kl_in, b + 1)
                    te.wait_ge(F_.free("out_img"), ONE + b)
                te.wait_ge(shifted, ONE + b * TILES + max(k - 1, 0))
                out = two(f"scores{k}")
                klf = kl[:].rearrange("p h m -> p (h m)")
                nc.tensor.matmul(out[0:n, 0:512], qb[:, 0, c0:c0 + n], klf[:, 0:512], start=True, stop=True)
                nc.tensor.matmul(out[0:n, 512:768], qb[:, 1, c0:c0 + n], klf[:, 512:768], start=True, stop=True
                                 ).then_inc(F_.full(f"scores{k}"), 1)

            def probs(k, b):
                c0, n = chunks[k]
                te.wait_ge(exp_in, b * TILES + (k + 1))
                F_.claim(te, f"probs{k}", b)
                out = two(f"probs{k}")
                for p in range(PAIRS):
                    last = nc.tensor.transpose(out[:, P * p:P * p + P], e1[:, k, HW * p:HW * p + HW], c.ident)
                last.then_inc(F_.full(f"probs{k}"), 1)

            def out(g, b):
                product = ("outA", "outB")[g]
                if g == 0:
                    te.wait_ge(zb_in, b + 1)
                    F_.claim(te, product, b)
                else:
                    te.wait_ge(shifted, ONE + b * TILES + TILES)
                for q in range(2):
                    for p in range(4 * g, min(4 * g + 4, PAIRS)):
                        j = p % 4
                        lhsT = c.ones_bd if q else zb[:, p, :]
                        last = nc.tensor.matmul(two(product)[32 * j:32 * j + 32, 512 * q:512 * q + S], lhsT,
                                                p1T[:, p, NI:N], start=True, stop=True)
                last.then_inc(F_.full(product), 1)

            def out_img(b):
                te.wait_ge(shifted, ONE + b * TILES + TILES)
                for p in range(PAIRS):
                    j = p % 4
                    for q in range(2):
                        c0 = 2 * NI * (p // 4) + NI * q
                        last = nc.tensor.matmul(two("out_img")[32 * j:32 * j + 32, c0:c0 + NI], c.ones_bd if q else zb[:, p, :],
                                                p1T[:, p, 0:NI], start=True, stop=True)
                last.then_inc(F_.full("out_img"), 1)

            def tail0(b, part):
                for product in ("outA", "out_img", "outB"):
                    F_.wait_free(te, product, b)
                for k in ((4, 0, 1), (2, 3))[part]:
                    n, c0 = tiles[k]
                    product = "proj0" if k == 4 else f"proj{1 + k // 2}"
                    lo = H * (k % 2) if k < 4 else 0
                    if k in (4, 0, 2):
                        R_.claim(te, product, b)
                    nc.tensor.matmul(one(product)[0:n, lo:lo + H], oA[:, c0:c0 + n], c.wprojT[:, 0, :], start=True, stop=False)
                    last = nc.tensor.matmul(one(product)[0:n, lo:lo + H], oB[:, c0:c0 + n], c.wprojT[0:M + 1, 1, :],
                                            start=False, stop=True)
                    if k in (4, 1, 3):
                        last.then_inc(R_.full(product), 1)

            def tail1(b):
                te.wait_ge(xn_in, b + 1)
                for k, (n, c0) in enumerate(tiles):
                    R_.claim(te, f"xnT{k}", b)
                    for e in range(2):
                        last = nc.tensor.transpose(one(f"xnT{k}")[0:K2, P * e:P * e + P], xn[:, k, K2 * e:K2 * e + K2], c.ident)
                    last.then_inc(R_.full(f"xnT{k}"), 1)

            def tail2(b):
                R_.wait_free(te, "xnT3", b)
                R_.wait_free(te, "xnT4", b)
                for product, c0, n in (("lgT", NI, S), ("lgT_img", 0, NI)):
                    R_.claim(te, product, b)
                    for e in range(2):
                        last = nc.tensor.matmul(one(product)[:, 0:n], c.phin[:, e, :], xnT[:, e, c0:c0 + n], start=(e == 0), stop=(e == 1))
                    last.then_inc(R_.full(product), 1)

            def tail3(b):
                te.wait_ge(eD_in, b + 1)
                R_.claim(te, "rt", b + 1)
                R_.claim(te, "rt_img", b + 1)
                for k in range(TT):
                    last = nc.tensor.transpose(one("rt")[:, P * k:P * k + P], rT[:, NI + P * k:NI + P * k + P], c.ident)
                last.then_inc(R_.full("rt"), 1)
                nc.tensor.transpose(one("rt_img")[0:NI, 0:P], rT[:, 0:NI], c.ident).then_inc(R_.full("rt_img"), 1)

            def tail4(b):
                R_.wait_free(te, "rt", b + 1)
                R_.wait_free(te, "rt_img", b + 1)
                R_.claim(te, "xs", b + 1)
                for k, (n, c0) in enumerate(tiles):
                    last = nc.tensor.matmul(one("xs")[NE:P, 0:H], rt[0:n, k, NE:P], xn[0:n, k, :], start=(k == 0), stop=(k == TT))
                last.then_inc(R_.full("xs"), 1)

            def tail5(b):
                R_.wait_free(te, "xs", b + 1)
                R_.claim(te, "xsT", b + 1)
                R_.claim(te, "eCT", b + 1)
                te.wait_ge(eC_in, b + 1)
                for e in range(2):
                    nc.tensor.transpose(one("xsT")[0:K2, P * e:P * e + P], xs[:, e:H:2], c.ident)
                nc.tensor.transpose(one("xsT")[0:NE, 2 * P:2 * P + NI], eC[0:NI, TT, :], c.ident[0:NI, 0:NI]).then_inc(R_.full("xsT"), 1)
                for k in range(TT):
                    last = nc.tensor.transpose(one("eCT")[0:NE, P * k:P * k + P], eC[:, k, :], c.ident)
                last.then_inc(R_.full("eCT"), 1)

            def skip(*products, i):
                for product in products:
                    R_.claim(te, product, i)
                    te.sem_inc(R_.full(product), 1)
                    te.sem_inc(R_.free(product), 1)

            def turn(i, front=True, tail=True, router=True):
                if front:
                    scores(0, i + 1)
                    scores(1, i + 1)
                if tail:
                    tail0(i, 0)
                else:
                    skip("proj0", "proj1", "proj2", i=i)
                if front:
                    scores(2, i + 1)
                if tail:
                    tail0(i, 1)
                if front:
                    probs(0, i + 1)
                    scores(3, i + 1)
                if router:
                    tail3(i - 1)
                if front:
                    probs(1, i + 1)
                    scores(4, i + 1)
                    probs(2, i + 1)
                if router:
                    tail4(i - 1)
                if front:
                    probs(3, i + 1)
                    probs(4, i + 1)
                if router:
                    tail5(i - 1)
                else:
                    skip(*AT_ROUTER, i=i)
                if front:
                    out(0, i + 1)
                    out(1, i + 1)
                    out_img(i + 1)
                if tail:
                    tail1(i)
                else:
                    skip(*(f"xnT{k}" for k in range(TILES)), "lgT", "lgT_img", i=i)
                if tail:
                    tail2(i)
            scores(0, 0)
            scores(1, 0)
            scores(2, 0)
            for k in range(TILES):
                probs(k, 0)
                if k + 3 < TILES:
                    scores(k + 3, 0)
            out(0, 0)
            out(1, 0)
            out_img(0)
            turn(0, router=False)
            with te.Fori(1, B - 1) as i:
                turn(i)
            turn(B - 1, front=False)
            turn(B, front=False, tail=False)

        @block.scalar
        def _(sc):
            def copy(dst, src, scale=1.0):
                return nc.scalar.activation(dst, src, ACT.Copy, scale=scale)

            def exps(k, b):
                n = chunks[k][1]
                sc.wait_ge(shifted, ONE + b * TILES + (k + 1))
                nc.scalar.activation(e1[0:n, k, :], e1[0:n, k, :], ACT.Exp).then_inc(exp_in, 1)

            def evac(k, b):
                c0, n = chunks[k]
                F_.wait_full(sc, f"probs{k}", b)
                src = two(f"probs{k}").rearrange("p (k n) -> p k n", n=P)
                copy(p1T[:, 0:4, c0:c0 + n], src[:, 0:4, 0:n])
                copy(p1T[:, 4:6, c0:c0 + n], src[:, 4:6, 0:n]).then_inc(F_.free(f"probs{k}"), 1)

            def tail0(b):
                sc.wait_ge(normed, b + 1)
                for k, (n, c0) in enumerate(tiles):
                    ins = nc.scalar.activation(xn[0:n, k, :], hw[0:n, k, :], ACT.Identity, bias=shift[0:n, k:k + 1], scale=rn[0:n, k:k + 1])
                ins.then_inc(xn_in, 1)

            def tail2(b):
                for product, c0, n in (("lgT", NI, S), ("lgT_img", 0, NI)):
                    R_.wait_full(sc, product, b)
                    copy(rT[:, c0:c0 + n], one(product)[:, 0:n]).then_inc(R_.free(product), 1)

            def tail3_exp(b):
                sc.wait_ge(d_shift, b + 1)
                nc.scalar.activation(rT[NE:P], rT[NE:P], ACT.Exp, bias=dstat[NE:P, 0:1], accum_out=dstat[NE:P, 1:2]).then_inc(eD_in, 1)

            def tail3(b):
                R_.wait_full(sc, "rt", b + 1)
                copy(rt[:, 0:TT, :], one("rt").rearrange("p (k n) -> p k n", n=P)).then_inc(R_.free("rt"), 1)
                R_.wait_full(sc, "rt_img", b + 1)
                copy(rt[0:NI, TT, :], one("rt_img")[0:NI, 0:P]).then_inc(R_.free("rt_img"), 1)

            def tail4(b):
                sc.wait_ge(c_shift, b + 1)
                nc.scalar.activation(eC[:, 0:TT, :], eC[:, 0:TT, :], ACT.Exp)
                nc.scalar.activation(eC[0:NI, TT, :], eC[0:NI, TT, :], ACT.Exp).then_inc(eC_in, 1)

            def tail4_xs(b):
                R_.wait_full(sc, "xs", b + 1)
                sc.wait_ge(d_scale, b + 1)
                copy(xs[NE:P], one("xs")[NE:P, 0:H], dstat[NE:P, 2:3]).then_inc(R_.free("xs"), 1)

            def tail5(b):
                R_.wait_full(sc, "eCT", b + 1)
                sc.wait_ge(c_stored, DMA + b * 16)
                copy(CT[:, NI:N], one("eCT")[0:NE, 0:S]).then_inc(R_.free("eCT"), 1)

            def out(b):
                for g, (product, n) in enumerate((("outA", P), ("outB", M))):
                    F_.wait_full(sc, product, b)
                    nc.scalar.activation(den[0:n, g, :], two(product)[0:n, 512:512 + S], ACT.Ln).then_inc(ln_in, 1)
                for g, n in enumerate((P, M)):
                    sc.wait_ge(ln_in, 2 * b + (g + 1))
                    nc.scalar.activation(den[0:n, g, :], den[0:n, g, :], ACT.Exp, scale=-1.0).then_inc(den_in, 1)

            def turn(i, front=True, tail=True, router=True):
                if router:
                    tail3_exp(i - 1)
                if front:
                    exps(0, i + 1)
                    exps(1, i + 1)
                    evac(0, i + 1)
                if router:
                    tail3(i - 1)
                if front:
                    exps(2, i + 1)
                    evac(1, i + 1)
                    exps(3, i + 1)
                    evac(2, i + 1)
                    exps(4, i + 1)
                    evac(3, i + 1)
                if router:
                    tail4(i - 1)
                    tail4_xs(i - 1)
                if front:
                    evac(4, i + 1)
                if router:
                    tail5(i - 1)
                if tail:
                    if router:
                        R_.wait_full(sc, "xs", i)
                    tail0(i)
                if front:
                    out(i + 1)
                if tail:
                    tail2(i)
            for k in range(TILES):
                exps(k, 0)
                evac(k, 0)
            out(0)
            turn(0, router=False)
            with sc.Fori(1, B - 1) as i:
                turn(i)
            turn(B - 1, front=False)
            turn(B, front=False, tail=False)

        @block.vector
        def _(ve):
            ch = Chain(ve, dve_done)
            for tile, value in ((e1[:, 0, :], 0.0), (mv[:], 0.0), (xn[:, TT, :], 0.0), (xs[:], 0.0), (oB[M:M + 1, :], 1.0)):
                nc.vector.memset(tile, value).then_inc(cleared, 1)
            ve.wait_ge(cleared, 5)

            def front(k, b):
                c0, n = chunks[k]
                F_.wait_full(ve, f"scores{k}", b)
                src = two(f"scores{k}")[0:n, 0:NH * M].rearrange("p (h m) -> p h m", m=M)
                ve.wait_ge(shifted, ONE + b * TILES + max(k - 1, 0))
                ch.link(nc.vector.tensor_reduce(neg[0:n, k % 2, :], src, AX.X, ALU.max, negate=True))
                nc.vector.tensor_tensor(e1[0:n, k, :].rearrange("p (h m) -> p h m", m=M), src,
                                        neg[0:n, k % 2, :].unsqueeze(2).to_broadcast([n, NH, M]), ALU.add).then_inc(shifted, 1)

            def out(g, b):
                product, o, n = (("outA", oA, P), ("outB", oB, M))[g]
                ve.wait_ge(den_in, 2 * b + (g + 1))
                nc.vector.tensor_tensor(o[0:n, NI:N], two(product)[0:n, 0:S], den[0:n, g, :], ALU.mult).then_inc(F_.free(product), 1)

            def out_img(b):
                F_.wait_full(ve, "out_img", b)
                for g, (o, n) in enumerate(((oA, P), (oB, M))):
                    ch(nc.vector.reciprocal(rden_img[0:n, NI * g:NI * g + NI], two("out_img")[0:n, 2 * NI * g + NI:2 * NI * g + 2 * NI]))
                ch.wait()
                for g, (o, n) in enumerate(((oA, P), (oB, M))):
                    ins = nc.vector.tensor_tensor(o[0:n, 0:NI], two("out_img")[0:n, 2 * NI * g:2 * NI * g + NI],
                                                  rden_img[0:n, NI * g:NI * g + NI], ALU.mult)
                ins.then_inc(F_.free("out_img"), 1)

            def tail0(b, part):
                if part == 0:
                    R_.wait_full(ve, "proj0", b)
                    h = c.h_img[:, bass.ds(b, 1), :].rearrange("p a h -> p (a h)")
                    ve.wait_ge(h_in, ONE + b)
                    nc.vector.tensor_tensor(hw[0:NI, TT, :], one("proj0")[0:NI, 0:H], h, ALU.add).then_inc(R_.free("proj0"), 1)
                product = f"proj{1 + part}"
                R_.wait_full(ve, product, b)
                h = c.h[:, bass.ds(b * TT + 2 * part, 2), :]
                nc.vector.tensor_tensor(hw[:, 2 * part:2 * part + 2, :], one(product)[:, 0:2 * H].rearrange("p (a h) -> p a h", h=H), h, ALU.add
                                        ).then_inc(R_.free(product), 1)

            def tail1(b):
                for k, (n, c0) in enumerate(tiles):
                    R_.wait_full(ve, f"xnT{k}", b)
                    src = one(f"xnT{k}")[0:K2, 0:2 * P].rearrange("p (e n) -> p e n", e=2)[:, :, 0:n]
                    nc.vector.tensor_copy(xnT[:, :, c0:c0 + n], src).then_inc(R_.free(f"xnT{k}"), 1)

            def statistics(b):
                R_.wait_free(ve, "proj1", b)
                R_.wait_free(ve, "proj2", b)
                for k in range(TT):
                    ch(nc.vector.bn_stats(stats[:, k, :], hw[:, k, :]))
                ch(nc.vector.bn_stats(stats[0:NI, TT, :], hw[0:NI, TT, :]))
                ch.wait()
                nc.vector.tensor_copy(t1[:, 0:1], stats[:, 0, 0:1])
                for k in range(TILES):
                    n = tiles[k][0]
                    ch(nc.vector.bn_aggr(mv[0:n, k, :], stats[0:n, k, :]))
                ch.wait()

            def norms(b):
                ch.link(nc.vector.tensor_scalar(t1[:], mv[:, :, 1], 1e-24, 1e-29, ALU.mult, ALU.add))
                ch.link(nc.vector.scalar_tensor_tensor(v192[:], mv[:, :, 1], float(H), t1[:], ALU.mult, ALU.max))
                rsqrt(nc, ch, rn[:], t1[:], v192[:])
                nc.vector.scalar_tensor_tensor(shift[:], mv[:, :, 0], -1.0, rn[:], ALU.mult, ALU.mult).then_inc(normed, 1)

            def tail2(b):
                R_.wait_free(ve, "lgT", b)
                R_.wait_free(ve, "lgT_img", b)
                nc.vector.tensor_reduce(dstat[:, 0:1], rT[:], AX.X, ALU.max, negate=True).then_inc(d_shift, 1)

            def tail3(b):
                R_.wait_free(ve, "rt", b + 1)
                R_.wait_free(ve, "rt_img", b + 1)
                R_.wait_full(ve, "eCT", b)
                nc.vector.reciprocal(dstat[NE:P, 2:3], dstat[NE:P, 1:2]).then_inc(d_scale, 1)
                ch(nc.vector.tensor_reduce(negC[:, 0:TT], rt[:, 0:TT, 0:NE], AX.X, ALU.max, negate=True))
                ch.link(nc.vector.tensor_reduce(negC[0:NI, TT:TILES], rt[0:NI, TT:TILES, 0:NE], AX.X, ALU.max, negate=True))
                nc.vector.tensor_tensor(eC[:, 0:TT, :], rt[:, 0:TT, 0:NE], negC[:, 0:TT].unsqueeze(2).to_broadcast([P, TT, NE]), ALU.add)
                nc.vector.tensor_tensor(eC[0:NI, TT:TILES, :], rt[0:NI, TT:TILES, 0:NE],
                                        negC[0:NI, TT:TILES].unsqueeze(2).to_broadcast([NI, 1, NE]), ALU.add).then_inc(c_shift, 1)

            def tail4(b):
                ve.wait_ge(eC_in, b + 1)
                ch(nc.vector.tensor_reduce(sumC[:, 0:TT], eC[:, 0:TT, :], AX.X, ALU.add))
                ch.link(nc.vector.tensor_reduce(sumC[0:NI, TT:TILES], eC[0:NI, TT:TILES, :], AX.X, ALU.add))
                at = c.rsum[:, bass.ds(b, 1), :].rearrange("p b k -> p (b k)")
                ch(nc.vector.reciprocal(at[:, 0:TT], sumC[:, 0:TT]))
                ch(nc.vector.reciprocal(at[0:NI, TT:TILES], sumC[0:NI, TT:TILES]))

            def tail5(b):
                R_.wait_full(ve, "xsT", b + 1)
                ve.wait_ge(c_stored, DMA + b * 16)
                ch(nc.vector.tensor_copy(CT[:, 0:NI], one("xsT")[0:NE, 2 * P:2 * P + NI]))
                src = one("xsT")[0:K2, 0:2 * P].rearrange("p (e n) -> p e n", e=2)[:, :, NE:P]
                nc.vector.tensor_copy(c.xsT[0:K2, :, :, bass.ds(b, 1)].rearrange("p e n b -> p e (n b)"), src).then_inc(R_.free("xsT"), 1)

            def turn(i, front_=True, tail=True, router=True):
                if router:
                    tail2(i - 1)
                if front_:
                    front(0, i + 1)
                    front(1, i + 1)
                if tail:
                    tail0(i, 0)
                if front_:
                    front(2, i + 1)
                if tail:
                    tail0(i, 1)
                if front_:
                    front(3, i + 1)
                if front_:
                    front(4, i + 1)
                if tail:
                    statistics(i)
                if router:
                    tail3(i - 1)
                if tail:
                    norms(i)
                if router:
                    tail4(i - 1)
                    tail5(i - 1)
                if front_:
                    out_img(i + 1)
                if tail:
                    tail1(i)
                if front_:
                    out(0, i + 1)
                    out(1, i + 1)
            for k in range(TILES):
                front(k, 0)
            out_img(0)
            out(0, 0)
            out(1, 0)
            ve.wait_ge(room_cleared, 1)
            turn(0, router=False)
            with ve.Fori(1, B - 1) as i:
                ch.enter(i - 1, AT_DVE)
                turn(i)
                ch.leave(B - 2, "attention dve")
            turn(B - 1, front_=False)
            turn(B, front_=False, tail=False)


GROUPS = NE // G


def load_experts(sp, c, t, i, u):
    e0 = i * (2 * G) + G * u
    if not isinstance(i, int):
        sp.wait_ge(c.first[u], ONE + i)
    sp.dma_start(c.w1[u][0:K2], t["L0_ffn_w1"][bass.ds(e0, G)].rearrange("n (p t) h -> p n t h", t=2)).then_inc(c.w1_in[u], 16)
    sp.dma_start(c.w1[u][K2:K2 + 1, :, 0, :], t["L0_ffn_b1"][bass.ds(e0, G)].rearrange("(a n) h -> a n h", a=1)
                 ).then_inc(c.w1_in[u], 16)
    if not isinstance(i, int):
        sp.wait_ge(c.second[u], ONE + i)
    sp.dma_start(c.w2[u][:], t["L0_ffn_w2"][bass.ds(e0, G)].rearrange("n (p c) d -> p n c d", c=FC)).then_inc(c.w2_in[u], 16)


def experts(nc, c, t, sb, sem):
    w1, w2 = c.w1, c.w2
    xg = sb("xg", [K2 + 1, 2, 2, G, R32])
    hs = sb("hs", [P, 2, F])
    hT = sb("hT", [P, 2, FC, P])
    ys = sb("ys", [P, 2, H])
    names = ("xg_in", "gelu", "turned", "turned_in", "ys_in", "ys_out")
    w1_in, w2_in, first, second = c.w1_in, c.w2_in, c.first, c.second
    xg_in, gelu, turned, turned_in, ys_in, ys_out = ([sem(f"ex_{n}_{u}") for u in range(2)] for n in names)
    ps = c.psum
    hid = [ps[:, 2 * u:2 * u + 2, :].rearrange("p k n -> p (k n)") for u in range(2)]
    flip = ps[:, 4:6, :].rearrange("p k n -> p (k n)")
    turns = GROUPS // 2

    with nc.Block() as block:
        @block.sync
        def _(sp):
            give(sp, [*first, *second, *gelu, *turned_in, *ys_in], [*ys_out])
            def store(i, u):
                sp.wait_ge(ys_in[u], ONE + i + 1)
                for j in range(G):
                    sp.dma_start(c.y_dram[bass.ds(i * (2 * G) + (G * u + j), 1)].rearrange("n b d -> (n b) d"),
                                 ys[R32 * j:R32 * j + B, u, :]).then_inc(ys_out[u], 16)
            load_experts(sp, c, t, 0, 1)
            with sp.Fori(0, turns - 1) as i:
                for u in range(2):
                    load_experts(sp, c, t, i + 1, u)
                    store(i, u)
            for u in range(2):
                store(turns - 1, u)
            for u in range(2):
                sp.wait_ge(ys_out[u], DMA + 16 * G * turns)

        @block.gpsimd
        def _(gp):
            with gp.Fori(0, turns) as i:
                for u in range(2):
                    gp.wait_ge(first[u], ONE + i)
                    nc.gpsimd.tensor_copy(xg[:, u], c.xsT[:, :, bass.ds(i * (2 * G) + G * u, G), :]).then_inc(xg_in[u], 1)
                    gp.wait_ge(xg_in[u], i + 1)

        @block.tensor
        def _(te):
            def layer1(i, u):
                te.wait_ge(w1_in[u], i * 32 + 32)
                te.wait_ge(xg_in[u], i + 1)
                te.wait_ge(gelu[u], ONE + i)
                for c0, n in ((0, 512), (512, F - 512)):
                    for k in range(2):
                        rows = K2 + 1 - k
                        for j in range(G):
                            last = nc.tensor.matmul(hid[u][R32 * j:R32 * j + R32, c0:c0 + n], xg[0:rows, u, k, j, :],
                                                    w1[u][0:rows, j, k, c0:c0 + n], start=(k == 0), stop=(k == 1))
                last.then_inc(first[u], 1)

            def layer2(i, u):
                te.wait_ge(gelu[u], ONE + i + 1)
                if u:
                    te.wait_ge(turned_in[0], ONE + i + 1)
                else:
                    te.wait_ge(turned_in[1], ONE + i)
                for f in range(FC):
                    last = nc.tensor.transpose(flip[:, P * f:P * f + P], hs[:, u, f:F:FC], c.ident)
                last.then_inc(turned[u], 1)
                te.wait_ge(turned_in[u], ONE + i + 1)
                te.wait_ge(w2_in[u], i * 16 + 16)
                te.wait_ge(ys_in[u], ONE + i)
                for f in range(FC):
                    for j in range(G):
                        last = nc.tensor.matmul(ps[R32 * j:R32 * j + R32, 6 + u, 0:H], hT[:, u, f, R32 * j:R32 * j + R32],
                                                w2[u][:, j, f, :], start=(f == 0), stop=(f == FC - 1))
                last.then_inc(second[u], 1)
            with te.Fori(0, turns) as i:
                layer1(i, 0)
                layer1(i, 1)
                layer2(i, 0)
                layer2(i, 1)

        @block.scalar
        def _(sc):
            with sc.Fori(0, turns) as i:
                for u in range(2):
                    sc.wait_ge(first[u], ONE + i + 1)
                    nc.scalar.activation(hs[:, u, :], hid[u][:, 0:F], ACT.Gelu).then_inc(gelu[u], 1)

        @block.vector
        def _(ve):
            with ve.Fori(0, turns) as i:
                for u in range(2):
                    ve.wait_ge(turned[u], i + 1)
                    nc.vector.tensor_copy(hT[:, u].rearrange("p c n -> p (c n)"), flip[:, 0:F]).then_inc(turned_in[u], 1)
                    ve.wait_ge(second[u], ONE + i + 1)
                    ve.wait_ge(ys_out[u], DMA + i * (16 * G))
                    nc.vector.tensor_copy(ys[:, u, :], ps[:, 6 + u, 0:H]).then_inc(ys_in[u], 1)


def combine(nc, c, t, sb, sem):
    Y = sb("Y", [NE, B, H])
    b2 = sb("b2", [NE, H])
    CT = sb("CT", [NE, 2, N])
    yb = sb("yb", [NE, 2, H])
    y_in, b2_in = sem("co_y_in"), sem("co_b2_in")
    c_in, yb_in = ([sem(f"co_{n}_{u}") for u in range(2)] for n in ("c_in", "yb_in"))
    full, added = ([sem(f"co_{n}_{u}") for u in range(2)] for n in ("full", "added"))
    stored = sem("co_stored")
    parts = ((0, 2), (2, 4), (4, 5))
    tiles = [(P, NI + P * k) for k in range(TT)] + [(NI, 0)]
    ps = c.psum

    def bank(u, j):
        return ps[:, 3 * u + j, :]
    turns = B // 2

    with nc.Block() as block:
        @block.sync
        def _(sp):
            give(sp, [*full, *added], [])
            sp.dma_start(Y[:], c.y_dram).then_inc(y_in, 16)
            sp.dma_start(b2[:], t["L0_ffn_b2"]).then_inc(b2_in, 16)
            with sp.Fori(0, turns) as i:
                for u in range(2):
                    sp.wait_ge(full[u], ONE + i * 3)
                    sp.dma_start(CT[:, u], c.c_dram[bass.ds(i * 2 + u, 1)].rearrange("b n t -> (b n) t")).then_inc(c_in[u], 16)

        @block.gpsimd
        def _(gp):
            with gp.Fori(0, turns) as i:
                for u in range(2):
                    b = i * 2 + u
                    gp.wait_ge(added[u], ONE + i * 5 + 4)
                    dst = t["out"][bass.ds(b, 1), NI:N, :].rearrange("b (k p) h -> p (b k) h", p=P)
                    gp.dma_start(dst, c.h[:, bass.ds(i * (2 * TT) + TT * u, TT), :]).then_inc(stored, 16)
                    gp.wait_ge(added[u], ONE + i * 5 + 5)
                    gp.dma_start(t["out"][bass.ds(b, 1), 0:NI, :].rearrange("b p h -> (b p) h"),
                                 c.h_img[:, bass.ds(b, 1), :].rearrange("p b h -> p (b h)")).then_inc(stored, 16)
            gp.wait_ge(stored, 32 * B)

        @block.tensor
        def _(te):
            with te.Fori(0, turns) as i:
                for u in range(2):
                    te.wait_ge(c_in[u], i * 16 + 16)
                    te.wait_ge(yb_in[u], i + 1)
                    for j, (k0, k1) in enumerate(parts):
                        if j == 0:
                            te.wait_ge(added[u], ONE + i * 5)
                        for k in range(k0, k1):
                            n, c0 = tiles[k]
                            last = nc.tensor.matmul(bank(u, j)[0:n, H * (k - k0):H * (k - k0) + H], CT[:, u, c0:c0 + n], yb[:, u, :],
                                                    start=True, stop=True)
                        last.then_inc(full[u], 1)

        @block.vector
        def _(ve):
            ve.wait_ge(y_in, 16)
            ve.wait_ge(b2_in, 16)

            def rows(i, u):
                nc.vector.tensor_tensor(yb[:, u, :], Y[:, bass.ds(i * 2 + u, 1), :].rearrange("p b h -> p (b h)"), b2[:], ALU.add
                                        ).then_inc(yb_in[u], 1)

            def add(i, u):
                b = i * 2 + u
                for j, (k0, k1) in enumerate(parts):
                    ve.wait_ge(full[u], ONE + i * 3 + (j + 1))
                    for k in range(k0, k1):
                        n = tiles[k][0]
                        h = (c.h[:, bass.ds(i * (2 * TT) + (TT * u + k), 1), :] if k < TT else c.h_img[:, bass.ds(b, 1), :]
                             ).rearrange("p a h -> p (a h)")
                        scale = c.rsum[0:n, bass.ds(b, 1), k:k + 1].rearrange("p a k -> p (a k)")
                        nc.vector.scalar_tensor_tensor(h, bank(u, j)[0:n, H * (k - k0):H * (k - k0) + H], scale, h,
                                                       ALU.mult, ALU.add).then_inc(added[u], 1)
            for u in range(2):
                rows(0, u)
            with ve.Fori(0, turns - 1) as i:
                for u in range(2):
                    add(i, u)
                    rows(i + 1, u)
            for u in range(2):
                add(turns - 1, u)


INPUTS = ["x", "x_txt", "itok_BS_0_15", "itok_BS_0_3", "itok_BS_0_9999", "itok_BS_0_2047", "fside_BS_age_tau", "fside_BS_delays_tau",
          "L0_tok_W", "L0_tok_b", "L0_txt_word_table", "L0_txt_modalities_table", "L0_txt_seg_table", "L0_txt_npi_table",
          "L0_txt_posi_table", "L0_txt_age_w", "L0_txt_age_b", "L0_txt_age_w0", "L0_txt_age_b0", "L0_txt_delay_w", "L0_txt_delay_b",
          "L0_txt_delay_w0", "L0_txt_delay_b0", "L0_txt_ln_gamma", "L0_txt_ln_beta", "L0_attn_w_qkv", "L0_attn_w_proj",
          "L0_attn_b_proj", "L0_ffn_phi", "L0_ffn_scale", "L0_ffn_w1", "L0_ffn_b1", "L0_ffn_w2", "L0_ffn_b2"]


def kernel(**inputs):
    import concourse.bacc as bacc
    from concourse.bass_utils import run_bass_kernel_spmd

    nc = bacc.Bacc("TRN2", target_bir_lowering=False, num_devices=1)
    arrays = {f"in_{name}": np.ascontiguousarray(inputs[name]) for name in INPUTS}
    arrays["in_const"] = constants()
    t = {name[3:]: nc.dram_tensor(name, a.shape, mybir.dt.from_np(a.dtype), kind="ExternalInput").ap() for name, a in arrays.items()}
    t["out"] = nc.dram_tensor("out", (B, N, H), F32, kind="ExternalOutput").ap()
    build(nc, t)
    result = run_bass_kernel_spmd(nc, [arrays], core_ids=[0])
    return result.results[0]["out"]
```
